# Optimizing a Trainium2 kernel written in Bass

```python
import numpy as np
import jax
import jax.numpy as jnp

def _softmax(x, axis=-1):
    return jax.nn.softmax(x, axis=axis)

def _gelu(x):
    return jax.nn.gelu(x, approximate=True)

def _silu(x):
    return jax.nn.silu(x)

def _sigmoid(x):
    return jax.nn.sigmoid(x)

def _layernorm(x, axis=-1, eps=1e-05):
    m = jnp.mean(x, axis=axis, keepdims=True)
    v = jnp.var(x, axis=axis, keepdims=True)
    return (x - m) / jnp.sqrt(v + eps)

def _scatter_add(tgt, idx, src, axis=0):
    return tgt.at[idx].add(src)

def _segment_sum(src, seg, n):
    return jax.ops.segment_sum(src, seg, n)
kernel_name = 'mk_decoder_preln_d1_seqx_r8_5dadac'

def setup_inputs(seed: int=0):
    np.random.seed(seed)
    _w = jnp.asarray

    def _rec_inputs():
        import jax
        import jax.numpy as jnp
        _rk = jax.random.key(seed)
        x = -0.0003929 + 0.9999 * jax.random.normal(jax.random.fold_in(_rk, 1), (32, 128, 128), jnp.float32)
        _lenS = 128 - jax.random.randint(jax.random.fold_in(_rk, 7), (32,), 0, max(1, 128 // 4) + 1, jnp.int32)
        _lenS2 = 128 - jax.random.randint(jax.random.fold_in(_rk, 8), (32,), 0, max(1, 128 // 4) + 1, jnp.int32)
        _ctx_512P = jax.random.normal(jax.random.fold_in(_rk, 11), (32, 16, 64), jnp.float32)
        _ctx_512c = jax.random.dirichlet(jax.random.fold_in(_rk, 511), 0.3 * jnp.ones((16,), jnp.float32), (32, 128))
        _ctx_512t = jnp.einsum('bsk,bkd->bsd', _ctx_512c, _ctx_512P)
        _ctx_512t = _ctx_512t * jax.lax.rsqrt(jnp.mean(jnp.square(_ctx_512t)) + 1e-12) * 0.953939
        ctx_512 = -1.39393e-06 + 0.999914 * (_ctx_512t + 0.3 * jax.random.normal(jax.random.fold_in(_rk, 611), (32, 128, 64), jnp.float32))
        return (x, ctx_512)
    x, ctx_512 = _rec_inputs()

    def _L0_attn_setup():
        import jax, jax.numpy as jnp
        import numpy as np
        HEADS = 8
        BLOCK = 32
        key = jax.random.key(seed)
        ks = jax.random.split(key, 4)
        b, n, d, f = (4, 512, 128, 128)
        x = jax.random.normal(ks[0], (b, n, d), dtype=jnp.float32)
        w_qkv = jax.random.normal(ks[1], (3 * d, d), dtype=jnp.float32) * d ** (-0.5)
        w_out = jax.random.normal(ks[2], (d, d), dtype=jnp.float32) * d ** (-0.5)
        b_out = jnp.zeros((d,), dtype=jnp.float32)
        proj = jax.random.normal(ks[3], (HEADS, d // HEADS, f), dtype=jnp.float32) * (d // HEADS) ** (-0.5)
        return {'x': x, 'w_qkv': w_qkv, 'w_out': w_out, 'b_out': b_out, 'proj': proj}
    _L0_attn_all = _L0_attn_setup()
    _L0_attn_in = {k: v for k, v in _L0_attn_all.items() if k in ('w_qkv', 'w_out', 'b_out', 'proj')}
    del _L0_attn_all

    def _L0_xattn_setup():
        import jax, jax.numpy as jnp
        import numpy as np
        HEADS = 16
        D_MODEL = 128
        IMG_MODEL = 64
        D_K = D_MODEL // HEADS
        key = jax.random.key(seed)
        ks = jax.random.split(key, 12)
        B, LQ, LKV = (8, 256, 128)
        s_dm = 1.0 / np.sqrt(D_MODEL)
        s_im = 1.0 / np.sqrt(IMG_MODEL)
        return {'q': jax.random.normal(ks[0], (B, LQ, D_MODEL), jnp.float32), 'k': jax.random.normal(ks[1], (B, LKV, IMG_MODEL), jnp.float32), 'v': jax.random.normal(ks[2], (B, LKV, IMG_MODEL), jnp.float32), 'Wq': jax.random.normal(ks[3], (D_MODEL, D_MODEL), jnp.float32) * s_dm, 'bq': jnp.zeros((D_MODEL,), jnp.float32), 'Wk': jax.random.normal(ks[4], (IMG_MODEL, D_MODEL), jnp.float32) * s_im, 'bk': jnp.zeros((D_MODEL,), jnp.float32), 'Wv': jax.random.normal(ks[5], (IMG_MODEL, D_MODEL), jnp.float32) * s_im, 'bv': jnp.zeros((D_MODEL,), jnp.float32), 'Wo': jax.random.normal(ks[6], (D_MODEL, D_MODEL), jnp.float32) * s_dm, 'bo': jnp.zeros((D_MODEL,), jnp.float32)}
    _L0_xattn_all = _L0_xattn_setup()
    _L0_xattn_in = {k: v for k, v in _L0_xattn_all.items() if k in ('Wq', 'bq', 'Wk', 'bk', 'Wv', 'bv', 'Wo', 'bo')}
    del _L0_xattn_all

    def _L0_ffn_setup():
        import jax, jax.numpy as jnp
        import numpy as np
        H, I, E, K = (128, 64, 32, 8)
        B, S = (4, 128)

        def silu(x):
            return x * jax.nn.sigmoid(x)
        key = jax.random.key(seed)
        ks = jax.random.split(key, 14)

        def w(k, shape, fan_in):
            return jax.random.normal(k, shape, jnp.float32) / np.float32(np.sqrt(fan_in))
        return {'hidden_states': jax.random.normal(ks[0], (B, S, H), jnp.float32), 'Wr': w(ks[1], (H, E), H), 'br': jnp.zeros((E,), jnp.float32), 'Wg_s': w(ks[2], (H, I), H), 'bg_s': jnp.zeros((I,), jnp.float32), 'Wu_s': w(ks[3], (H, I), H), 'bu_s': jnp.zeros((I,), jnp.float32), 'Wd_s': w(ks[4], (I, H), I), 'bd_s': jnp.zeros((H,), jnp.float32), 'Wg': w(ks[5], (E, H, I), H), 'bg': jnp.zeros((E, I), jnp.float32), 'Wu': w(ks[6], (E, H, I), H), 'bu': jnp.zeros((E, I), jnp.float32), 'Wd': w(ks[7], (E, I, H), I), 'bd': jnp.zeros((E, H), jnp.float32)}
    _L0_ffn_all = _L0_ffn_setup()
    _L0_ffn_in = {k: v for k, v in _L0_ffn_all.items() if k in ('Wr', 'br', 'Wg_s', 'bg_s', 'Wu_s', 'bu_s', 'Wd_s', 'bd_s', 'Wg', 'bg', 'Wu', 'bu', 'Wd', 'bd')}
    del _L0_ffn_all
    return {'x': x, 'ctx_512': ctx_512, 'L0_attn_w_qkv': _L0_attn_in['w_qkv'], 'L0_attn_w_out': _L0_attn_in['w_out'], 'L0_attn_b_out': _L0_attn_in['b_out'], 'L0_attn_proj': _L0_attn_in['proj'], 'L0_xattn_Wq': _L0_xattn_in['Wq'], 'L0_xattn_bq': _L0_xattn_in['bq'], 'L0_xattn_Wk': _L0_xattn_in['Wk'], 'L0_xattn_bk': _L0_xattn_in['bk'], 'L0_xattn_Wv': _L0_xattn_in['Wv'], 'L0_xattn_bv': _L0_xattn_in['bv'], 'L0_xattn_Wo': _L0_xattn_in['Wo'], 'L0_xattn_bo': _L0_xattn_in['bo'], 'L0_ffn_Wr': _L0_ffn_in['Wr'], 'L0_ffn_br': _L0_ffn_in['br'], 'L0_ffn_Wg_s': _L0_ffn_in['Wg_s'], 'L0_ffn_bg_s': _L0_ffn_in['bg_s'], 'L0_ffn_Wu_s': _L0_ffn_in['Wu_s'], 'L0_ffn_bu_s': _L0_ffn_in['bu_s'], 'L0_ffn_Wd_s': _L0_ffn_in['Wd_s'], 'L0_ffn_bd_s': _L0_ffn_in['bd_s'], 'L0_ffn_Wg': _L0_ffn_in['Wg'], 'L0_ffn_bg': _L0_ffn_in['bg'], 'L0_ffn_Wu': _L0_ffn_in['Wu'], 'L0_ffn_bu': _L0_ffn_in['bu'], 'L0_ffn_Wd': _L0_ffn_in['Wd'], 'L0_ffn_bd': _L0_ffn_in['bd']}

def reference(x, ctx_512, L0_attn_w_qkv, L0_attn_w_out, L0_attn_b_out, L0_attn_proj, L0_xattn_Wq, L0_xattn_bq, L0_xattn_Wk, L0_xattn_bk, L0_xattn_Wv, L0_xattn_bv, L0_xattn_Wo, L0_xattn_bo, L0_ffn_Wr, L0_ffn_br, L0_ffn_Wg_s, L0_ffn_bg_s, L0_ffn_Wu_s, L0_ffn_bu_s, L0_ffn_Wd_s, L0_ffn_bd_s, L0_ffn_Wg, L0_ffn_bg, L0_ffn_Wu, L0_ffn_bu, L0_ffn_Wd, L0_ffn_bd):
    import jax
    import jax.numpy as jnp

    def _L0_attn_ref(x, w_qkv, w_out, b_out, proj):
        import jax, jax.numpy as jnp
        import numpy as np
        HEADS = 8
        BLOCK = 32
        b, n, d = x.shape
        h = HEADS
        hd = d // h
        nb = n // BLOCK
        qkv = x @ w_qkv.T
        q, k, v = jnp.split(qkv, 3, axis=-1)

        def to_blocks(t):
            return t.reshape(b, n, h, hd).transpose(0, 2, 1, 3).reshape(b, h, nb, BLOCK, hd)
        q, k, v = (to_blocks(q), to_blocks(k), to_blocks(v))
        qp = jax.nn.elu(jnp.einsum('bhcsd,hdf->bhcsf', q, proj)) + 1.0
        kp = jax.nn.elu(jnp.einsum('bhcsd,hdf->bhcsf', k, proj)) + 1.0
        kv = jnp.einsum('bhcsf,bhcsd->bhcfd', kp, v)
        num = jnp.einsum('bhcsf,bhcfd->bhcsd', qp, kv)
        ksum = kp.sum(axis=3)
        z = 1.0 / (jnp.einsum('bhcsf,bhcf->bhcs', qp, ksum) + 1e-08)
        out = num * z[..., None]
        out = out.reshape(b, h, n, hd).transpose(0, 2, 1, 3).reshape(b, n, d)
        return out @ w_out.T + b_out

    def _L0_xattn_ref(q, k, v, Wq, bq, Wk, bk, Wv, bv, Wo, bo):
        import jax, jax.numpy as jnp
        import numpy as np
        HEADS = 16
        D_MODEL = 128
        IMG_MODEL = 64
        D_K = D_MODEL // HEADS
        B, LQ, _ = q.shape
        LKV = k.shape[1]
        qh = (q @ Wq + bq).reshape(B, LQ, HEADS, D_K).transpose(0, 2, 1, 3)
        kh = (k @ Wk + bk).reshape(B, LKV, HEADS, D_K).transpose(0, 2, 1, 3)
        vh = (v @ Wv + bv).reshape(B, LKV, HEADS, D_K).transpose(0, 2, 1, 3)
        scale = 1.0 / np.sqrt(D_K)
        scores = jnp.einsum('bhqd,bhkd->bhqk', qh, kh) * scale
        attn = jax.nn.softmax(scores, axis=-1)
        out = jnp.einsum('bhqk,bhkd->bhqd', attn, vh)
        concat = out.transpose(0, 2, 1, 3).reshape(B, LQ, D_MODEL)
        return concat @ Wo + bo

    def _L0_ffn_ref(hidden_states, Wr, br, Wg_s, bg_s, Wu_s, bu_s, Wd_s, bd_s, Wg, bg, Wu, bu, Wd, bd):
        import jax, jax.numpy as jnp
        import numpy as np
        H, I, E, K = (128, 64, 32, 8)
        B, S = (4, 128)

        def silu(x):
            return x * jax.nn.sigmoid(x)
        b, s, h = hidden_states.shape
        T = b * s
        x = hidden_states.reshape(T, h)
        logits = jnp.dot(x.astype(jnp.float32), Wr) + br
        aff = jax.nn.sigmoid(logits)
        top_v, top_i = jax.lax.top_k(aff, K)
        top_w = top_v / (jnp.sum(top_v, axis=-1, keepdims=True) + 1e-09)
        top_w = top_w.astype(hidden_states.dtype)
        e_total = Wr.shape[1]
        w_full = jnp.zeros((T, e_total), hidden_states.dtype)
        w_full = w_full.at[jnp.arange(T)[:, None], top_i].set(top_w)
        shared = jnp.dot(silu(jnp.dot(x, Wg_s) + bg_s) * (jnp.dot(x, Wu_s) + bu_s), Wd_s) + bd_s
        gate = silu(jnp.einsum('th,ehi->eti', x, Wg) + bg[:, None, :])
        up = jnp.einsum('th,ehi->eti', x, Wu) + bu[:, None, :]
        down = jnp.einsum('eti,eih->eth', gate * up, Wd) + bd[:, None, :]
        routed = jnp.einsum('te,eth->th', w_full, down)
        return (shared + routed).reshape(b, s, h)
    x = x + _L0_attn_ref(_layernorm(x, axis=-1), L0_attn_w_qkv, L0_attn_w_out, L0_attn_b_out, L0_attn_proj)
    x = x + _L0_xattn_ref(_layernorm(x, axis=-1), ctx_512, ctx_512, L0_xattn_Wq, L0_xattn_bq, L0_xattn_Wk, L0_xattn_bk, L0_xattn_Wv, L0_xattn_bv, L0_xattn_Wo, L0_xattn_bo)
    x = x + _L0_ffn_ref(_layernorm(x, axis=-1), L0_ffn_Wr, L0_ffn_br, L0_ffn_Wg_s, L0_ffn_bg_s, L0_ffn_Wu_s, L0_ffn_bu_s, L0_ffn_Wd_s, L0_ffn_bd_s, L0_ffn_Wg, L0_ffn_bg, L0_ffn_Wu, L0_ffn_bu, L0_ffn_Wd, L0_ffn_bd)
    return x

_drawn_inputs = setup_inputs


def setup_inputs(seed=0):
    import zlib

    import numpy as np

    out = dict(_drawn_inputs(seed))
    spreads = {'L0_attn_b_out': (0.0, 0.1),
     'L0_xattn_bq': (0.0, 0.1),
     'L0_xattn_bk': (0.0, 0.8),
     'L0_xattn_bv': (0.0, 0.1),
     'L0_xattn_bo': (0.0, 0.1),
     'L0_ffn_br': (0.0, 0.1),
     'L0_ffn_bg_s': (0.0, 0.1),
     'L0_ffn_bu_s': (0.0, 0.1),
     'L0_ffn_bd_s': (0.0, 0.1),
     'L0_ffn_bg': (0.0, 0.484),
     'L0_ffn_bu': (0.0, 0.506),
     'L0_ffn_bd': (0.0, 0.3)}
    factors = {'L0_attn_proj': 2.754}
    for name, (base, spread) in spreads.items():
        noise = np.random.default_rng([zlib.crc32(name.encode()), seed]).standard_normal(out[name].shape)
        drawn = base * np.exp(spread * noise) if base else spread * noise
        out[name] = jnp.asarray(drawn.astype(out[name].dtype))
    for name, factor in factors.items():
        out[name] = (out[name] * factor).astype(out[name].dtype)
    return out
```

```python
from contextlib import ExitStack

import concourse.bass as bass
from concourse import mybir

F32 = mybir.dt.float32
F32R = mybir.dt.float32r
ALU = mybir.AluOpType
ACT = mybir.ActivationFunctionType
AX = mybir.AxisListType

P = 128
D = 128
EPS = 1e-5
TPG = 4
GW = TPG * P

AH = 8
AHD = D // AH
NF = 128
BLK = 32
DEN_EPS = 1e-8

XH = 16
XHD = D // XH
XG = XH // 4
CW = 64

E = 32
TOPK = 8
FI = 64
NP = E // 2
NU = NP + 1


def ds(i, n):
    return bass.ds(i, n)


def decoder_layer(nc, x_in, ctx_in, w_qkv, w_out, b_out, proj, Wq, bq, Wk, bk, Wv, bv, Wo, bo,
                  Wr, br, Wg_s, bg_s, Wu_s, bu_s, Wd_s, bd_s, Wg, bg, Wu, bu, Wd, bd, out, phases=3):
    NT = x_in.shape[0] * x_in.shape[1] // P
    G = NT // TPG
    assert x_in.shape[1] == P and G % 2 == 0 and G >= 4

    x_tiles = x_in.rearrange("n p d -> p n d")
    ctx_tiles = ctx_in.rearrange("n p d -> p n d")
    out_tiles = out.rearrange("n p d -> p n d")

    with ExitStack() as ctx:
        def sb(name, shape, dt=F32):
            return ctx.enter_context(nc.sbuf_tensor(name, shape, dt))

        def sem(name):
            return ctx.enter_context(nc.semaphore(name))

        bank = [ctx.enter_context(nc.psum_tensor(f"bank{i}", [P, 512], F32)) for i in range(8)]
        tbank = bank[7]

        X = sb("X", [P, NT, D])
        ident = sb("ident", [P, P])
        neg_half = sb("neg_half", [P, TPG])
        eps_b = sb("eps_b", [P, TPG])
        stats = sb("stats", [P, TPG, 6])
        mv = sb("mv", [P, TPG, 2])
        veps = sb("veps", [P, TPG])
        rstd = sb("rstd", [P, TPG])
        xn = sb("xn", [P, TPG, D])
        xb = sb("xb", [P, TPG, D])
        XTH = [sb(f"XTH{i}", [P, GW], F32R) for i in range(2)]
        XTL = [sb(f"XTL{i}", [P, GW], F32R) for i in range(2)]

        raw = sb("raw", [P, 2, NU, P])
        raw_flat = raw[:, :, :, :].rearrange("p a n c -> p (a n c)")
        wqk_rows = raw_flat[0:AHD, 0:3 * AH * D].rearrange("p (h d) -> p h d", d=D)
        proj_sb = raw_flat[0:AHD, 3 * AH * D:4 * AH * D].rearrange("p (h f) -> p h f", f=NF)
        wrow0 = 4 * AH * D
        wv_rows = raw_flat[:, wrow0:wrow0 + D]
        wout_rows = raw_flat[:, wrow0 + D:wrow0 + 2 * D]
        CH = sb("CH", [P, NU, P], F32R)
        CL = sb("CL", [P, NU, P], F32R)
        WVH = sb("WVH", [P, D], F32R)
        WVL = sb("WVL", [P, D], F32R)
        WOT = sb("WOT", [P, D])
        bout_b = sb("bout_b", [P, D])
        blockmask = sb("blockmask", [P, P])
        work = sb("work", [P, 4 * TPG * XG * P])

        def part(n, width=GW):
            return work[:, n * GW:n * GW + width]

        expf = [part(i) for i in range(4)]
        phiK = [part(4 + i) for i in range(2)]
        phiQ = [part(6 + i) for i in range(2)]
        AM = [part(8 + i).rearrange("p (b s) -> p b s", s=P) for i in range(2)]
        V1 = part(10, 2 * GW).rearrange("p (b h c) -> p b h c", b=TPG, c=32)
        OS = [sb(f"OS{i}", [P, TPG, P]) for i in range(2)]
        den = sb("den", [P, TPG, 8])
        rden = sb("rden", [P, TPG, 8])
        ON = sb("ON", [P, TPG, D])
        ONT = sb("ONT", [P, TPG, P])

        ctxr = [sb(f"ctxr{i}", [P, TPG, 2, CW]) for i in range(2)]
        wqx = sb("wqx", [P, D])
        wkx = sb("wkx", [P, D])
        wvx = sb("wvx", [P, D])
        wx_hi = sb("wx_hi", [P, 2, D], F32R)
        wx_lo = sb("wx_lo", [P, 2, D], F32R)
        WQS = [sb(f"WQS{i}", [P, XG, 4, 4, XHD], F32R) for i in range(2)]
        WKS = [sb(f"WKS{i}", [P, XG, 4, 4, XHD], F32R) for i in range(2)]
        WVX = [sb(f"WVX{i}", [P, D], F32R) for i in range(2)]
        WOX = sb("WOX", [P, D])
        bo_b = sb("bo_b", [P, D])
        bv_b = sb("bv_b", [P, TPG, D])
        bqs = sb("bqs", [P, XG])
        bks = sb("bks", [P, XG])
        bqm = sb("bqm", [P, XG])
        bkm = sb("bkm", [P, XG])
        lo_q = sb("lo_q", [P, 1])
        lo_k = sb("lo_k", [P, 1])
        lo_c = sb("lo_c", [P, 1])
        ones_k = sb("ones_k", [P, 1])
        HM = [sb(f"HM{i}", [P, GW], F32R) for i in range(2)]
        CS = [sb(f"CS{i}", [P, GW], F32R) for i in range(2)]
        QS = sb("QS", [P, XG, GW], F32R)
        KS = sb("KS", [P, XG, GW], F32R)
        V2 = [sb(f"V2{i}", [P, TPG * XG, 4, 32]) for i in range(2)]
        PT = work[:, :].rearrange("p (u g q) -> p u g q", u=4 * TPG, q=P)
        negm = sb("negm", [P, 4, XG, TPG])
        MM = sb("MM", [P, 4, 2, XG * TPG], F32R)
        MT = sb("MT", [P, P], F32R)

        GATE = (CH, CL)
        UP = [sb(f"UP{i}", [P, NU, P], F32R) for i in range(2)]
        WD = sb("WD", [P, NU, D])
        wr_sb = sb("wr_sb", [P, E])
        WR = [sb(f"WR{i}", [P, E], F32R) for i in range(2)]
        br_b = sb("br_b", [P, E])
        bd_rows = sb("bd_rows", [P, D])
        BD = [sb(f"BD{i}", [P, D], F32R) for i in range(2)]
        bias_rows = sb("bias_rows", [64, P])
        BT = sb("BT", [P, 64])
        SEL = QS[:, :, :].rearrange("p g (u m) -> p (g u) m", m=P)
        lg = sb("lg", [P, TPG, E])
        sig = sb("sig", [P, TPG, E])
        zap = sb("zap", [P, TPG, E])
        wsel = sb("wsel", [P, TPG, E])
        wfull = sb("wfull", [P, TPG, E])
        top8 = sb("top8", [P, TPG, 8])
        wsum = sb("wsum", [P, TPG])
        winv = sb("winv", [P, TPG])
        WS = sb("WS", [P, TPG, P], F32R)
        WT = [sb(f"WT{i}", [P, GW], F32R) for i in range(2)]
        silu = [part(i) for i in range(2)]
        upm = [part(2 + i) for i in range(2)]
        hid = [part(4 + i) for i in range(2)]
        YS = part(6)
        OST = [part(7 + i).rearrange("p (b d) -> p b d", d=D) for i in range(2)]

        ld_w = sem("ld_w")
        ld_x0 = sem("ld_x0")
        ld_x = sem("ld_x")
        c_pool = sem("c_pool")
        c_wT = sem("c_wT")
        c_hi = sem("c_hi")
        c_lo = sem("c_lo")
        ln_mv = sem("ln_mv")
        ln_eps = sem("ln_eps")
        ln_rstd = sem("ln_rstd")
        ln_xn = sem("ln_xn")
        xt_full = sem("xt_full")
        xt_hi_ok = sem("xt_hi_ok")
        xt_lo_ok = sem("xt_lo_ok")
        a_feat = sem("a_feat")
        a_exp = sem("a_exp")
        a_mink = sem("a_mink")
        a_neg = sem("a_neg")
        a_phi = sem("a_phi")
        a_score = sem("a_score")
        a_mask = sem("a_mask")
        a_o = sem("a_o")
        a_os = sem("a_os")
        a_vp = sem("a_vp")
        a_v1 = sem("a_v1")
        a_ot = sem("a_ot")
        a_den = sem("a_den")
        a_rden = sem("a_rden")
        a_norm = sem("a_norm")
        a_ontp = sem("a_ontp")
        a_ont = sem("a_ont")
        a_proj = sem("a_proj")
        a_xb = sem("a_xb")
        a_x1 = sem("a_x1")
        ld_c = [sem(f"ld_c{i}") for i in range(2)]
        ld_b = sem("ld_b")
        s_pool = sem("s_pool")
        s_dve = sem("s_dve")
        b_ctx = sem("b_ctx")
        b_cm = sem("b_cm")
        b_cs = sem("b_cs")
        b_pp = sem("b_pp")
        b_hm = sem("b_hm")
        b_split = sem("b_split")
        b_vp = sem("b_vp")
        b_v2 = sem("b_v2")
        b_s = sem("b_s")
        b_max = sem("b_max")
        b_mm = sem("b_mm")
        b_mtp = sem("b_mtp")
        b_mt = sem("b_mt")
        b_mq = sem("b_mq")
        b_st = sem("b_st")
        b_exp = sem("b_exp")
        b_pv = sem("b_pv")
        b_os = sem("b_os")
        b_ot = sem("b_ot")
        b_rden = sem("b_rden")
        b_norm = sem("b_norm")
        b_ontp = sem("b_ontp")
        b_ont = sem("b_ont")
        b_proj = sem("b_proj")
        b_xb = sem("b_xb")
        b_x2 = sem("b_x2")
        ld_f = sem("ld_f")
        ld_raw = sem("ld_raw")
        f_pool = sem("f_pool")
        f_zero = sem("f_zero")
        f_prep = sem("f_prep")
        f_bt = sem("f_bt")
        f_g = sem("f_g")
        f_u = sem("f_u")
        f_w = sem("f_w")
        f_s = sem("f_s")
        f_t = sem("f_t")
        f_h = sem("f_h")
        f_d = sem("f_d")
        f_y = sem("f_y")
        f_yt = sem("f_yt")
        f_o = sem("f_o")
        st_y = [sem(f"st_y{i}") for i in range(2)]
        r_lp = sem("r_lp")
        r_lg = sem("r_lg")
        r_sig = sem("r_sig")
        r_zap = sem("r_zap")
        r_w = sem("r_w")
        r_wp = sem("r_wp")
        r_wt = sem("r_wt")
        st_out = sem("st_out")

        FPREP = 6
        LDF = 16 * 11
        SPOOL = 14
        SDVE = 24
        LDB = 16 * (4 + 2 + TPG + XH + 24)

        block = ctx.enter_context(nc.Block())

        def walk(eng, body):
            body(0, 0)
            body(1, 1)
            with eng.Fori(1, G // 2 - 1) as i:
                body(i * 2, 0)
                body(i * 2 + 1, 1)
            body(G - 2, 0)
            body(G - 1, 1)

        def is_first(g):
            return isinstance(g, int) and g == 0

        def is_last(g):
            return isinstance(g, int) and g == G - 1

        @block.sync
        def _(sp):
            sp.dma_start(X[:, 0:TPG, :], x_tiles[:, 0:TPG, :]).then_inc(ld_x0, 16)
            sp.dma_start(wqk_rows[:, :, :], w_qkv.rearrange("(h r) d -> r h d", r=AHD)).then_inc(ld_w, 16)
            sp.dma_start(proj_sb[:, :, :], proj.rearrange("h r f -> r h f")).then_inc(ld_w, 16)
            sp.dma_start(wv_rows[:, :], w_qkv[2 * D:3 * D, :]).then_inc(ld_w, 16)
            sp.dma_start(wout_rows[:, :], w_out).then_inc(ld_w, 16)
            sp.dma_start(bout_b[:, :], b_out.partition_broadcast(P)).then_inc(ld_w, 16)
            sp.dma_start(X[:, TPG:NT, :], x_tiles[:, TPG:NT, :]).then_inc(ld_x, 16)
            for i in range(2):
                rows = slice(i * CW, (i + 1) * CW)
                sp.dma_start(wkx[rows, :], Wk).then_inc(ld_b, 16)
                sp.dma_start(wvx[rows, :], Wv).then_inc(ld_b, 16)
            sp.dma_start(wqx[:, :], Wq).then_inc(ld_b, 16)
            sp.dma_start(bo_b[:, :], bo.partition_broadcast(P)).then_inc(ld_b, 16)
            for b in range(TPG):
                sp.dma_start(bv_b[:, b, :], bv.partition_broadcast(P)).then_inc(ld_b, 16)
            for h in range(XH):
                gi, j = h // 4, h % 4
                row = (gi // 2) * 64 + j * 16 + (gi % 2) * 8
                sp.dma_start(WOX[row:row + XHD, :], Wo[h * XHD:(h + 1) * XHD, :]).then_inc(ld_b, 16)
            sp.wait_ge(s_pool, 2)
            for j in range(4):
                for t in range(3):
                    row = 32 * j + 8 * t
                    for dst, src in ((bqs, bq), (bks, bk)):
                        v = src.rearrange("(g j d) -> j d g", j=4, d=XHD)
                        sp.dma_start(dst[row:row + XHD, :], v[j], allow_slow_non_contiguous=True).then_inc(ld_b, 16)

            sp.wait_ge(f_zero, 4)
            sp.dma_start(WD[:, 0:NP, :], Wd.rearrange("(n e) i d -> (e i) n d", e=2)).then_inc(ld_f, 16)
            sp.dma_start(WD[0:FI, NP, :], Wd_s).then_inc(ld_f, 16)
            sp.dma_start(wr_sb[:, :], Wr).then_inc(ld_f, 16)
            sp.dma_start(br_b[:, :], br.partition_broadcast(P)).then_inc(ld_f, 16)
            for i in range(2):
                sp.dma_start(bd_rows[i * E:(i + 1) * E, :], bd).then_inc(ld_f, 16)
            for row, pairs, shared in ((0, bg, bg_s), (32, bu, bu_s)):
                sp.dma_start(bias_rows[row:row + NP, :],
                             pairs.rearrange("(n e) i -> n (e i)", e=2)).then_inc(ld_f, 16)
                sp.dma_start(bias_rows[row + NP:row + NP + 1, 0:FI],
                             shared.rearrange("(a n) -> a n", a=1)).then_inc(ld_f, 16)
            sp.dma_start(bias_rows[49:50, :], bd_s.rearrange("(a n) -> a n", a=1)).then_inc(ld_f, 16)
            sp.wait_ge(c_wT, 5)
            sp.wait_ge(f_zero, 5)
            for i, (pairs, shared) in enumerate(((Wg, Wg_s), (Wu, Wu_s))):
                sp.dma_start(raw[:, i, 0:NP, :].rearrange("p n (e c) -> p (n e) c", e=2),
                             pairs.rearrange("e d c -> d e c")).then_inc(ld_raw, 16)
                sp.dma_start(raw[:, i, NP, 0:FI], shared).then_inc(ld_raw, 16)

            def load_ctx(g, par):
                for i in range(2):
                    sp.dma_start(ctxr[par][:, :, i, :], ctx_tiles[:, ds(g * TPG, TPG), :]).then_inc(ld_c[par], 16)

            load_ctx(0, 0)

            def xattn(g, par):
                if not is_last(g):
                    if not is_first(g):
                        sp.wait_ge(b_ctx, g)
                    load_ctx(g + 1, 1 - par)
                sp.wait_ge(b_mt, g + 1)
                for j in range(4):
                    sp.dma_start(QS[32 * j + 24:32 * j + 26, :, :].bitcast(F32),
                                 MT[32 * j:32 * j + 32, :].bitcast(F32)).then_inc(b_mq, 16)

            if phases > 1:
                walk(sp, xattn)
            def store(g, par):
                sp.wait_ge(f_o, g + 1)
                sp.dma_start(out_tiles[:, ds(g * TPG, TPG), :], OST[par]).then_inc(st_y[par], 16)

            if phases > 2:
                walk(sp, store)
                for i in range(2):
                    sp.wait_ge(st_y[i], G * 8)
            if phases == 2:
                sp.wait_ge(b_x2, G)
                sp.dma_start(out_tiles, X[:, :, :]).then_inc(st_out, 16)
                sp.wait_ge(st_out, 16)
            if phases == 1:
                sp.wait_ge(a_x1, G)
                sp.dma_start(out_tiles, X[:, :, :]).then_inc(st_out, 16)
                sp.wait_ge(st_out, 16)

        @block.gpsimd
        def _(pool):
            pool.memset(ident[:, :], 0.0).then_inc(c_pool, 1)
            pool.wait_ge(c_pool, 1)
            pool.affine_select(out=ident[:, :], in_=ident[:, :], compare_op=ALU.not_equal, fill=1.0,
                               base=0, pattern=[[-1, P]], channel_multiplier=1).then_inc(c_pool, 1)
            pool.memset(neg_half[:, :], -0.5).then_inc(c_pool, 1)
            pool.memset(eps_b[:, :], EPS).then_inc(c_pool, 1)
            pool.memset(blockmask[:, :], 0.0).then_inc(c_pool, 1)
            for j in range(P // BLK):
                pool.wait_ge(c_pool, 5 + j)
                pool.memset(blockmask[j * BLK:(j + 1) * BLK, j * BLK:(j + 1) * BLK], 1.0).then_inc(c_pool, 1)
            pool.wait_ge(c_pool, 9)
            pool.memset(V1[:, :, :, :], 0.0).then_inc(c_pool, 1)
            pool.wait_ge(c_pool, 10)
            pool.memset(V1[:, :, :, AHD:AHD + 1], 1.0).then_inc(c_pool, 1)

            def rstd_of(n):
                pool.wait_ge(ln_mv, n * TPG + TPG)
                pool.tensor_tensor(veps[:, :], mv[:, :, 1], eps_b[:, :], ALU.add).then_inc(ln_eps, 1)
                pool.wait_ge(ln_eps, n + 1)
                pool.tensor_tensor(rstd[:, :], veps[:, :], neg_half[:, :], ALU.pow).then_inc(ln_rstd, 1)

            rstd_of(0)

            def attn(g, par):
                for h in range(AH):
                    if h == 6 and not is_last(g):
                        rstd_of(g + 1)
                    if h == 2 and not is_first(g):
                        residual_bias(g - 1)

            def residual_bias(g):
                if not is_first(g):
                    pool.wait_ge(a_x1, g)
                pool.tensor_tensor(xb[:, :, :], X[:, ds(g * TPG, TPG), :],
                                   bout_b[:, :].unsqueeze(1).to_broadcast([P, TPG, D]),
                                   ALU.add).then_inc(a_xb, 1)

            pool.wait_ge(ld_w, 5 * 16)
            pool.wait_ge(ld_x, 16)
            pool.memset(bqs[:, :], 0.0).then_inc(s_pool, 1)
            pool.memset(bks[:, :], 0.0).then_inc(s_pool, 1)
            pool.memset(lo_c[:, :], 0.0).then_inc(s_pool, 1)
            pool.wait_ge(s_pool, 3)
            pool.memset(lo_c[CW:P, :], 1.0).then_inc(s_pool, 1)
            pool.wait_ge(s_pool, 4)
            for i in range(2):
                pool.memset(V2[i][:, :, :, :], 0.0).then_inc(s_pool, 1)
                pool.wait_ge(s_pool, 5 + 3 * i)
                for half in range(2):
                    pool.memset(V2[i][:, half::2, :, 16 * half + XHD:16 * half + XHD + 1], 1.0).then_inc(s_pool, 1)
            for i in range(2):
                pool.memset(WQS[i][:, :, :, 3, :].bitcast(F32), 0.0).then_inc(s_pool, 1)
                pool.memset(WKS[i][:, :, :, 3, :].bitcast(F32), 0.0).then_inc(s_pool, 1)
            pool.wait_ge(s_pool, SPOOL)
            pool.memset(WD[FI:P, NP, :], 0.0).then_inc(f_zero, 1)
            pool.wait_ge(f_zero, 1)
            pool.memset(bd_rows[:, :], 0.0).then_inc(f_zero, 1)
            pool.memset(bias_rows[:, :], 0.0).then_inc(f_zero, 1)
            pool.memset(WS[:, :, 2 * E:P].bitcast(F32), 0.0).then_inc(f_zero, 1)
            pool.wait_ge(c_wT, 5)
            pool.memset(raw[:, :, NP, FI:P], 0.0).then_inc(f_zero, 1)
            walk(pool, attn)
            residual_bias(G - 1)

            def split_experts():
                pool.wait_ge(ld_raw, 4 * 16)
                pool.wait_ge(f_zero, 5)
                for i, dst in enumerate((GATE, UP)):
                    pool.tensor_copy(dst[0][:, :, :], raw[:, i]).then_inc(f_pool, 1)
                    pool.wait_ge(f_pool, 2 * i + 1)
                    pool.tensor_tensor(dst[1][:, :, :], raw[:, i], dst[0][:, :, :].bitcast(F32),
                                       ALU.subtract).then_inc(f_pool, 1)

            def residual_bias_x(g):
                if not is_first(g):
                    pool.wait_ge(b_x2, g)
                pool.tensor_tensor(xb[:, :, :], X[:, ds(g * TPG, TPG), :],
                                   bo_b[:, :].unsqueeze(1).to_broadcast([P, TPG, D]),
                                   ALU.add).then_inc(b_xb, 1)

            def xattn(g, par):
                if not is_first(g):
                    residual_bias_x(g - 1)
                if not is_last(g):
                    rstd_of(g + 1 + G)
                if is_first(g):
                    split_experts()

            if phases > 1:
                pool.wait_ge(ld_b, LDB)
                pool.wait_ge(a_x1, G)
                rstd_of(G)
                walk(pool, xattn)
                residual_bias_x(G - 1)

            def experts(g, par):
                if not is_last(g):
                    rstd_of(g + 1 + 2 * G)

            if phases > 2:
                rstd_of(2 * G)
                walk(pool, experts)

        @block.scalar
        def _(act):
            act.wait_ge(c_wT, 1)
            act.activation(WVH[:, :], bank[6][:, 0:D], ACT.Copy).then_inc(c_hi, 1)
            act.activation(WOT[:, :], bank[6][:, D:2 * D], ACT.Copy).then_inc(c_hi, 1)
            for q in range(4):
                act.wait_ge(c_wT, q + 2)
                act.activation(CH[:, 4 * q:4 * q + 4, :], bank[q][:, :].rearrange("p (h f) -> p h f", f=NF),
                               ACT.Copy).then_inc(c_hi, 1)

            def xt_hi(n, par):
                act.wait_ge(xt_full, n + 1)
                act.activation(XTH[par][:, :], tbank[:, :], ACT.Copy).then_inc(xt_hi_ok, 1)

            xt_hi(0, 0)

            def drain_outputs(g):
                act.wait_ge(a_o, g * AH + AH)
                for r in range(2):
                    act.activation(OS[r][:, :, :], bank[5 + r][:, :].rearrange("p (b s) -> p b s", s=P),
                                   ACT.Copy).then_inc(a_os, 1)

            def ont_copy(g):
                act.wait_ge(a_ontp, g + 1)
                act.activation(ONT[:, :, :], tbank[:, :].rearrange("p (b s) -> p b s", s=P),
                               ACT.Copy).then_inc(a_ont, 1)

            def attn(g, par):
                for h in range(AH):
                    if h == 2:
                        if not is_first(g):
                            drain_outputs(g - 1)
                        act.wait_ge(a_vp, g + 1)
                        act.activation(V1[:, :, :, 0:AHD],
                                       tbank[:, :].rearrange("p (b h d) -> p b h d", b=TPG, d=AHD),
                                       ACT.Copy).then_inc(a_v1, 1)
                    if h == 5 and not is_first(g):
                        ont_copy(g - 1)
                    if h == 7 and not is_last(g):
                        xt_hi(g + 1, 1 - par)
                    for f in range(2):
                        n = 2 * h + f
                        act.wait_ge(a_feat, g * 16 + n + 1)
                        if f == 0:
                            act.activation(expf[n % 4], bank[n % 4][:, :], ACT.Exp).then_inc(a_exp, 1)
                        else:
                            act.activation(expf[n % 4], bank[n % 4][:, :], ACT.Relu, scale=-1.0).then_inc(a_neg, 1)
                            act.wait_ge(a_neg, g * AH + h + 1)
                            act.activation(expf[n % 4], expf[n % 4], ACT.Exp, scale=-1.0).then_inc(a_exp, 1)

            act.wait_ge(c_pool, 11)
            walk(act, attn)
            drain_outputs(G - 1)
            ont_copy(G - 1)

            def ctx_hi(g):
                act.wait_ge(b_ctx, g + 1)
                if not is_first(g):
                    act.wait_ge(b_split, g * 8)
                act.activation(HM[0][:, :], tbank[:, :], ACT.Copy, scale=lo_c[:, 0:1]).then_inc(b_cm, 1)

            def drain_outputs_x(g):
                act.wait_ge(b_pv, g * TPG + TPG)
                for r in range(2):
                    act.activation(OS[r][:, :, :], bank[4 + r][:, :].rearrange("p (b s) -> p b s", s=P),
                                   ACT.Copy).then_inc(b_os, 1)

            def ont_copy_x(g):
                act.wait_ge(b_ontp, g + 1)
                act.activation(ONT[:, :, :], tbank[:, :].rearrange("p (b s) -> p b s", s=P),
                               ACT.Copy).then_inc(b_ont, 1)

            def xattn(g, par):
                for r in range(8):
                    lo, bias = ((lo_q, bqm), (lo_k, bkm))[r // 4]
                    act.wait_ge(b_pp, g * 8 + r + 1)
                    if r < 2:
                        act.wait_ge(b_cs, g + 1)
                    else:
                        act.wait_ge(b_split, g * 8 + r - 1)
                    act.activation(HM[r % 2][:, :], bank[r % 4][:, :], ACT.Identity, scale=lo[:, 0:1],
                                   bias=bias[:, r % 4:r % 4 + 1]).then_inc(b_hm, 1)
                act.wait_ge(b_mtp, g + 1)
                if not is_first(g):
                    act.wait_ge(b_mq, g * 64)
                act.activation(MT[:, :], tbank[:, 0:P], ACT.Copy).then_inc(b_mt, 1)
                if not is_first(g):
                    drain_outputs_x(g - 1)
                for u in range(4 * TPG):
                    act.wait_ge(b_st, g * 16 + u + 1)
                    act.activation(PT[:, u, :, :], bank[u % 4][:, :].rearrange("p (g q) -> p g q", q=P),
                                   ACT.Exp, scale=float(XHD) ** -0.5).then_inc(b_exp, 1)
                    if u == 7 and not is_first(g):
                        ont_copy_x(g - 1)
                    if u == 13 and not is_last(g):
                        xt_hi(g + 1 + G, 1 - par)
                if not is_last(g):
                    ctx_hi(g + 1)

            if phases > 1:
                act.wait_ge(a_x1, G)
                act.wait_ge(s_dve, SDVE)
                act.wait_ge(s_pool, SPOOL)
                xt_hi(G, 0)
                ctx_hi(0)
                walk(act, xattn)
                drain_outputs_x(G - 1)
                ont_copy_x(G - 1)

            def sigmoids(g):
                act.wait_ge(r_lg, g + 1)
                act.activation(sig[:, :, :], lg[:, :, :], ACT.Sigmoid).then_inc(r_sig, 1)

            def weights_copy(g, par):
                act.wait_ge(r_wp, g + 1)
                act.activation(WT[par][:, :], tbank[:, :], ACT.Copy).then_inc(r_wt, 1)

            def drain_sum(g):
                act.wait_ge(f_d, g * NU + NU)
                act.activation(YS, bank[6][:, :], ACT.Identity, bias=BT[:, 49:50]).then_inc(f_y, 1)

            def experts(g, par):
                for u in range(NU):
                    act.wait_ge(f_g, g * NU + u + 1)
                    act.activation(silu[(par + u) % 2], bank[(par + u) % 2][:, :], ACT.Silu,
                                   bias=BT[:, u:u + 1]).then_inc(f_s, 1)
                    if u == 0 and not is_first(g):
                        drain_sum(g - 1)
                    if not is_last(g):
                        if u == 5:
                            xt_hi(g + 1 + 2 * G, 1 - par)
                        if u == 8:
                            sigmoids(g + 1)
                        if u == 13:
                            weights_copy(g + 1, 1 - par)

            if phases > 2:
                act.wait_ge(b_x2, G)
                xt_hi(2 * G, 0)
                sigmoids(0)
                act.wait_ge(f_prep, FPREP)
                weights_copy(0, 0)
                walk(act, experts)
                drain_sum(G - 1)

        @block.vector
        def _(dve):
            def ln_moments(n, g):
                for t in range(TPG):
                    dve.bn_stats(stats[:, t, :], X[:, ds(g * TPG + t, 1), :])
                dve.drain()
                for t in range(TPG):
                    dve.bn_aggr(mv[:, t, :], stats[:, t, :]).then_inc(ln_mv, 1)

            def ln_apply(n, g):
                dve.wait_ge(ln_rstd, n + 1)
                for t in range(TPG):
                    dve.tensor_scalar(xn[:, t:t + 1, :], X[:, ds(g * TPG + t, 1), :], mv[:, t, 0:1],
                                      rstd[:, t:t + 1], ALU.subtract, ALU.mult).then_inc(ln_xn, 1)

            dve.wait_ge(ld_x0, 16)
            ln_moments(0, 0)
            ln_apply(0, 0)
            dve.wait_ge(c_hi, 2)
            dve.tensor_tensor(WVL[:, :], bank[6][:, 0:D], WVH[:, :].bitcast(F32), ALU.subtract).then_inc(c_lo, 1)
            for q in range(4):
                dve.wait_ge(c_hi, q + 3)
                dve.tensor_tensor(CL[:, 4 * q:4 * q + 4, :],
                                  bank[q][:, :].rearrange("p (h f) -> p h f", f=NF),
                                  CH[:, 4 * q:4 * q + 4, :].bitcast(F32), ALU.subtract).then_inc(c_lo, 1)

            def xt_lo(n, par):
                dve.wait_ge(xt_hi_ok, n + 1)
                dve.tensor_tensor(XTL[par][:, :], tbank[:, :], XTH[par][:, :].bitcast(F32),
                                  ALU.subtract).then_inc(xt_lo_ok, 1)

            xt_lo(0, 0)

            def mask_scores(gh, par):
                dve.wait_ge(a_score, gh)
                dve.tensor_tensor(AM[par][:, :, :], bank[4][:, :].rearrange("p (b s) -> p b s", s=P),
                                  blockmask[:, :].unsqueeze(1).to_broadcast([P, TPG, P]),
                                  ALU.mult).then_inc(a_mask, 1)

            def normalise(g, r):
                ot = tbank[:, :].rearrange("p (b j c) -> p b j c", b=TPG, c=32)
                dve.wait_ge(a_ot, g * 2 + r + 1)
                dve.tensor_scalar(den[:, :, 0:4], ot[:, :, :, AHD], DEN_EPS, None, ALU.add).then_inc(a_den, 1)
                dve.wait_ge(a_den, g * 2 + r + 1)
                dve.reciprocal(rden[:, :, 0:4], den[:, :, 0:4]).then_inc(a_rden, 1)
                dve.wait_ge(a_rden, g * 2 + r + 1)
                dve.tensor_tensor(ON[:, :, r * 64:r * 64 + 64].rearrange("p b (j c) -> p b j c", c=AHD),
                                  ot[:, :, :, 0:AHD],
                                  rden[:, :, 0:4].unsqueeze(3).to_broadcast([P, TPG, 4, AHD]),
                                  ALU.mult).then_inc(a_norm, 1)

            def residual(g):
                dve.wait_ge(a_proj, g + 1)
                dve.wait_ge(a_xb, g + 1)
                dve.tensor_tensor(X[:, ds(g * TPG, TPG), :], tbank[:, :].rearrange("p (b d) -> p b d", d=D),
                                  xb[:, :, :], ALU.add).then_inc(a_x1, 1)

            def attn(g, par):
                for h in range(AH):
                    gh = g * AH + h
                    dve.wait_ge(a_exp, gh * 2 + 1)
                    ek = expf[(2 * h) % 4]
                    eq = expf[(2 * h + 1) % 4]
                    dve.tensor_scalar(ek[:, :], ek[:, :], 1.0, None, ALU.min).then_inc(a_mink, 1)
                    if not (is_first(g) and h == 0):
                        mask_scores(gh, (h + 1) % 2)
                    dve.wait_ge(a_mink, gh + 1)
                    dve.scalar_tensor_tensor(out=phiK[h % 2][:, :], in0=bank[(2 * h) % 4][:, :], scalar=1.0,
                                             in1=ek[:, :], op0=ALU.add, op1=ALU.max).then_inc(a_phi, 1)
                    dve.wait_ge(a_exp, gh * 2 + 2)
                    dve.scalar_tensor_tensor(out=phiQ[h % 2][:, :], in0=bank[(2 * h + 1) % 4][:, :], scalar=0.0,
                                             in1=eq[:, :], op0=ALU.max, op1=ALU.add).then_inc(a_phi, 1)
                    if h == 2 and not is_first(g):
                        normalise(g - 1, 0)
                    if h == 3 and not is_first(g):
                        normalise(g - 1, 1)
                    if h == 4 and not is_last(g):
                        ln_moments(g + 1, g + 1)
                    if h == 5 and not is_first(g):
                        residual(g - 1)
                    if h == 6 and not is_last(g):
                        ln_apply(g + 1, g + 1)
                    if h == 7 and not is_last(g):
                        xt_lo(g + 1, 1 - par)

            dve.wait_ge(ld_x, 16)
            dve.wait_ge(c_pool, 9)
            walk(dve, attn)
            mask_scores(G * AH, 1)
            normalise(G - 1, 0)
            normalise(G - 1, 1)
            residual(G - 1)

            def stack_weights():
                cnt = [0]

                def done(ins):
                    cnt[0] += 1
                    ins.then_inc(s_dve, 1)

                dve.wait_ge(ld_b, LDB)
                dve.wait_ge(s_pool, SPOOL)
                for i, w in enumerate((wqx, wkx)):
                    done(dve.tensor_copy(wx_hi[:, i, :], w[:, :]))
                done(dve.tensor_copy(WVX[0][:, :], wvx[:, :]))
                dve.wait_ge(s_dve, 3)
                for i, w in enumerate((wqx, wkx)):
                    done(dve.tensor_tensor(wx_lo[:, i, :], w[:, :], wx_hi[:, i, :].bitcast(F32), ALU.subtract))
                done(dve.tensor_tensor(WVX[1][:, :], wvx[:, :], WVX[0][:, :].bitcast(F32), ALU.subtract))
                kinds = ident[:, :].rearrange("p (j t d) -> p t j d", j=4, d=XHD)
                done(dve.tensor_reduce(lo_k[:, :], kinds[:, 1], AX.XY, ALU.add))
                done(dve.tensor_reduce(lo_q[:, :], kinds[:, 2], AX.XY, ALU.add))
                done(dve.tensor_reduce(ones_k[:, :], kinds[:, 3, :, 0:2], AX.XY, ALU.add))
                dve.wait_ge(s_dve, 9)
                for part, w in enumerate((wx_hi, wx_lo)):
                    for i, stacked in enumerate((WQS, WKS)):
                        v = w[:, i, :].bitcast(F32).rearrange("p (g j d) -> p (g j) d", g=XG, j=4)
                        for t in range(3):
                            done(dve.tensor_copy(
                                stacked[part][:, :, :, t, :].rearrange("p g j d -> p (g j) d"), v))
                done(dve.tensor_scalar(bks[:, :], bks[:, :], ones_k[:, 0:1], None, ALU.add))
                dve.wait_ge(s_dve, 22)
                done(dve.tensor_scalar(bqm[:, :], bqs[:, :], lo_q[:, 0:1], None, ALU.mult))
                done(dve.tensor_scalar(bkm[:, :], bks[:, :], lo_k[:, 0:1], None, ALU.mult))
                assert cnt[0] == SDVE

            def ctx_lo(g, par):
                dve.wait_ge(b_cm, g + 1)
                dve.tensor_tensor(CS[par][:, :], tbank[:, :], HM[0][:, :].bitcast(F32), ALU.subtract).then_inc(b_cs, 1)

            def normalise_x(g, r):
                ot = tbank[:, :].rearrange("p (b c w) -> p b c w", b=TPG, w=16)
                dve.wait_ge(b_ot, g * 2 + r + 1)
                dve.reciprocal(rden[:, :, :], ot[:, :, :, XHD]).then_inc(b_rden, 1)
                dve.wait_ge(b_rden, g * 2 + r + 1)
                dve.tensor_tensor(ON[:, :, r * 64:r * 64 + 64].rearrange("p b (c d) -> p b c d", d=XHD),
                                  ot[:, :, :, 0:XHD],
                                  rden[:, :, :].unsqueeze(3).to_broadcast([P, TPG, 8, XHD]),
                                  ALU.mult).then_inc(b_norm, 1)

            def residual_x(g):
                dve.wait_ge(b_proj, g + 1)
                dve.wait_ge(b_xb, g + 1)
                dve.tensor_tensor(X[:, ds(g * TPG, TPG), :], tbank[:, :].rearrange("p (b d) -> p b d", d=D),
                                  xb[:, :, :], ALU.add).then_inc(b_x2, 1)

            def xattn(g, par):
                for r in range(8):
                    gi = r % 4
                    dst, bias = ((QS, bqs), (KS, bks))[r // 4]
                    dve.wait_ge(b_hm, g * 8 + r + 1)
                    if r == 0 and not is_first(g):
                        dve.wait_ge(b_st, g * 16)
                    dve.scalar_tensor_tensor(out=dst[:, gi, :], in0=bank[r % 4][:, :], scalar=bias[:, gi:gi + 1],
                                             in1=HM[r % 2][:, :].bitcast(F32), op0=ALU.add,
                                             op1=ALU.subtract).then_inc(b_split, 1)
                dve.wait_ge(b_vp, g + 1)
                for half in range(2):
                    dve.tensor_tensor(
                        V2[par][:, half::2, :, 16 * half:16 * half + XHD],
                        tbank[:, :].rearrange("p (c j d) -> p c j d", j=4, d=XHD)[:, half::2],
                        bv_b[:, :, :].rearrange("p b (g j d) -> p (b g) j d", g=XG, d=XHD)[:, half::2],
                        ALU.add).then_inc(b_v2, 1)
                for u in range(4 * TPG):
                    dve.wait_ge(b_s, g * 16 + u + 1)
                    dve.tensor_reduce(negm[:, u % 4, :, u // 4], bank[u % 4][:, :].rearrange("p (g k) -> p g k", k=P),
                                      AX.X, ALU.max, negate=True).then_inc(b_max, 1)
                dve.wait_ge(b_max, g * 16 + 16)
                m = negm[:, :, :, :].rearrange("p j g b -> p j (g b)")
                dve.tensor_copy(MM[:, :, 0, :], m).then_inc(b_mm, 1)
                dve.wait_ge(b_mm, g * 2 + 1)
                dve.tensor_tensor(MM[:, :, 1, :], m, MM[:, :, 0, :].bitcast(F32), ALU.subtract).then_inc(b_mm, 1)
                if not is_last(g):
                    ln_moments(g + 1 + G, g + 1)
                if not is_first(g):
                    normalise_x(g - 1, 0)
                    normalise_x(g - 1, 1)
                    residual_x(g - 1)
                if not is_last(g):
                    ln_apply(g + 1 + G, g + 1)
                    xt_lo(g + 1 + G, 1 - par)
                    ctx_lo(g + 1, 1 - par)

            if phases > 1:
                dve.wait_ge(a_x1, G)
                ln_moments(G, 0)
                stack_weights()
                ln_apply(G, 0)
                xt_lo(G, 0)
                ctx_lo(0, 0)
                walk(dve, xattn)
                normalise_x(G - 1, 0)
                normalise_x(G - 1, 1)
                residual_x(G - 1)

            def small_weights():
                dve.wait_ge(ld_f, LDF)
                dve.tensor_copy(WR[0][:, :], wr_sb[:, :]).then_inc(f_prep, 1)
                dve.tensor_copy(BD[0][:, :], bd_rows[:, :]).then_inc(f_prep, 1)
                dve.wait_ge(f_prep, 2)
                dve.tensor_tensor(WR[1][:, :], wr_sb[:, :], WR[0][:, :].bitcast(F32), ALU.subtract).then_inc(f_prep, 1)
                dve.tensor_tensor(BD[1][:, :], bd_rows[:, :], BD[0][:, :].bitcast(F32), ALU.subtract).then_inc(f_prep, 1)
                dve.tensor_tensor(SEL.rearrange("p u (e c) -> p (u e) c", e=2),
                                  ident[:, 0:E].unsqueeze(2).to_broadcast([P, E, FI]),
                                  ident[:, E:2 * E].unsqueeze(2).to_broadcast([P, E, FI]),
                                  ALU.add).then_inc(f_prep, 1)
                dve.wait_ge(f_bt, 1)
                dve.tensor_copy(BT[:, :], tbank[:, 0:64]).then_inc(f_prep, 1)

            def route_logits(g):
                dve.wait_ge(r_lp, g + 1)
                if not is_first(g):
                    dve.wait_ge(r_sig, g)
                dve.tensor_tensor(lg[:, :, :], tbank[:, 0:TPG * E].rearrange("p (t e) -> p t e", e=E),
                                  br_b[:, :].unsqueeze(1).to_broadcast([P, TPG, E]), ALU.add).then_inc(r_lg, 1)
                dve.drain()
                for t in range(TPG):
                    dve.max(top8[:, t, :], lg[:, t, :])
                dve.drain()
                for t in range(TPG):
                    dve.match_replace(zap[:, t, :], top8[:, t, :], lg[:, t, :], -3.0e38).then_inc(r_zap, 1)

            def route_weights(g):
                steps = [g * 8]

                def done(ins):
                    steps[0] = steps[0] + 1
                    ins.then_inc(r_w, 1)
                    dve.wait_ge(r_w, steps[0])

                dve.wait_ge(r_zap, g * TPG + TPG)
                done(dve.tensor_tensor(wfull[:, :, :], lg[:, :, :], zap[:, :, :], ALU.not_equal))
                dve.wait_ge(r_sig, g + 1)
                done(dve.tensor_tensor(wsel[:, :, :], wfull[:, :, :], sig[:, :, :], ALU.mult))
                done(dve.tensor_reduce(wsum[:, :], wsel[:, :, :], AX.X, ALU.add))
                done(dve.tensor_scalar(winv[:, :], wsum[:, :], 1e-9, None, ALU.add))
                done(dve.reciprocal(wsum[:, :], winv[:, :]))
                done(dve.tensor_tensor(wfull[:, :, :], wsel[:, :, :],
                                       wsum[:, :].unsqueeze(2).to_broadcast([P, TPG, E]), ALU.mult))
                done(dve.tensor_copy(WS[:, :, 0:E], wfull[:, :, :]))
                done(dve.tensor_tensor(WS[:, :, E:2 * E], wfull[:, :, :], WS[:, :, 0:E].bitcast(F32), ALU.subtract))

            def output(g, par):
                dve.wait_ge(f_yt, g + 1)
                if not (isinstance(g, int) and g < 2):
                    dve.wait_ge(st_y[par], (g - par) * 8)
                dve.tensor_tensor(OST[par], X[:, ds(g * TPG, TPG), :],
                                  tbank[:, :].rearrange("p (b d) -> p b d", d=D), ALU.add).then_inc(f_o, 1)

            def experts(g, par):
                for u in range(NU):
                    n = g * NU + u
                    k = (par + u) % 2
                    dve.wait_ge(f_s, n + 1)
                    dve.wait_ge(f_u, n + 1)
                    if not (is_first(g) and u < 2):
                        dve.wait_ge(f_d, n - 1)
                    dst = upm[k] if u < NP else hid[k]
                    dve.scalar_tensor_tensor(out=dst, in0=bank[2 + k][:, :], scalar=BT[:, 32 + u:33 + u],
                                             in1=silu[k], op0=ALU.add, op1=ALU.mult).then_inc(f_t, 1)
                    if u < NP:
                        dve.wait_ge(f_w, g * NP + u + 1)
                        dve.wait_ge(f_t, n + 1)
                        dve.tensor_tensor(hid[k], upm[k], bank[4 + u % 2][:, :], ALU.mult).then_inc(f_h, 1)
                    if u == 2 and not is_first(g):
                        output(g - 1, 1 - par)
                    if not is_last(g):
                        if u == 1:
                            ln_moments(g + 1 + 2 * G, g + 1)
                        if u == 3:
                            ln_apply(g + 1 + 2 * G, g + 1)
                        if u == 5:
                            xt_lo(g + 1 + 2 * G, 1 - par)
                        if u == 8:
                            route_logits(g + 1)
                        if u == 10:
                            route_weights(g + 1)

            if phases > 2:
                ln_moments(2 * G, 0)
                ln_apply(2 * G, 0)
                dve.wait_ge(b_st, G * 16)
                small_weights()
                xt_lo(2 * G, 0)
                route_logits(0)
                route_weights(0)
                walk(dve, experts)
                output(G - 1, 1)

        @block.tensor
        def _(pe):
            def product3(dst, wh, wl, mh, ml, start=True, stop=True):
                pe.matmul(dst, wh, mh, start=start, stop=False)
                pe.matmul(dst, wh, ml, start=False, stop=False)
                return pe.matmul(dst, wl, mh, start=False, stop=stop)

            def transposes(src, n=TPG):
                for t in range(n):
                    last = pe.transpose(tbank[:, t * P:(t + 1) * P], src[:, t, :], ident[:, :])
                return last

            pe.wait_ge(c_pool, 2)
            pe.wait_ge(ld_w, 5 * 16)
            pe.transpose(bank[6][:, 0:D], wv_rows[:, :], ident[:, :])
            pe.transpose(bank[6][:, D:2 * D], wout_rows[:, :], ident[:, :]).then_inc(c_wT, 1)
            for q in range(4):
                for j in range(4):
                    h = 4 * q + j
                    last = pe.matmul(bank[q][:, j * NF:(j + 1) * NF], wqk_rows[:, h, :], proj_sb[:, h % AH, :],
                                     start=True, stop=True)
                last.then_inc(c_wT, 1)

            def norm_transposed(n):
                pe.wait_ge(ln_xn, n * TPG + TPG)
                transposes(xn).then_inc(xt_full, 1)

            norm_transposed(0)
            def scores(gh, par):
                pe.wait_ge(a_phi, gh * 2 + 2)
                if not (isinstance(gh, int) and gh == 0):
                    pe.wait_ge(a_mask, gh)
                for b in range(TPG):
                    last = pe.matmul(bank[4][:, b * P:(b + 1) * P], phiK[par][:, b * P:(b + 1) * P],
                                     phiQ[par][:, b * P:(b + 1) * P], start=True, stop=True)
                last.then_inc(a_score, 1)

            def outputs(gh, h):
                pe.wait_ge(a_mask, gh + 1)
                j = h % 4
                for b in range(TPG):
                    last = pe.matmul(bank[5 + h // 4][32 * j:32 * j + 32, b * P:(b + 1) * P],
                                     V1[:, b, h, :], AM[h % 2][:, b, :], start=True, stop=True)
                last.then_inc(a_o, 1)

            def values(g, par):
                for b in range(TPG):
                    t = slice(b * P, (b + 1) * P)
                    last = product3(tbank[:, t], XTH[par][:, t], XTL[par][:, t], WVH[:, :], WVL[:, :])
                last.then_inc(a_vp, 1)

            def token_major(g, r):
                transposes(OS[r]).then_inc(a_ot, 1)

            def feature_major(g):
                pe.wait_ge(a_norm, g * 2 + 2)
                transposes(ON).then_inc(a_ontp, 1)

            def project(g):
                pe.wait_ge(a_ont, g + 1)
                for b in range(TPG):
                    last = pe.matmul(tbank[:, b * P:(b + 1) * P], ONT[:, b, :], WOT[:, :], start=True, stop=True)
                last.then_inc(a_proj, 1)

            def attn(g, par):
                for h in range(AH):
                    gh = g * AH + h
                    if h == 0:
                        pe.wait_ge(xt_lo_ok, g + 1)
                    for f in range(2):
                        n = 2 * h + f
                        head = (1 - f) * AH + h
                        if not (is_first(g) and n < 4):
                            pe.wait_ge(a_phi, g * 16 + n - 3)
                        product3(bank[n % 4][:, :], CH[:, head, :], CL[:, head, :],
                                 XTH[par][:, :], XTL[par][:, :]).then_inc(a_feat, 1)
                    if not (is_first(g) and h == 0):
                        scores(gh - 1, (h + 1) % 2)
                    if h == 2:
                        pe.wait_ge(a_v1, g + 1)
                    if not (is_first(g) and h < 2):
                        outputs(gh - 2, (h - 2) % AH)
                    if h == 1:
                        values(g, par)
                    if h == 2 and not is_first(g):
                        token_major(g - 1, 0)
                    if h == 3 and not is_first(g):
                        pe.wait_ge(a_norm, (g - 1) * 2 + 1)
                        token_major(g - 1, 1)
                    if h == 4 and not is_first(g):
                        feature_major(g - 1)
                    if h == 5 and not is_first(g):
                        project(g - 1)
                    if h == 6 and not is_last(g):
                        if not is_first(g):
                            pe.wait_ge(a_x1, g)
                        norm_transposed(g + 1)

            pe.wait_ge(c_lo, 5)
            walk(pe, attn)
            scores(G * AH - 1, 1)
            outputs(G * AH - 2, AH - 2)
            outputs(G * AH - 1, AH - 1)
            pe.wait_ge(a_os, G * 2)
            token_major(G - 1, 0)
            pe.wait_ge(a_norm, (G - 1) * 2 + 1)
            token_major(G - 1, 1)
            feature_major(G - 1)
            project(G - 1)

            def ctx_transposed(g, par):
                pe.wait_ge(ld_c[par], (g - par) * 16 + 32)
                for b in range(TPG):
                    last = pe.transpose(tbank[:, b * P:(b + 1) * P],
                                        ctxr[par][:, b, :, :].rearrange("p i c -> p (i c)"), ident[:, :])
                last.then_inc(b_ctx, 1)

            def projections(g, par):
                pe.wait_ge(b_cs, g + 1)
                for r in range(8):
                    gi = r % 4
                    if r < 4 and not is_first(g):
                        pe.wait_ge(b_exp, g * 16 - 3 + r)
                    if r >= 4:
                        pe.wait_ge(b_split, g * 8 + r - 3)
                    dst = bank[r % 4][:, :]
                    if r < 4:
                        w = [WQS[i][:, gi, :, :, :].rearrange("p j t d -> p (j t d)") for i in range(2)]
                        last = product3(dst, w[0], w[1], XTH[par][:, :], XTL[par][:, :])
                    else:
                        w = [WKS[i][:, gi, :, :, :].rearrange("p j t d -> p (j t d)") for i in range(2)]
                        pe.matmul(dst, w[0], CS[par][:, :], start=True, stop=False)
                        last = pe.matmul(dst, w[1], CS[par][:, :], start=False, stop=True)
                    last.then_inc(b_pp, 1)

            def values_x(g, par):
                for b in range(TPG):
                    t = slice(b * P, (b + 1) * P)
                    pe.matmul(tbank[:, t], CS[par][:, t], WVX[0][:, :], start=True, stop=False)
                    last = pe.matmul(tbank[:, t], CS[par][:, t], WVX[1][:, :], start=False, stop=True)
                last.then_inc(b_vp, 1)

            def scores_x(lhs, rhs, u):
                b, j = u // 4, u % 4
                for gi in range(XG):
                    rows, t = slice(32 * j, 32 * j + 32), slice(b * P, (b + 1) * P)
                    last = pe.matmul(bank[j][:, gi * P:(gi + 1) * P], lhs[rows, gi, t], rhs[rows, gi, t],
                                     start=True, stop=True)
                return last

            def attend(g, par, b):
                if b == 0:
                    pe.wait_ge(b_exp, g * 16 + 16)
                    if not is_first(g):
                        pe.wait_ge(b_os, g * 2)
                for r in range(2):
                    for half in range(2):
                        gi = 2 * r + half
                        for j in range(4):
                            last = pe.matmul(bank[4 + r][32 * j:32 * j + 32, b * P:(b + 1) * P],
                                             V2[par][:, b * XG + gi, j, :], PT[:, b * 4 + j, gi, :],
                                             start=(half == 0), stop=(half == 1))
                last.then_inc(b_pv, 1)

            def token_major_x(g, r):
                pe.wait_ge(b_os, g * 2 + r + 1)
                transposes(OS[r]).then_inc(b_ot, 1)

            def feature_major_x(g):
                pe.wait_ge(b_norm, g * 2 + 2)
                transposes(ON).then_inc(b_ontp, 1)

            def project_x(g):
                pe.wait_ge(b_ont, g + 1)
                for b in range(TPG):
                    last = pe.matmul(tbank[:, b * P:(b + 1) * P], ONT[:, b, :], WOX[:, :], start=True, stop=True)
                last.then_inc(b_proj, 1)

            def xattn(g, par):
                projections(g, par)
                values_x(g, par)
                for u in range(4 * TPG):
                    if u == 0:
                        pe.wait_ge(b_split, g * 8 + 8)
                    if u >= 4:
                        pe.wait_ge(b_max, g * 16 + u - 3)
                    scores_x(QS, KS, u).then_inc(b_s, 1)
                    if u % 8 == 5 and not is_first(g):
                        attend(g - 1, 1 - par, u // 8)
                if not is_first(g):
                    attend(g - 1, 1 - par, 2)
                pe.wait_ge(b_mm, g * 2 + 2)
                pe.wait_ge(b_v2, g * 2 + 2)
                pe.transpose(tbank[:, 0:P], MM[:, :, :, :].bitcast(F32).rearrange("p j t c -> p (j t c)"),
                             ident[:, :]).then_inc(b_mtp, 1)
                if not is_first(g):
                    attend(g - 1, 1 - par, 3)
                for u in range(4 * TPG):
                    if u == 0:
                        pe.wait_ge(b_mq, g * 64 + 64)
                    if u >= 4:
                        pe.wait_ge(b_exp, g * 16 + u - 3)
                    scores_x(KS, QS, u).then_inc(b_st, 1)
                    if u == 1 and not is_first(g):
                        token_major_x(g - 1, 0)
                    if u == 4 and not is_first(g):
                        pe.wait_ge(b_norm, (g - 1) * 2 + 1)
                        token_major_x(g - 1, 1)
                    if u == 7 and not is_first(g):
                        feature_major_x(g - 1)
                    if u == 9 and not is_first(g):
                        project_x(g - 1)
                    if u == 12 and not is_last(g):
                        pe.wait_ge(b_mt, g + 1)
                        if not is_first(g):
                            pe.wait_ge(b_x2, g)
                        norm_transposed(g + 1 + G)
                    if u == 15 and not is_last(g):
                        pe.wait_ge(xt_lo_ok, g + 2 + G)
                        ctx_transposed(g + 1, 1 - par)

            if phases > 1:
                pe.wait_ge(a_x1, G)
                norm_transposed(G)
                pe.wait_ge(xt_lo_ok, G + 1)
                ctx_transposed(0, 0)
                pe.wait_ge(s_dve, SDVE)
                walk(pe, xattn)
                for b in range(TPG):
                    attend(G - 1, 1, b)
                pe.wait_ge(b_x2, G - 1)
                token_major_x(G - 1, 0)
                pe.wait_ge(b_norm, (G - 1) * 2 + 1)
                token_major_x(G - 1, 1)
                feature_major_x(G - 1)
                project_x(G - 1)

            def logits(g, par):
                for t in range(TPG):
                    c = slice(t * P, (t + 1) * P)
                    last = product3(tbank[:, t * E:(t + 1) * E], XTH[par][:, c], XTL[par][:, c],
                                    WR[0][:, :], WR[1][:, :])
                last.then_inc(r_lp, 1)

            def weights_transposed(g):
                pe.wait_ge(r_w, g * 8 + 8)
                transposes(WS[:, :, :].bitcast(F32)).then_inc(r_wp, 1)

            def down(g, par, u):
                if u == 0:
                    if not is_first(g):
                        pe.wait_ge(f_y, g)
                    pe.matmul(bank[6][:, :], BD[0][:, :], WT[par][:, :], start=True, stop=False)
                    pe.matmul(bank[6][:, :], BD[1][:, :], WT[par][:, :], start=False, stop=False)
                if u < NP:
                    pe.wait_ge(f_h, g * NP + u + 1)
                else:
                    pe.wait_ge(f_t, g * NU + NU)
                pe.matmul(bank[6][:, :], WD[:, u, :], hid[(par + u) % 2], start=False,
                          stop=(u == NP)).then_inc(f_d, 1)

            def sum_transposed(g):
                pe.wait_ge(f_y, g + 1)
                transposes(YS.rearrange("p (t c) -> p t c", c=P)).then_inc(f_yt, 1)

            def experts(g, par):
                for u in range(NU):
                    n = g * NU + u
                    k = (par + u) % 2
                    if u == 0:
                        pe.wait_ge(xt_lo_ok, g + 1 + 2 * G)
                    if not (is_first(g) and u < 2):
                        pe.wait_ge(f_t, n - 1)
                    for w, b, full in ((GATE, k, f_g), (UP, 2 + k, f_u)):
                        product3(bank[b][:, :], w[0][:, u, :], w[1][:, u, :], XTH[par][:, :],
                                 XTL[par][:, :]).then_inc(full, 1)
                    if u < NP:
                        if u == 0:
                            pe.wait_ge(r_wt, g + 1)
                        if not (is_first(g) and u < 2):
                            pe.wait_ge(f_h, g * NP + u - 1)
                        pe.matmul(bank[4 + u % 2][:, :], SEL[:, u, :], WT[par][:, :],
                                  start=True, stop=True).then_inc(f_w, 1)
                    if u > 0:
                        down(g, par, u - 1)
                    elif not is_first(g):
                        down(g - 1, 1 - par, NP)
                    if u == 2 and not is_first(g):
                        sum_transposed(g - 1)
                    if not is_last(g):
                        if u == 4:
                            if not is_first(g):
                                pe.wait_ge(f_o, g)
                            norm_transposed(g + 1 + 2 * G)
                        if u == 7:
                            pe.wait_ge(xt_lo_ok, g + 2 + 2 * G)
                            logits(g + 1, 1 - par)
                        if u == 12:
                            weights_transposed(g + 1)

            if phases > 2:
                pe.wait_ge(b_x2, G)
                pe.wait_ge(ld_f, LDF)
                pe.transpose(tbank[:, 0:64], bias_rows[:, :], ident[0:64, 0:64]).then_inc(f_bt, 1)
                pe.wait_ge(f_prep, FPREP)
                norm_transposed(2 * G)
                pe.wait_ge(xt_lo_ok, 2 * G + 1)
                logits(0, 0)
                weights_transposed(0)
                pe.wait_ge(f_pool, 4)
                walk(pe, experts)
                down(G - 1, 1, NP)
                sum_transposed(G - 1)


_INS = ['x', 'ctx_512', 'L0_attn_w_qkv', 'L0_attn_w_out', 'L0_attn_b_out', 'L0_attn_proj',
        'L0_xattn_Wq', 'L0_xattn_bq', 'L0_xattn_Wk', 'L0_xattn_bk', 'L0_xattn_Wv', 'L0_xattn_bv',
        'L0_xattn_Wo', 'L0_xattn_bo', 'L0_ffn_Wr', 'L0_ffn_br', 'L0_ffn_Wg_s', 'L0_ffn_bg_s',
        'L0_ffn_Wu_s', 'L0_ffn_bu_s', 'L0_ffn_Wd_s', 'L0_ffn_bd_s', 'L0_ffn_Wg', 'L0_ffn_bg',
        'L0_ffn_Wu', 'L0_ffn_bu', 'L0_ffn_Wd', 'L0_ffn_bd']


def kernel(**inputs):
    import numpy as _np
    import concourse.bacc as _bacc
    from concourse import mybir as _mybir
    from concourse.bass_utils import run_bass_kernel_spmd as _run

    nc = _bacc.Bacc("TRN2", target_bir_lowering=False, num_devices=1)
    arrays, args = {}, []
    for name in _INS:
        a = _np.ascontiguousarray(inputs[name])
        arrays[f"in_{name}_dram"] = a
        args.append(nc.dram_tensor(f"in_{name}_dram", a.shape, _mybir.dt.from_np(a.dtype), kind="ExternalInput").ap())
    shape = tuple(inputs["x"].shape)
    args.append(nc.dram_tensor("out_0_dram", shape, _mybir.dt.float32, kind="ExternalOutput").ap())
    decoder_layer(nc, *args)
    r = _run(nc, [arrays], core_ids=[0])
    return r.results[0]["out_0_dram"]
```

```python
from contextlib import ExitStack

import concourse.bass as bass
from concourse import mybir

F32 = mybir.dt.float32
F32R = mybir.dt.float32r
ALU = mybir.AluOpType
ACT = mybir.ActivationFunctionType
AX = mybir.AxisListType

P = 128
D = 128
EPS = 1e-5
TPG = 4
GW = TPG * P

AH = 8
AHD = D // AH
NF = 128
BLK = 32
DEN_EPS = 1e-8

XH = 16
XHD = D // XH
XG = XH // 4
CW = 64

E = 32
TOPK = 8
FI = 64
NP = E // 2
NU = NP + 1


def ds(i, n):
    return bass.ds(i, n)


def decoder_layer(nc, x_in, ctx_in, w_qkv, w_out, b_out, proj, Wq, bq, Wk, bk, Wv, bv, Wo, bo,
                  Wr, br, Wg_s, bg_s, Wu_s, bu_s, Wd_s, bd_s, Wg, bg, Wu, bu, Wd, bd, out, phases=3):
    NT = x_in.shape[0] * x_in.shape[1] // P
    G = NT // TPG
    assert x_in.shape[1] == P and G % 2 == 0 and G >= 4

    x_tiles = x_in.rearrange("n p d -> p n d")
    ctx_tiles = ctx_in.rearrange("n p d -> p n d")
    out_tiles = out.rearrange("n p d -> p n d")

    with ExitStack() as ctx:
        def sb(name, shape, dt=F32):
            return ctx.enter_context(nc.sbuf_tensor(name, shape, dt))

        def sem(name):
            return ctx.enter_context(nc.semaphore(name))

        bank = [ctx.enter_context(nc.psum_tensor(f"bank{i}", [P, 512], F32)) for i in range(8)]
        tbank = bank[7]

        X = sb("X", [P, NT, D])
        ident = sb("ident", [P, P])
        neg_half = sb("neg_half", [P, TPG])
        eps_b = sb("eps_b", [P, TPG])
        stats = sb("stats", [P, TPG, 6])
        mv = sb("mv", [P, TPG, 2])
        veps = sb("veps", [P, TPG])
        rstd = sb("rstd", [P, TPG])
        xn = sb("xn", [P, TPG, D])
        xb = sb("xb", [P, TPG, D])
        XTH = [sb(f"XTH{i}", [P, GW], F32R) for i in range(2)]
        XTL = [sb(f"XTL{i}", [P, GW], F32R) for i in range(2)]

        raw_flat = sb("raw", [P, 2 * NU * P])
        raw = raw_flat[:, :].rearrange("p (a n c) -> p a n c", a=2, c=P)
        wqk_rows = raw_flat[0:AHD, 0:3 * AH * D].rearrange("p (h d) -> p h d", d=D)
        proj_sb = raw_flat[0:AHD, 3 * AH * D:4 * AH * D].rearrange("p (h f) -> p h f", f=NF)
        wrow0 = 4 * AH * D
        wv_rows = raw_flat[:, wrow0:wrow0 + D]
        wout_rows = raw_flat[:, wrow0 + D:wrow0 + 2 * D]
        CH = sb("CH", [P, 2 * AH, NF], F32R)
        CL = sb("CL", [P, 2 * AH, NF], F32R)
        WVH = sb("WVH", [P, D], F32R)
        WVL = sb("WVL", [P, D], F32R)
        WOT = sb("WOT", [P, D])
        bout_b = sb("bout_b", [P, D])
        blockmask = sb("blockmask", [P, P])
        work = sb("work", [P, 12 * GW])

        def part(n, width=GW):
            return work[:, n * GW:n * GW + width]

        expf = [part(i) for i in range(4)]
        phiK = [part(4 + i) for i in range(2)]
        phiQ = [part(6 + i) for i in range(2)]
        AM = [part(8 + i).rearrange("p (b s) -> p b s", s=P) for i in range(2)]
        V1 = part(10, 2 * GW).rearrange("p (b h c) -> p b h c", b=TPG, c=32)
        OS = [sb(f"OS{i}", [P, TPG, P]) for i in range(2)]
        den = sb("den", [P, TPG, 8])
        rden = sb("rden", [P, TPG, 8])
        ON = sb("ON", [P, TPG, D])
        ONT = sb("ONT", [P, TPG, P])

        ctxr = [sb(f"ctxr{i}", [P, TPG, 2, CW]) for i in range(2)]
        wqx = sb("wqx", [P, D])
        wkx = sb("wkx", [P, D])
        wvx = sb("wvx", [P, D])
        wx_hi = sb("wx_hi", [P, 2, D], F32R)
        wx_lo = sb("wx_lo", [P, 2, D], F32R)
        WQS = [sb(f"WQS{i}", [P, XG, 4, 4, XHD], F32R) for i in range(2)]
        WKS = [sb(f"WKS{i}", [P, XG, 4, 4, XHD], F32R) for i in range(2)]
        WVX = [sb(f"WVX{i}", [P, D], F32R) for i in range(2)]
        WOX = sb("WOX", [P, D])
        bo_b = sb("bo_b", [P, D])
        bv_b = sb("bv_b", [P, TPG, D])
        bqs = sb("bqs", [P, XG])
        bks = sb("bks", [P, XG])
        bqm = sb("bqm", [P, XG])
        bkm = sb("bkm", [P, XG])
        lo_q = sb("lo_q", [P, 1])
        lo_k = sb("lo_k", [P, 1])
        lo_c = sb("lo_c", [P, 1])
        ones_k = sb("ones_k", [P, 1])
        HM = [sb(f"HM{i}", [P, GW], F32R) for i in range(2)]
        HC = sb("HC", [P, GW], F32R)
        CS = [sb(f"CS{i}", [P, GW], F32R) for i in range(2)]
        QS = sb("QS", [P, XG, GW], F32R)
        KS = [sb(f"KS{i}", [P, GW], F32R) for i in range(2)]
        UP = [sb(f"UP{i}", [P, NU, P], F32R) for i in range(2)]
        KB = [t[:, 0:16, :].rearrange("p (b j) k -> p b j k", j=4) for t in (UP[0], UP[1], CH, CL)]
        V2 = [sb(f"V2{i}", [P, TPG * XG, 4, 32]) for i in range(2)]
        PT = [t.rearrange("p (b j q) -> p b j q", b=TPG, q=P)
              for t in (work[:, 0:4 * GW], work[:, 4 * GW:8 * GW], work[:, 8 * GW:12 * GW], raw_flat[:, 0:4 * GW])]
        negm = [sb(f"negm{i}", [P, 4, TPG]) for i in range(2)]
        MM = sb("MM", [P, 2, 4, TPG], F32R)
        MT = [sb(f"MT{i}", [32, P], F32R) for i in range(2)]

        GATE = [sb(f"GATE{i}", [P, NU, P], F32R) for i in range(2)]
        WD = raw[:, 0]
        wr_sb = sb("wr_sb", [P, E])
        WR = [sb(f"WR{i}", [P, E], F32R) for i in range(2)]
        br_b = sb("br_b", [P, E])
        bd_rows = sb("bd_rows", [P, D])
        BD = [sb(f"BD{i}", [P, D], F32R) for i in range(2)]
        bias_rows = sb("bias_rows", [64, P])
        BT = sb("BT", [P, 64])
        SEL = QS[:, :, :].rearrange("p g (u m) -> p (g u) m", m=P)
        lg = sb("lg", [P, TPG, E])
        sig = sb("sig", [P, TPG, E])
        zap = sb("zap", [P, TPG, E])
        wsel = sb("wsel", [P, TPG, E])
        wfull = sb("wfull", [P, TPG, E])
        top8 = sb("top8", [P, TPG, 8])
        wsum = sb("wsum", [P, TPG])
        winv = sb("winv", [P, TPG])
        WS = KS[0][:, :].rearrange("p (t c) -> p t c", c=P)
        WT = CS
        silu = [part(i) for i in range(2)]
        upm = [part(2 + i) for i in range(2)]
        hid = [part(4 + i) for i in range(2)]
        YS = part(6)
        OST = [part(7 + i).rearrange("p (b d) -> p b d", d=D) for i in range(2)]

        ld_w = sem("ld_w")
        ld_x0 = sem("ld_x0")
        ld_x = sem("ld_x")
        c_pool = sem("c_pool")
        c_wT = sem("c_wT")
        c_hi = sem("c_hi")
        c_lo = sem("c_lo")
        ln_mv = sem("ln_mv")
        ln_eps = sem("ln_eps")
        ln_rstd = sem("ln_rstd")
        ln_xn = sem("ln_xn")
        xt_full = sem("xt_full")
        xt_hi_ok = sem("xt_hi_ok")
        xt_lo_ok = sem("xt_lo_ok")
        a_feat = sem("a_feat")
        a_exp = sem("a_exp")
        a_mink = sem("a_mink")
        a_neg = sem("a_neg")
        a_phi = sem("a_phi")
        a_score = sem("a_score")
        a_mask = sem("a_mask")
        a_o = sem("a_o")
        a_os = sem("a_os")
        a_vp = sem("a_vp")
        a_v1 = sem("a_v1")
        a_ot = sem("a_ot")
        a_den = sem("a_den")
        a_rden = sem("a_rden")
        a_norm = sem("a_norm")
        a_ontp = sem("a_ontp")
        a_ont = sem("a_ont")
        a_proj = sem("a_proj")
        a_xb = sem("a_xb")
        a_x1 = sem("a_x1")
        ld_c = [sem(f"ld_c{i}") for i in range(2)]
        ld_b = sem("ld_b")
        s_pool = sem("s_pool")
        s_dve = sem("s_dve")
        b_ctx = sem("b_ctx")
        b_cm = sem("b_cm")
        b_cs = sem("b_cs")
        b_pp = sem("b_pp")
        b_hm = sem("b_hm")
        b_split = sem("b_split")
        b_vp = sem("b_vp")
        b_v2 = sem("b_v2")
        b_kb = [sem(f"b_kb{i}") for i in range(2)]
        b_s = sem("b_s")
        b_max = sem("b_max")
        b_mm = sem("b_mm")
        b_mtp = sem("b_mtp")
        b_mt = sem("b_mt")
        b_mq = sem("b_mq")
        b_st = sem("b_st")
        b_exp = sem("b_exp")
        b_pv = sem("b_pv")
        b_os = sem("b_os")
        b_ot = sem("b_ot")
        b_rden = sem("b_rden")
        b_norm = sem("b_norm")
        b_ontp = sem("b_ontp")
        b_ont = sem("b_ont")
        b_proj = sem("b_proj")
        b_xb = sem("b_xb")
        b_x2 = sem("b_x2")
        ld_f = sem("ld_f")
        ld_raw = sem("ld_raw")
        s_zero = sem("s_zero")
        f_pool = sem("f_pool")
        f_zero = sem("f_zero")
        f_prep = sem("f_prep")
        f_bt = sem("f_bt")
        f_g = sem("f_g")
        f_u = sem("f_u")
        f_w = sem("f_w")
        f_s = sem("f_s")
        f_t = sem("f_t")
        f_h = sem("f_h")
        f_d = sem("f_d")
        f_y = sem("f_y")
        f_yt = sem("f_yt")
        f_o = sem("f_o")
        st_y = [sem(f"st_y{i}") for i in range(2)]
        r_lp = sem("r_lp")
        r_lg = sem("r_lg")
        r_sig = sem("r_sig")
        r_zap = sem("r_zap")
        r_w = sem("r_w")
        r_wp = sem("r_wp")
        r_wt = sem("r_wt")
        st_out = sem("st_out")

        FPREP = 6
        LDF = 16 * 11
        SPOOL = 14
        SDVE = 24
        LDB = 16 * (4 + 2 + TPG + XH + 24)

        block = ctx.enter_context(nc.Block())

        def walk(eng, body):
            body(0, 0)
            body(1, 1)
            with eng.Fori(1, G // 2 - 1) as i:
                body(i * 2, 0)
                body(i * 2 + 1, 1)
            body(G - 2, 0)
            body(G - 1, 1)

        def walk_pipelined(eng, body):
            body(-1, 1)
            walk(eng, body)
            body(G, 0)

        def some(g):
            return not isinstance(g, int) or 0 <= g < G

        def needed(count):
            return not isinstance(count, int) or count > 0

        def after(g, gi, par, k):
            over = (gi + k) // XG
            return g + over, (gi + k) % XG, (par + over) % 2, g * XG + gi + k

        def head_copy(gi, j):
            rows = slice(32 * j, 32 * j + 32)
            return KB[gi][rows, :, j, :], KS[gi % 2][rows, :].bitcast(F32).rearrange("p (b k) -> p b k", k=P)

        def is_first(g):
            return isinstance(g, int) and g == 0

        def is_last(g):
            return isinstance(g, int) and g == G - 1

        @block.sync
        def _(sp):
            sp.dma_start(X[:, 0:TPG, :], x_tiles[:, 0:TPG, :]).then_inc(ld_x0, 16)
            sp.dma_start(wqk_rows[:, :, :], w_qkv.rearrange("(h r) d -> r h d", r=AHD)).then_inc(ld_w, 16)
            sp.dma_start(proj_sb[:, :, :], proj.rearrange("h r f -> r h f")).then_inc(ld_w, 16)
            sp.dma_start(wv_rows[:, :], w_qkv[2 * D:3 * D, :]).then_inc(ld_w, 16)
            sp.dma_start(wout_rows[:, :], w_out).then_inc(ld_w, 16)
            sp.dma_start(bout_b[:, :], b_out.partition_broadcast(P)).then_inc(ld_w, 16)
            sp.dma_start(X[:, TPG:NT, :], x_tiles[:, TPG:NT, :]).then_inc(ld_x, 16)
            for i in range(2):
                rows = slice(i * CW, (i + 1) * CW)
                sp.dma_start(wkx[rows, :], Wk).then_inc(ld_b, 16)
                sp.dma_start(wvx[rows, :], Wv).then_inc(ld_b, 16)
            sp.dma_start(wqx[:, :], Wq).then_inc(ld_b, 16)
            sp.dma_start(bo_b[:, :], bo.partition_broadcast(P)).then_inc(ld_b, 16)
            for b in range(TPG):
                sp.dma_start(bv_b[:, b, :], bv.partition_broadcast(P)).then_inc(ld_b, 16)
            for h in range(XH):
                gi, j = h // 4, h % 4
                row = (gi // 2) * 64 + j * 16 + (gi % 2) * 8
                sp.dma_start(WOX[row:row + XHD, :], Wo[h * XHD:(h + 1) * XHD, :]).then_inc(ld_b, 16)
            sp.wait_ge(s_pool, 2)
            for j in range(4):
                for t in range(3):
                    row = 32 * j + 8 * t
                    for dst, src in ((bqs, bq), (bks, bk)):
                        v = src.rearrange("(g j d) -> j d g", j=4, d=XHD)
                        sp.dma_start(dst[row:row + XHD, :], v[j], allow_slow_non_contiguous=True).then_inc(ld_b, 16)

            sp.wait_ge(f_zero, 3)
            sp.dma_start(wr_sb[:, :], Wr).then_inc(ld_f, 16)
            sp.dma_start(br_b[:, :], br.partition_broadcast(P)).then_inc(ld_f, 16)
            for i in range(2):
                sp.dma_start(bd_rows[i * E:(i + 1) * E, :], bd).then_inc(ld_f, 16)
            for row, pairs, shared in ((0, bg, bg_s), (32, bu, bu_s)):
                sp.dma_start(bias_rows[row:row + NP, :],
                             pairs.rearrange("(n e) i -> n (e i)", e=2)).then_inc(ld_f, 16)
                sp.dma_start(bias_rows[row + NP:row + NP + 1, 0:FI],
                             shared.rearrange("(a n) -> a n", a=1)).then_inc(ld_f, 16)
            sp.dma_start(bias_rows[49:50, :], bd_s.rearrange("(a n) -> a n", a=1)).then_inc(ld_f, 16)
            sp.wait_ge(c_wT, 5)
            for i, (pairs, shared) in enumerate(((Wg, Wg_s), (Wu, Wu_s))):
                sp.dma_start(raw[:, i, 0:NP, :].rearrange("p n (e c) -> p (n e) c", e=2),
                             pairs.rearrange("e d c -> d e c")).then_inc(ld_raw, 16)
                sp.dma_start(raw[:, i, NP, 0:FI], shared).then_inc(ld_raw, 16)

            def load_ctx(g, par):
                for i in range(2):
                    sp.dma_start(ctxr[par][:, :, i, :], ctx_tiles[:, ds(g * TPG, TPG), :]).then_inc(ld_c[par], 16)

            load_ctx(0, 0)

            def xattn(g, par):
                for gi in range(XG):
                    g1, _, par1, q1 = after(g, gi, par, 1)
                    if gi == 1 and some(g + 2):
                        if needed(g + 1):
                            sp.wait_ge(b_ctx, g + 1)
                        load_ctx(g + 2, par)
                    if some(g1):
                        if not (isinstance(q1, int) and q1 < 0):
                            sp.wait_ge(b_mt, q1 + 1)
                            for i in range(2):
                                sp.dma_start(QS[24 + i:P:32, (gi + 1) % XG, :].bitcast(F32),
                                             MT[(gi + 1) % 2][16 * i:16 * i + 16, :].bitcast(F32)).then_inc(b_mq, 16)

            if phases > 1:
                walk_pipelined(sp, xattn)
            if phases > 2:
                sp.wait_ge(b_pv, G * 8)
                sp.wait_ge(f_zero, 4)
                sp.dma_start(WD[:, 0:NP, :], Wd.rearrange("(n e) i d -> (e i) n d", e=2)).then_inc(ld_f, 16)
                sp.dma_start(WD[0:FI, NP, :], Wd_s).then_inc(ld_f, 16)

            def store(g, par):
                sp.wait_ge(f_o, g + 1)
                sp.dma_start(out_tiles[:, ds(g * TPG, TPG), :], OST[par]).then_inc(st_y[par], 16)

            if phases > 2:
                walk(sp, store)
                for i in range(2):
                    sp.wait_ge(st_y[i], G * 8)
            if phases == 2:
                sp.wait_ge(b_x2, G)
                sp.dma_start(out_tiles, X[:, :, :]).then_inc(st_out, 16)
                sp.wait_ge(st_out, 16)
            if phases == 1:
                sp.wait_ge(a_x1, G)
                sp.dma_start(out_tiles, X[:, :, :]).then_inc(st_out, 16)
                sp.wait_ge(st_out, 16)

        @block.gpsimd
        def _(pool):
            pool.memset(ident[:, :], 0.0).then_inc(c_pool, 1)
            pool.wait_ge(c_pool, 1)
            pool.affine_select(out=ident[:, :], in_=ident[:, :], compare_op=ALU.not_equal, fill=1.0,
                               base=0, pattern=[[-1, P]], channel_multiplier=1).then_inc(c_pool, 1)
            pool.memset(neg_half[:, :], -0.5).then_inc(c_pool, 1)
            pool.memset(eps_b[:, :], EPS).then_inc(c_pool, 1)
            pool.memset(blockmask[:, :], 0.0).then_inc(c_pool, 1)
            for j in range(P // BLK):
                pool.wait_ge(c_pool, 5 + j)
                pool.memset(blockmask[j * BLK:(j + 1) * BLK, j * BLK:(j + 1) * BLK], 1.0).then_inc(c_pool, 1)
            pool.wait_ge(c_pool, 9)
            pool.memset(V1[:, :, :, :], 0.0).then_inc(c_pool, 1)
            pool.wait_ge(c_pool, 10)
            pool.memset(V1[:, :, :, AHD:AHD + 1], 1.0).then_inc(c_pool, 1)

            def rstd_of(n):
                pool.wait_ge(ln_mv, n * TPG + TPG)
                pool.tensor_tensor(veps[:, :], mv[:, :, 1], eps_b[:, :], ALU.add).then_inc(ln_eps, 1)
                pool.wait_ge(ln_eps, n + 1)
                pool.tensor_tensor(rstd[:, :], veps[:, :], neg_half[:, :], ALU.pow).then_inc(ln_rstd, 1)

            rstd_of(0)

            def attn(g, par):
                for h in range(AH):
                    if h == 1 and not is_last(g):
                        rstd_of(g + 1)
                    if h == 2 and not is_first(g):
                        residual_bias(g - 1)
                    if h == 7 and is_first(g):
                        split_experts(0, GATE)

            def residual_bias(g):
                if not is_first(g):
                    pool.wait_ge(a_x1, g)
                pool.tensor_tensor(xb[:, :, :], X[:, ds(g * TPG, TPG), :],
                                   bout_b[:, :].unsqueeze(1).to_broadcast([P, TPG, D]),
                                   ALU.add).then_inc(a_xb, 1)

            pool.wait_ge(ld_w, 5 * 16)
            pool.wait_ge(ld_x, 16)
            pool.memset(bqs[:, :], 0.0).then_inc(s_pool, 1)
            pool.memset(bks[:, :], 0.0).then_inc(s_pool, 1)
            pool.memset(lo_c[:, :], 0.0).then_inc(s_pool, 1)
            pool.wait_ge(s_pool, 3)
            pool.memset(lo_c[CW:P, :], 1.0).then_inc(s_pool, 1)
            pool.wait_ge(s_pool, 4)
            for i in range(2):
                pool.memset(V2[i][:, :, :, :], 0.0).then_inc(s_pool, 1)
                pool.wait_ge(s_pool, 5 + 3 * i)
                for half in range(2):
                    pool.memset(V2[i][:, half::2, :, 16 * half + XHD:16 * half + XHD + 1], 1.0).then_inc(s_pool, 1)
            for i in range(2):
                pool.memset(WQS[i][:, :, :, 3, :].bitcast(F32), 0.0).then_inc(s_pool, 1)
                pool.memset(WKS[i][:, :, :, 3, :].bitcast(F32), 0.0).then_inc(s_pool, 1)
            pool.wait_ge(s_pool, SPOOL)
            pool.memset(bd_rows[:, :], 0.0).then_inc(f_zero, 1)
            pool.memset(bias_rows[:, :], 0.0).then_inc(f_zero, 1)
            pool.wait_ge(c_wT, 5)
            pool.memset(raw[:, :, NP, FI:P], 0.0).then_inc(f_zero, 1)

            def split_experts(i, dst):
                pool.wait_ge(ld_raw, 4 * 16)
                pool.wait_ge(f_zero, 3)
                pool.tensor_copy(dst[0][:, :, :], raw[:, i]).then_inc(f_pool, 1)
                pool.wait_ge(f_pool, 2 * i + 1)
                pool.tensor_tensor(dst[1][:, :, :], raw[:, i], dst[0][:, :, :].bitcast(F32),
                                   ALU.subtract).then_inc(f_pool, 1)

            for i in range(2):
                pool.memset(KB[i].bitcast(F32), 0.0).then_inc(s_zero, 1)

            walk(pool, attn)
            residual_bias(G - 1)

            def residual_bias_x(g):
                if not is_first(g):
                    pool.wait_ge(b_x2, g)
                pool.tensor_tensor(xb[:, :, :], X[:, ds(g * TPG, TPG), :],
                                   bo_b[:, :].unsqueeze(1).to_broadcast([P, TPG, D]),
                                   ALU.add).then_inc(b_xb, 1)

            def xattn(g, par):
                for gi in range(XG):
                    if gi == 1 and some(g - 1):
                        residual_bias_x(g - 1)
                    if gi == 2 and some(g + 2):
                        rstd_of(g + 2 + G)
                if is_last(g):
                    pool.wait_ge(b_st, 16 * g + 8)
                    split_experts(1, UP)

            if phases > 1:
                pool.wait_ge(ld_b, LDB)
                pool.wait_ge(a_x1, G)
                for i in range(2, 4):
                    pool.memset(KB[i].bitcast(F32), 0.0).then_inc(s_zero, 1)
                rstd_of(G)
                walk_pipelined(pool, xattn)
            if phases > 2:
                pool.wait_ge(b_pv, G * 8)
                pool.wait_ge(b_xb, G)
                pool.memset(WD[FI:P, NP, :], 0.0).then_inc(f_zero, 1)
                pool.wait_ge(f_zero, 4)
                pool.memset(WS[:, :, 2 * E:P].bitcast(F32), 0.0).then_inc(f_zero, 1)

            def experts(g, par):
                if not is_last(g):
                    rstd_of(g + 1 + 2 * G)

            if phases > 2:
                rstd_of(2 * G)
                walk(pool, experts)

        @block.scalar
        def _(act):
            act.wait_ge(c_wT, 1)
            act.activation(WVH[:, :], bank[6][:, 0:D], ACT.Copy).then_inc(c_hi, 1)
            act.activation(WOT[:, :], bank[6][:, D:2 * D], ACT.Copy).then_inc(c_hi, 1)
            for q in range(4):
                act.wait_ge(c_wT, q + 2)
                act.activation(CH[:, 4 * q:4 * q + 4, :], bank[q][:, :].rearrange("p (h f) -> p h f", f=NF),
                               ACT.Copy).then_inc(c_hi, 1)

            def xt_hi(n, par):
                act.wait_ge(xt_full, n + 1)
                act.activation(XTH[par][:, :], tbank[:, :], ACT.Copy).then_inc(xt_hi_ok, 1)

            xt_hi(0, 0)

            def drain_outputs(g):
                act.wait_ge(a_o, g * AH + AH)
                for r in range(2):
                    act.activation(OS[r][:, :, :], bank[5 + r][:, :].rearrange("p (b s) -> p b s", s=P),
                                   ACT.Copy).then_inc(a_os, 1)

            def ont_copy(g):
                act.wait_ge(a_ontp, g + 1)
                act.activation(ONT[:, :, :], tbank[:, :].rearrange("p (b s) -> p b s", s=P),
                               ACT.Copy).then_inc(a_ont, 1)

            def attn(g, par):
                for h in range(AH):
                    if h == 2:
                        if not is_first(g):
                            drain_outputs(g - 1)
                        act.wait_ge(a_vp, g + 1)
                        act.activation(V1[:, :, :, 0:AHD],
                                       tbank[:, :].rearrange("p (b h d) -> p b h d", b=TPG, d=AHD),
                                       ACT.Copy).then_inc(a_v1, 1)
                    if h == 5 and not is_first(g):
                        ont_copy(g - 1)
                    if h == 6 and not is_last(g):
                        xt_hi(g + 1, 1 - par)
                    for f in range(2):
                        n = 2 * h + f
                        act.wait_ge(a_feat, g * 16 + n + 1)
                        if f == 0:
                            act.activation(expf[n % 4], bank[n % 4][:, :], ACT.Exp).then_inc(a_exp, 1)
                        else:
                            act.activation(expf[n % 4], bank[n % 4][:, :], ACT.Relu, scale=-1.0).then_inc(a_neg, 1)
                            act.wait_ge(a_neg, g * AH + h + 1)
                            act.activation(expf[n % 4], expf[n % 4], ACT.Exp, scale=-1.0).then_inc(a_exp, 1)

            act.wait_ge(c_pool, 11)
            walk(act, attn)
            drain_outputs(G - 1)
            ont_copy(G - 1)

            def ctx_hi(g):
                act.wait_ge(b_ctx, g + 1)
                if needed(g):
                    act.wait_ge(b_cs, g)
                act.activation(HC[:, :], tbank[:, :], ACT.Copy, scale=lo_c[:, 0:1]).then_inc(b_cm, 1)

            def drain_outputs_x(g, r):
                act.wait_ge(b_pv, g * 8 + r * 4 + 4)
                if needed(g * 2 + r - 1):
                    act.wait_ge(b_ot, g * 2 + r - 1)
                act.activation(OS[r][:, :, :], bank[4][:, :].rearrange("p (b s) -> p b s", s=P),
                               ACT.Copy).then_inc(b_os, 1)

            def ont_copy_x(g):
                act.wait_ge(b_ontp, g + 1)
                act.activation(ONT[:, :, :], tbank[:, :].rearrange("p (b s) -> p b s", s=P),
                               ACT.Copy).then_inc(b_ont, 1)

            def hi_part(f, q, gi):
                lo, bias = ((lo_k, bkm), (lo_q, bqm))[f]
                act.wait_ge(b_pp, q * 2 + f + 1)
                if needed(q * 2 + f - 1):
                    act.wait_ge(b_split, q * 2 + f - 1)
                act.activation(HM[f][:, :], bank[5 + f][:, :], ACT.Identity, scale=lo[:, 0:1],
                               bias=bias[:, gi:gi + 1]).then_inc(b_hm, 1)

            def exp_scores(q, gi, b):
                act.wait_ge(b_st, q * 4 + b + 1)
                act.activation(PT[gi][:, b, :, :], bank[2 + b % 2][:, :].rearrange("p (j q) -> p j q", q=P),
                               ACT.Exp, scale=float(XHD) ** -0.5).then_inc(b_exp, 1)

            def xattn(g, par):
                for gi in range(XG):
                    g1, _, _, q1 = after(g, gi, par, 1)
                    g3, gi3, _, q3 = after(g, gi, par, 3)
                    q0 = g * XG + gi
                    if gi == 0 and some(g - 1):
                        drain_outputs_x(g - 1, 0)
                    if gi == 2 and some(g - 1):
                        drain_outputs_x(g - 1, 1)
                    if some(g3):
                        hi_part(0, q3, gi3)
                    if some(g):
                        exp_scores(q0, gi, 0)
                    if some(g1) and not (isinstance(q1, int) and q1 < 0):
                        act.wait_ge(b_mtp, q1 + 1)
                        if needed(q1 - 1):
                            act.wait_ge(b_mq, (q1 - 1) * 32)
                        act.activation(MT[(gi + 1) % 2][:, :], bank[6][0:32, 0:P], ACT.Copy).then_inc(b_mt, 1)
                    if gi == 0 and some(g + 1):
                        xt_hi(g + 1 + G, 1 - par)
                    if gi == 3 and some(g - 1):
                        ont_copy_x(g - 1)
                    if some(g):
                        exp_scores(q0, gi, 1)
                    if some(g3):
                        for j in range(2):
                            act.wait_ge(b_split, q3 * 2 + 1)
                            if isinstance(g, int) and g < 0:
                                act.wait_ge(s_zero, gi3 + 1)
                            if needed(q3 * 4 - 12):
                                act.wait_ge(b_st, q3 * 4 - 12)
                            to, frm = head_copy(gi3, j)
                            act.activation(to, frm, ACT.Copy).then_inc(b_kb[0], 1)
                        hi_part(1, q3, gi3)
                    if some(g):
                        exp_scores(q0, gi, 2)
                        exp_scores(q0, gi, 3)
                    if gi == 0 and some(g + 1):
                        ctx_hi(g + 1)

            if phases > 1:
                act.wait_ge(a_x1, G)
                act.wait_ge(s_dve, SDVE)
                act.wait_ge(s_pool, SPOOL)
                act.wait_ge(f_pool, 2)
                walk_pipelined(act, xattn)

            def sigmoids(g):
                act.wait_ge(r_lg, g + 1)
                act.activation(sig[:, :, :], lg[:, :, :], ACT.Sigmoid).then_inc(r_sig, 1)

            def weights_copy(g, par):
                act.wait_ge(r_wp, g + 1)
                act.activation(WT[par][:, :], tbank[:, :], ACT.Copy).then_inc(r_wt, 1)

            def drain_sum(g):
                act.wait_ge(f_d, g * NU + NU)
                act.activation(YS, bank[6][:, :], ACT.Identity, bias=BT[:, 49:50]).then_inc(f_y, 1)

            def experts(g, par):
                for u in range(NU):
                    act.wait_ge(f_g, g * NU + u + 1)
                    act.activation(silu[(par + u) % 2], bank[(par + u) % 2][:, :], ACT.Silu,
                                   bias=BT[:, u:u + 1]).then_inc(f_s, 1)
                    if u == 0 and not is_first(g):
                        drain_sum(g - 1)
                    if not is_last(g):
                        if u == 5:
                            xt_hi(g + 1 + 2 * G, 1 - par)
                        if u == 8:
                            sigmoids(g + 1)
                        if u == 13:
                            weights_copy(g + 1, 1 - par)

            if phases > 2:
                act.wait_ge(b_x2, G)
                xt_hi(2 * G, 0)
                sigmoids(0)
                act.wait_ge(f_prep, FPREP)
                weights_copy(0, 0)
                walk(act, experts)
                drain_sum(G - 1)

        @block.vector
        def _(dve):
            def ln_moments(n, g):
                for t in range(TPG):
                    dve.bn_stats(stats[:, t, :], X[:, ds(g * TPG + t, 1), :])
                dve.drain()
                for t in range(TPG):
                    dve.bn_aggr(mv[:, t, :], stats[:, t, :]).then_inc(ln_mv, 1)

            def ln_apply(n, g):
                dve.wait_ge(ln_rstd, n + 1)
                for t in range(TPG):
                    dve.tensor_scalar(xn[:, t:t + 1, :], X[:, ds(g * TPG + t, 1), :], mv[:, t, 0:1],
                                      rstd[:, t:t + 1], ALU.subtract, ALU.mult).then_inc(ln_xn, 1)

            dve.wait_ge(ld_x0, 16)
            ln_moments(0, 0)
            ln_apply(0, 0)
            dve.wait_ge(c_hi, 2)
            dve.tensor_tensor(WVL[:, :], bank[6][:, 0:D], WVH[:, :].bitcast(F32), ALU.subtract).then_inc(c_lo, 1)
            for q in range(4):
                dve.wait_ge(c_hi, q + 3)
                dve.tensor_tensor(CL[:, 4 * q:4 * q + 4, :],
                                  bank[q][:, :].rearrange("p (h f) -> p h f", f=NF),
                                  CH[:, 4 * q:4 * q + 4, :].bitcast(F32), ALU.subtract).then_inc(c_lo, 1)

            def xt_lo(n, par):
                dve.wait_ge(xt_hi_ok, n + 1)
                dve.tensor_tensor(XTL[par][:, :], tbank[:, :], XTH[par][:, :].bitcast(F32),
                                  ALU.subtract).then_inc(xt_lo_ok, 1)

            xt_lo(0, 0)

            def mask_scores(gh, par):
                dve.wait_ge(a_score, gh)
                dve.tensor_tensor(AM[par][:, :, :], bank[4][:, :].rearrange("p (b s) -> p b s", s=P),
                                  blockmask[:, :].unsqueeze(1).to_broadcast([P, TPG, P]),
                                  ALU.mult).then_inc(a_mask, 1)

            def normalise(g, r):
                ot = tbank[:, :].rearrange("p (b j c) -> p b j c", b=TPG, c=32)
                dve.wait_ge(a_ot, g * 2 + r + 1)
                dve.tensor_scalar(den[:, :, 0:4], ot[:, :, :, AHD], DEN_EPS, None, ALU.add).then_inc(a_den, 1)
                dve.wait_ge(a_den, g * 2 + r + 1)
                dve.reciprocal(rden[:, :, 0:4], den[:, :, 0:4]).then_inc(a_rden, 1)
                dve.wait_ge(a_rden, g * 2 + r + 1)
                dve.tensor_tensor(ON[:, :, r * 64:r * 64 + 64].rearrange("p b (j c) -> p b j c", c=AHD),
                                  ot[:, :, :, 0:AHD],
                                  rden[:, :, 0:4].unsqueeze(3).to_broadcast([P, TPG, 4, AHD]),
                                  ALU.mult).then_inc(a_norm, 1)

            def residual(g):
                dve.wait_ge(a_proj, g + 1)
                dve.wait_ge(a_xb, g + 1)
                dve.tensor_tensor(X[:, ds(g * TPG, TPG), :], tbank[:, :].rearrange("p (b d) -> p b d", d=D),
                                  xb[:, :, :], ALU.add).then_inc(a_x1, 1)

            def attn(g, par):
                for h in range(AH):
                    gh = g * AH + h
                    dve.wait_ge(a_exp, gh * 2 + 1)
                    ek = expf[(2 * h) % 4]
                    eq = expf[(2 * h + 1) % 4]
                    dve.tensor_scalar(ek[:, :], ek[:, :], 1.0, None, ALU.min).then_inc(a_mink, 1)
                    if not (is_first(g) and h == 0):
                        mask_scores(gh, (h + 1) % 2)
                    dve.wait_ge(a_mink, gh + 1)
                    dve.scalar_tensor_tensor(out=phiK[h % 2][:, :], in0=bank[(2 * h) % 4][:, :], scalar=1.0,
                                             in1=ek[:, :], op0=ALU.add, op1=ALU.max).then_inc(a_phi, 1)
                    dve.wait_ge(a_exp, gh * 2 + 2)
                    dve.scalar_tensor_tensor(out=phiQ[h % 2][:, :], in0=bank[(2 * h + 1) % 4][:, :], scalar=0.0,
                                             in1=eq[:, :], op0=ALU.max, op1=ALU.add).then_inc(a_phi, 1)
                    if h == 5 and is_first(g):
                        stack_weights()
                    if h == 2 and not is_first(g):
                        normalise(g - 1, 0)
                    if h == 3 and not is_first(g):
                        normalise(g - 1, 1)
                    if h == 1 and not is_last(g):
                        ln_moments(g + 1, g + 1)
                    if h == 4 and not is_last(g):
                        ln_apply(g + 1, g + 1)
                    if h == 6 and not is_last(g):
                        xt_lo(g + 1, 1 - par)
                    if h == 7 and not is_first(g):
                        residual(g - 1)

            def stack_weights():
                cnt = [0]

                def done(ins):
                    cnt[0] += 1
                    ins.then_inc(s_dve, 1)

                dve.wait_ge(ld_b, LDB)
                dve.wait_ge(s_pool, SPOOL)
                for i, w in enumerate((wqx, wkx)):
                    done(dve.tensor_copy(wx_hi[:, i, :], w[:, :]))
                done(dve.tensor_copy(WVX[0][:, :], wvx[:, :]))
                dve.wait_ge(s_dve, 3)
                for i, w in enumerate((wqx, wkx)):
                    done(dve.tensor_tensor(wx_lo[:, i, :], w[:, :], wx_hi[:, i, :].bitcast(F32), ALU.subtract))
                done(dve.tensor_tensor(WVX[1][:, :], wvx[:, :], WVX[0][:, :].bitcast(F32), ALU.subtract))
                kinds = ident[:, :].rearrange("p (j t d) -> p t j d", j=4, d=XHD)
                done(dve.tensor_reduce(lo_k[:, :], kinds[:, 1], AX.XY, ALU.add))
                done(dve.tensor_reduce(lo_q[:, :], kinds[:, 2], AX.XY, ALU.add))
                done(dve.tensor_reduce(ones_k[:, :], kinds[:, 3, :, 0:2], AX.XY, ALU.add))
                dve.wait_ge(s_dve, 9)
                for part, w in enumerate((wx_hi, wx_lo)):
                    for i, stacked in enumerate((WQS, WKS)):
                        v = w[:, i, :].bitcast(F32).rearrange("p (g j d) -> p (g j) d", g=XG, j=4)
                        for t in range(3):
                            done(dve.tensor_copy(
                                stacked[part][:, :, :, t, :].rearrange("p g j d -> p (g j) d"), v))
                done(dve.tensor_scalar(bks[:, :], bks[:, :], ones_k[:, 0:1], None, ALU.add))
                dve.wait_ge(s_dve, 22)
                done(dve.tensor_scalar(bqm[:, :], bqs[:, :], lo_q[:, 0:1], None, ALU.mult))
                done(dve.tensor_scalar(bkm[:, :], bks[:, :], lo_k[:, 0:1], None, ALU.mult))
                assert cnt[0] == SDVE

            dve.wait_ge(ld_x, 16)
            dve.wait_ge(c_pool, 9)
            walk(dve, attn)
            mask_scores(G * AH, 1)
            normalise(G - 1, 0)
            normalise(G - 1, 1)
            residual(G - 1)

            def ctx_lo(g, par):
                dve.wait_ge(b_cm, g + 1)
                dve.tensor_tensor(CS[par][:, :], tbank[:, :], HC[:, :].bitcast(F32), ALU.subtract).then_inc(b_cs, 1)

            def normalise_x(g, r):
                ot = tbank[:, :].rearrange("p (b c w) -> p b c w", b=TPG, w=16)
                dve.wait_ge(b_ot, g * 2 + r + 1)
                dve.reciprocal(rden[:, :, :], ot[:, :, :, XHD]).then_inc(b_rden, 1)
                dve.wait_ge(b_rden, g * 2 + r + 1)
                dve.tensor_tensor(ON[:, :, r * 64:r * 64 + 64].rearrange("p b (c d) -> p b c d", d=XHD),
                                  ot[:, :, :, 0:XHD],
                                  rden[:, :, :].unsqueeze(3).to_broadcast([P, TPG, 8, XHD]),
                                  ALU.mult).then_inc(b_norm, 1)

            def residual_x(g):
                dve.wait_ge(b_proj, g + 1)
                dve.wait_ge(b_xb, g + 1)
                dve.tensor_tensor(X[:, ds(g * TPG, TPG), :], tbank[:, :].rearrange("p (b d) -> p b d", d=D),
                                  xb[:, :, :], ALU.add).then_inc(b_x2, 1)

            def split(f, q, gi):
                dst, bias = ((KS[gi % 2][:, :], bks), (QS[:, gi, :], bqs))[f]
                dve.wait_ge(b_hm, q * 2 + f + 1)
                if f == 0 and needed(q - 1):
                    for i in range(2):
                        dve.wait_ge(b_kb[i], (q - 1) * 2)
                if f == 1 and needed(q - 3):
                    dve.wait_ge(b_st, (q - 3) * 4)
                dve.scalar_tensor_tensor(out=dst, in0=bank[5 + f][:, :], scalar=bias[:, gi:gi + 1],
                                         in1=HM[f][:, :].bitcast(F32), op0=ALU.add,
                                         op1=ALU.subtract).then_inc(b_split, 1)

            def maxima(q, gi, b):
                dve.wait_ge(b_s, q * 4 + b + 1)
                dve.tensor_reduce(negm[gi % 2][:, :, b], bank[b % 2][:, :].rearrange("p (j k) -> p j k", k=P),
                                  AX.X, ALU.max, negate=True).then_inc(b_max, 1)

            def split_maxima(q, gi):
                dve.wait_ge(b_max, q * 4 + 4)
                if needed(q):
                    dve.wait_ge(b_mtp, q)
                dve.tensor_copy(MM[:, 0, :, :], negm[gi % 2][:, :, :]).then_inc(b_mm, 1)
                dve.wait_ge(b_mm, q * 2 + 1)
                dve.tensor_tensor(MM[:, 1, :, :], negm[gi % 2][:, :, :], MM[:, 0, :, :].bitcast(F32),
                                  ALU.subtract).then_inc(b_mm, 1)

            def values_bias(g, par):
                dve.wait_ge(b_vp, g + 1)
                if needed(g - 1):
                    dve.wait_ge(b_pv, (g - 1) * 8)
                for half in range(2):
                    dve.tensor_tensor(
                        V2[par][:, half::2, :, 16 * half:16 * half + XHD],
                        tbank[:, :].rearrange("p (c j d) -> p c j d", j=4, d=XHD)[:, half::2],
                        bv_b[:, :, :].rearrange("p b (g j d) -> p (b g) j d", g=XG, d=XHD)[:, half::2],
                        ALU.add).then_inc(b_v2, 1)

            def xattn(g, par):
                for gi in range(XG):
                    g2, gi2, _, q2 = after(g, gi, par, 2)
                    g3, gi3, _, q3 = after(g, gi, par, 3)
                    s2 = some(g2) and not (isinstance(q2, int) and q2 < 0)
                    if s2:
                        maxima(q2, gi2, 0)
                    if some(g3):
                        split(0, q3, gi3)
                    if s2:
                        maxima(q2, gi2, 1)
                    if some(g3):
                        dve.wait_ge(b_split, q3 * 2 + 1)
                        if isinstance(g, int) and g < 0:
                            dve.wait_ge(s_zero, gi3 + 1)
                        if needed(q3 * 4 - 12):
                            dve.wait_ge(b_st, q3 * 4 - 12)
                        for j in range(2, 4):
                            to, frm = head_copy(gi3, j)
                            dve.tensor_copy(to, frm).then_inc(b_kb[1], 1)
                    if gi == 0 and some(g + 1):
                        xt_lo(g + 1 + G, 1 - par)
                    if gi == 1 and some(g - 1):
                        normalise_x(g - 1, 0)
                    if gi == 2 and some(g + 1):
                        values_bias(g + 1, 1 - par)
                    if some(g3):
                        split(1, q3, gi3)
                    if s2:
                        maxima(q2, gi2, 2)
                        maxima(q2, gi2, 3)
                        split_maxima(q2, gi2)
                    if gi == 0 and some(g + 1):
                        ctx_lo(g + 1, 1 - par)
                    if gi == 1 and some(g + 2):
                        ln_moments(g + 2 + G, g + 2)
                    if gi == 2 and some(g - 1):
                        normalise_x(g - 1, 1)
                    if gi == 3 and some(g + 2):
                        ln_apply(g + 2 + G, g + 2)
                    if gi == 3 and some(g - 1):
                        residual_x(g - 1)

            if phases > 1:
                dve.wait_ge(a_x1, G)
                ln_moments(G, 0)
                ln_apply(G, 0)
                walk_pipelined(dve, xattn)

            def small_weights():
                dve.wait_ge(ld_f, LDF)
                dve.tensor_copy(WR[0][:, :], wr_sb[:, :]).then_inc(f_prep, 1)
                dve.tensor_copy(BD[0][:, :], bd_rows[:, :]).then_inc(f_prep, 1)
                dve.wait_ge(f_prep, 2)
                dve.tensor_tensor(WR[1][:, :], wr_sb[:, :], WR[0][:, :].bitcast(F32), ALU.subtract).then_inc(f_prep, 1)
                dve.tensor_tensor(BD[1][:, :], bd_rows[:, :], BD[0][:, :].bitcast(F32), ALU.subtract).then_inc(f_prep, 1)
                dve.tensor_tensor(SEL.rearrange("p u (e c) -> p (u e) c", e=2),
                                  ident[:, 0:E].unsqueeze(2).to_broadcast([P, E, FI]),
                                  ident[:, E:2 * E].unsqueeze(2).to_broadcast([P, E, FI]),
                                  ALU.add).then_inc(f_prep, 1)
                dve.wait_ge(f_bt, 1)
                dve.tensor_copy(BT[:, :], tbank[:, 0:64]).then_inc(f_prep, 1)

            def route_logits(g):
                dve.wait_ge(r_lp, g + 1)
                if not is_first(g):
                    dve.wait_ge(r_sig, g)
                dve.tensor_tensor(lg[:, :, :], tbank[:, 0:TPG * E].rearrange("p (t e) -> p t e", e=E),
                                  br_b[:, :].unsqueeze(1).to_broadcast([P, TPG, E]), ALU.add).then_inc(r_lg, 1)
                dve.drain()
                for t in range(TPG):
                    dve.max(top8[:, t, :], lg[:, t, :])
                dve.drain()
                for t in range(TPG):
                    dve.match_replace(zap[:, t, :], top8[:, t, :], lg[:, t, :], -3.0e38).then_inc(r_zap, 1)

            def route_weights(g):
                steps = [g * 8]

                def done(ins):
                    steps[0] = steps[0] + 1
                    ins.then_inc(r_w, 1)
                    dve.wait_ge(r_w, steps[0])

                dve.wait_ge(r_zap, g * TPG + TPG)
                done(dve.tensor_tensor(wfull[:, :, :], lg[:, :, :], zap[:, :, :], ALU.not_equal))
                dve.wait_ge(r_sig, g + 1)
                done(dve.tensor_tensor(wsel[:, :, :], wfull[:, :, :], sig[:, :, :], ALU.mult))
                done(dve.tensor_reduce(wsum[:, :], wsel[:, :, :], AX.X, ALU.add))
                done(dve.tensor_scalar(winv[:, :], wsum[:, :], 1e-9, None, ALU.add))
                done(dve.reciprocal(wsum[:, :], winv[:, :]))
                done(dve.tensor_tensor(wfull[:, :, :], wsel[:, :, :],
                                       wsum[:, :].unsqueeze(2).to_broadcast([P, TPG, E]), ALU.mult))
                done(dve.tensor_copy(WS[:, :, 0:E], wfull[:, :, :]))
                done(dve.tensor_tensor(WS[:, :, E:2 * E], wfull[:, :, :], WS[:, :, 0:E].bitcast(F32), ALU.subtract))

            def output(g, par):
                dve.wait_ge(f_yt, g + 1)
                if not (isinstance(g, int) and g < 2):
                    dve.wait_ge(st_y[par], (g - par) * 8)
                dve.tensor_tensor(OST[par], X[:, ds(g * TPG, TPG), :],
                                  tbank[:, :].rearrange("p (b d) -> p b d", d=D), ALU.add).then_inc(f_o, 1)

            def experts(g, par):
                for u in range(NU):
                    n = g * NU + u
                    k = (par + u) % 2
                    dve.wait_ge(f_s, n + 1)
                    dve.wait_ge(f_u, n + 1)
                    if not (is_first(g) and u < 2):
                        dve.wait_ge(f_d, n - 1)
                    dst = upm[k] if u < NP else hid[k]
                    dve.scalar_tensor_tensor(out=dst, in0=bank[2 + k][:, :], scalar=BT[:, 32 + u:33 + u],
                                             in1=silu[k], op0=ALU.add, op1=ALU.mult).then_inc(f_t, 1)
                    if u < NP:
                        dve.wait_ge(f_w, g * NP + u + 1)
                        dve.wait_ge(f_t, n + 1)
                        dve.tensor_tensor(hid[k], upm[k], bank[4 + u % 2][:, :], ALU.mult).then_inc(f_h, 1)
                    if u == 2 and not is_first(g):
                        output(g - 1, 1 - par)
                    if not is_last(g):
                        if u == 1:
                            ln_moments(g + 1 + 2 * G, g + 1)
                        if u == 3:
                            ln_apply(g + 1 + 2 * G, g + 1)
                        if u == 5:
                            xt_lo(g + 1 + 2 * G, 1 - par)
                        if u == 8:
                            route_logits(g + 1)
                        if u == 10:
                            route_weights(g + 1)

            if phases > 2:
                ln_moments(2 * G, 0)
                ln_apply(2 * G, 0)
                dve.wait_ge(b_st, G * 16)
                small_weights()
                xt_lo(2 * G, 0)
                route_logits(0)
                route_weights(0)
                walk(dve, experts)
                output(G - 1, 1)

        @block.tensor
        def _(pe):
            def product3(dst, wh, wl, mh, ml, start=True, stop=True):
                pe.matmul(dst, wh, mh, start=start, stop=False)
                pe.matmul(dst, wh, ml, start=False, stop=False)
                return pe.matmul(dst, wl, mh, start=False, stop=stop)

            def transposes(src, n=TPG):
                for t in range(n):
                    last = pe.transpose(tbank[:, t * P:(t + 1) * P], src[:, t, :], ident[:, :])
                return last

            pe.wait_ge(c_pool, 2)
            pe.wait_ge(ld_w, 5 * 16)
            pe.transpose(bank[6][:, 0:D], wv_rows[:, :], ident[:, :])
            pe.transpose(bank[6][:, D:2 * D], wout_rows[:, :], ident[:, :]).then_inc(c_wT, 1)
            for q in range(4):
                for j in range(4):
                    h = 4 * q + j
                    last = pe.matmul(bank[q][:, j * NF:(j + 1) * NF], wqk_rows[:, h, :], proj_sb[:, h % AH, :],
                                     start=True, stop=True)
                last.then_inc(c_wT, 1)

            def norm_transposed(n):
                pe.wait_ge(ln_xn, n * TPG + TPG)
                transposes(xn).then_inc(xt_full, 1)

            norm_transposed(0)
            def scores(gh, par):
                pe.wait_ge(a_phi, gh * 2 + 2)
                if not (isinstance(gh, int) and gh == 0):
                    pe.wait_ge(a_mask, gh)
                for b in range(TPG):
                    last = pe.matmul(bank[4][:, b * P:(b + 1) * P], phiK[par][:, b * P:(b + 1) * P],
                                     phiQ[par][:, b * P:(b + 1) * P], start=True, stop=True)
                last.then_inc(a_score, 1)

            def outputs(gh, h):
                pe.wait_ge(a_mask, gh + 1)
                j = h % 4
                for b in range(TPG):
                    last = pe.matmul(bank[5 + h // 4][32 * j:32 * j + 32, b * P:(b + 1) * P],
                                     V1[:, b, h, :], AM[h % 2][:, b, :], start=True, stop=True)
                last.then_inc(a_o, 1)

            def values(g, par):
                for b in range(TPG):
                    t = slice(b * P, (b + 1) * P)
                    last = product3(tbank[:, t], XTH[par][:, t], XTL[par][:, t], WVH[:, :], WVL[:, :])
                last.then_inc(a_vp, 1)

            def token_major(g, r):
                transposes(OS[r]).then_inc(a_ot, 1)

            def feature_major(g):
                pe.wait_ge(a_norm, g * 2 + 2)
                transposes(ON).then_inc(a_ontp, 1)

            def project(g):
                pe.wait_ge(a_ont, g + 1)
                for b in range(TPG):
                    last = pe.matmul(tbank[:, b * P:(b + 1) * P], ONT[:, b, :], WOT[:, :], start=True, stop=True)
                last.then_inc(a_proj, 1)

            def attn(g, par):
                for h in range(AH):
                    gh = g * AH + h
                    if h == 0:
                        pe.wait_ge(xt_lo_ok, g + 1)
                    for f in range(2):
                        n = 2 * h + f
                        head = (1 - f) * AH + h
                        if not (is_first(g) and n < 4):
                            pe.wait_ge(a_phi, g * 16 + n - 3)
                        product3(bank[n % 4][:, :], CH[:, head, :], CL[:, head, :],
                                 XTH[par][:, :], XTL[par][:, :]).then_inc(a_feat, 1)
                    if not (is_first(g) and h == 0):
                        scores(gh - 1, (h + 1) % 2)
                    if h == 2:
                        pe.wait_ge(a_v1, g + 1)
                    if not (is_first(g) and h < 2):
                        outputs(gh - 2, (h - 2) % AH)
                    if h == 1:
                        if not is_first(g) and not (isinstance(g, int) and g == 1):
                            pe.wait_ge(a_x1, g - 1)
                        values(g, par)
                    if h == 2 and not is_first(g):
                        token_major(g - 1, 0)
                    if h == 3 and not is_first(g):
                        pe.wait_ge(a_norm, (g - 1) * 2 + 1)
                        token_major(g - 1, 1)
                    if h == 4 and not is_first(g):
                        feature_major(g - 1)
                    if h == 5 and not is_last(g):
                        if not is_first(g):
                            pe.wait_ge(a_ont, g)
                        norm_transposed(g + 1)
                    if h == 7 and not is_first(g):
                        if not is_last(g):
                            pe.wait_ge(xt_lo_ok, g + 2)
                        project(g - 1)

            pe.wait_ge(c_lo, 5)
            walk(pe, attn)
            scores(G * AH - 1, 1)
            outputs(G * AH - 2, AH - 2)
            outputs(G * AH - 1, AH - 1)
            pe.wait_ge(a_os, G * 2)
            token_major(G - 1, 0)
            pe.wait_ge(a_norm, (G - 1) * 2 + 1)
            token_major(G - 1, 1)
            feature_major(G - 1)
            project(G - 1)

            def ctx_transposed(g, par):
                pe.wait_ge(ld_c[par], (g - par) * 16 + 32)
                pe.wait_ge(xt_lo_ok, g + 1 + G)
                for b in range(TPG):
                    last = pe.transpose(tbank[:, b * P:(b + 1) * P],
                                        ctxr[par][:, b, :, :].rearrange("p i c -> p (i c)"), ident[:, :])
                last.then_inc(b_ctx, 1)

            def project_k(g, q, gi, par):
                if gi == 0:
                    pe.wait_ge(b_cs, g + 1)
                if needed(q):
                    pe.wait_ge(b_split, q * 2 - 1)
                w = [WKS[i][:, gi, :, :, :].rearrange("p j t d -> p (j t d)") for i in range(2)]
                pe.matmul(bank[5][:, :], w[0], CS[par][:, :], start=True, stop=False)
                pe.matmul(bank[5][:, :], w[1], CS[par][:, :], start=False, stop=True).then_inc(b_pp, 1)

            def project_q(g, q, gi, par):
                if gi == 0:
                    pe.wait_ge(xt_lo_ok, g + 1 + G)
                if needed(q - 1):
                    pe.wait_ge(b_mt, q - 1)
                elif needed(q):
                    pe.wait_ge(b_split, q * 2)
                w = [WQS[i][:, gi, :, :, :].rearrange("p j t d -> p (j t d)") for i in range(2)]
                product3(bank[6][:, :], w[0], w[1], XTH[par][:, :], XTL[par][:, :]).then_inc(b_pp, 1)

            def values_x(g, par):
                for b in range(TPG):
                    t = slice(b * P, (b + 1) * P)
                    pe.matmul(tbank[:, t], CS[par][:, t], WVX[0][:, :], start=True, stop=False)
                    last = pe.matmul(tbank[:, t], CS[par][:, t], WVX[1][:, :], start=False, stop=True)
                last.then_inc(b_vp, 1)

            def scores_by_query(q, gi, b):
                if b == 0:
                    for i in range(2):
                        pe.wait_ge(b_kb[i], q * 2 + 2)
                    pe.wait_ge(b_split, q * 2 + 2)
                if needed(q * 4 + b - 1):
                    pe.wait_ge(b_max, q * 4 + b - 1)
                pe.matmul(bank[b % 2][:, :], QS[:, gi, b * P:(b + 1) * P],
                          KB[gi][:, b, :, :].rearrange("p j k -> p (j k)"),
                          start=True, stop=True).then_inc(b_s, 1)

            def maxima_transposed(q):
                pe.wait_ge(b_mm, q * 2 + 2)
                pe.wait_ge(b_split, min(q * 2 + 4, 8 * G) if isinstance(q, int) else q * 2 + 4)
                if needed(q):
                    pe.wait_ge(b_mt, q)
                pe.transpose(bank[6][0:32, 0:P], MM[:, :, :, :].bitcast(F32).rearrange("p i j b -> p (i j b)"),
                             ident[:, :]).then_inc(b_mtp, 1)

            def scores_by_key(q, gi, b):
                if b == 0:
                    pe.wait_ge(b_mq, q * 32 + 32)
                if needed(q * 4 + b - 1):
                    pe.wait_ge(b_exp, q * 4 + b - 1)
                for j in range(4):
                    last = pe.matmul(bank[2 + b % 2][:, j * P:(j + 1) * P], KB[gi][:, b, j, :],
                                     QS[:, gi, b * P:(b + 1) * P], start=True, stop=True)
                last.then_inc(b_st, 1)

            def attend(g, par, r, b):
                if b == 0:
                    pe.wait_ge(b_exp, g * 16 + r * 8 + 8)
                    if needed(g * 2 + r):
                        pe.wait_ge(b_os, g * 2 + r)
                    if r == 0:
                        pe.wait_ge(b_v2, g * 2 + 2)
                for half in range(2):
                    gi = 2 * r + half
                    for j in range(4):
                        last = pe.matmul(bank[4][32 * j:32 * j + 32, b * P:(b + 1) * P],
                                         V2[par][:, b * XG + gi, j, :], PT[gi][:, b, j, :],
                                         start=(half == 0), stop=(half == 1))
                last.then_inc(b_pv, 1)

            def token_major_x(g, r):
                pe.wait_ge(b_os, g * 2 + r + 1)
                transposes(OS[r]).then_inc(b_ot, 1)

            def xattn(g, par):
                for gi in range(XG):
                    q0 = g * XG + gi
                    g1, _, _, q1 = after(g, gi, par, 1)
                    g2, gi2, _, q2 = after(g, gi, par, 2)
                    g3, gi3, par3, q3 = after(g, gi, par, 3)
                    s1 = some(g1) and not (isinstance(q1, int) and q1 < 0)
                    s2 = some(g2) and not (isinstance(q2, int) and q2 < 0)
                    ga, para = (g, par) if gi >= 2 else (g - 1, 1 - par)
                    if some(g3):
                        project_k(g3, q3, gi3, par3)
                    if s2:
                        scores_by_query(q2, gi2, 0)
                    if some(g):
                        scores_by_key(q0, gi, 0)
                    if s1:
                        maxima_transposed(q1)
                    if gi == 0 and some(g + 1):
                        if needed(g - 1):
                            pe.wait_ge(b_x2, g - 1)
                        if isinstance(g, int) and g == 1:
                            pe.wait_ge(b_v2, 4)
                        if isinstance(g, int) and g == 0:
                            pe.wait_ge(b_v2, 2)
                        norm_transposed(g + 1 + G)
                    if gi == 1 and some(g - 1):
                        if some(g + 1):
                            pe.wait_ge(b_cs, g + 2)
                        elif needed(g - 1):
                            pe.wait_ge(b_x2, g - 1)
                        token_major_x(g - 1, 0)
                    if gi == 2 and some(g + 1):
                        if some(g - 1):
                            pe.wait_ge(b_norm, (g - 1) * 2 + 1)
                        values_x(g + 1, 1 - par)
                    if gi == 3 and some(g - 1):
                        pe.wait_ge(b_norm, g * 2)
                        transposes(ON).then_inc(b_ontp, 1)
                    if s2:
                        scores_by_query(q2, gi2, 1)
                    if some(g):
                        scores_by_key(q0, gi, 1)
                    if some(g3):
                        project_q(g3, q3, gi3, par3)
                    if some(ga):
                        attend(ga, para, 1 - gi // 2, 2 * (gi % 2))
                    if s2:
                        scores_by_query(q2, gi2, 2)
                    if some(g):
                        scores_by_key(q0, gi, 2)
                    if gi == 0 and some(g + 1):
                        ctx_transposed(g + 1, 1 - par)
                    if gi == 2 and some(g - 1):
                        pe.wait_ge(b_norm, (g - 1) * 2 + 1)
                        if some(g + 1):
                            pe.wait_ge(b_v2, g * 2 + 4)
                        token_major_x(g - 1, 1)
                    if gi == 3 and some(g - 1):
                        pe.wait_ge(b_ont, g)
                        for b in range(TPG):
                            last = pe.matmul(tbank[:, b * P:(b + 1) * P], ONT[:, b, :], WOX[:, :],
                                             start=True, stop=True)
                        last.then_inc(b_proj, 1)
                    if s2:
                        scores_by_query(q2, gi2, 3)
                    if some(g):
                        scores_by_key(q0, gi, 3)
                    if some(ga):
                        attend(ga, para, 1 - gi // 2, 2 * (gi % 2) + 1)

            if phases > 1:
                pe.wait_ge(a_x1, G)
                pe.wait_ge(s_dve, SDVE)
                walk_pipelined(pe, xattn)

            def logits(g, par):
                for t in range(TPG):
                    c = slice(t * P, (t + 1) * P)
                    last = product3(tbank[:, t * E:(t + 1) * E], XTH[par][:, c], XTL[par][:, c],
                                    WR[0][:, :], WR[1][:, :])
                last.then_inc(r_lp, 1)

            def weights_transposed(g):
                pe.wait_ge(r_w, g * 8 + 8)
                transposes(WS.bitcast(F32)).then_inc(r_wp, 1)

            def down(g, par, u):
                if u == 0:
                    if not is_first(g):
                        pe.wait_ge(f_y, g)
                    pe.matmul(bank[6][:, :], BD[0][:, :], WT[par][:, :], start=True, stop=False)
                    pe.matmul(bank[6][:, :], BD[1][:, :], WT[par][:, :], start=False, stop=False)
                if u < NP:
                    pe.wait_ge(f_h, g * NP + u + 1)
                else:
                    pe.wait_ge(f_t, g * NU + NU)
                pe.matmul(bank[6][:, :], WD[:, u, :], hid[(par + u) % 2], start=False,
                          stop=(u == NP)).then_inc(f_d, 1)

            def sum_transposed(g):
                pe.wait_ge(f_y, g + 1)
                transposes(YS.rearrange("p (t c) -> p t c", c=P)).then_inc(f_yt, 1)

            def experts(g, par):
                for u in range(NU):
                    n = g * NU + u
                    k = (par + u) % 2
                    if u == 0:
                        pe.wait_ge(xt_lo_ok, g + 1 + 2 * G)
                    if not (is_first(g) and u < 2):
                        pe.wait_ge(f_t, n - 1)
                    for w, b, full in ((GATE, k, f_g), (UP, 2 + k, f_u)):
                        product3(bank[b][:, :], w[0][:, u, :], w[1][:, u, :], XTH[par][:, :],
                                 XTL[par][:, :]).then_inc(full, 1)
                    if u < NP:
                        if u == 0:
                            pe.wait_ge(r_wt, g + 1)
                        if not (is_first(g) and u < 2):
                            pe.wait_ge(f_h, g * NP + u - 1)
                        pe.matmul(bank[4 + u % 2][:, :], SEL[:, u, :], WT[par][:, :],
                                  start=True, stop=True).then_inc(f_w, 1)
                    if u > 0:
                        down(g, par, u - 1)
                    elif not is_first(g):
                        down(g - 1, 1 - par, NP)
                    if u == 2 and not is_first(g):
                        sum_transposed(g - 1)
                    if not is_last(g):
                        if u == 4:
                            if not is_first(g):
                                pe.wait_ge(f_o, g)
                            norm_transposed(g + 1 + 2 * G)
                        if u == 7:
                            pe.wait_ge(xt_lo_ok, g + 2 + 2 * G)
                            logits(g + 1, 1 - par)
                        if u == 12:
                            weights_transposed(g + 1)

            if phases > 2:
                pe.wait_ge(b_x2, G)
                pe.wait_ge(ld_f, LDF)
                pe.wait_ge(f_zero, 5)
                pe.transpose(tbank[:, 0:64], bias_rows[:, :], ident[0:64, 0:64]).then_inc(f_bt, 1)
                pe.wait_ge(f_prep, FPREP)
                norm_transposed(2 * G)
                pe.wait_ge(xt_lo_ok, 2 * G + 1)
                logits(0, 0)
                weights_transposed(0)
                pe.wait_ge(f_pool, 4)
                walk(pe, experts)
                down(G - 1, 1, NP)
                sum_transposed(G - 1)


_INS = ['x', 'ctx_512', 'L0_attn_w_qkv', 'L0_attn_w_out', 'L0_attn_b_out', 'L0_attn_proj',
        'L0_xattn_Wq', 'L0_xattn_bq', 'L0_xattn_Wk', 'L0_xattn_bk', 'L0_xattn_Wv', 'L0_xattn_bv',
        'L0_xattn_Wo', 'L0_xattn_bo', 'L0_ffn_Wr', 'L0_ffn_br', 'L0_ffn_Wg_s', 'L0_ffn_bg_s',
        'L0_ffn_Wu_s', 'L0_ffn_bu_s', 'L0_ffn_Wd_s', 'L0_ffn_bd_s', 'L0_ffn_Wg', 'L0_ffn_bg',
        'L0_ffn_Wu', 'L0_ffn_bu', 'L0_ffn_Wd', 'L0_ffn_bd']


def kernel(**inputs):
    import numpy as _np
    import concourse.bacc as _bacc
    from concourse import mybir as _mybir
    from concourse.bass_utils import run_bass_kernel_spmd as _run

    nc = _bacc.Bacc("TRN2", target_bir_lowering=False, num_devices=1)
    arrays, args = {}, []
    for name in _INS:
        a = _np.ascontiguousarray(inputs[name])
        arrays[f"in_{name}_dram"] = a
        args.append(nc.dram_tensor(f"in_{name}_dram", a.shape, _mybir.dt.from_np(a.dtype), kind="ExternalInput").ap())
    shape = tuple(inputs["x"].shape)
    args.append(nc.dram_tensor("out_0_dram", shape, _mybir.dt.float32, kind="ExternalOutput").ap())
    decoder_layer(nc, *args)
    r = _run(nc, [arrays], core_ids=[0])
    return r.results[0]["out_0_dram"]
```

```python
from contextlib import ExitStack

import concourse.bass as bass
from concourse import mybir

F32 = mybir.dt.float32
F32R = mybir.dt.float32r
ALU = mybir.AluOpType
ACT = mybir.ActivationFunctionType
AX = mybir.AxisListType

P = 128
D = 128
EPS = 1e-5
TPG = 4
GW = TPG * P

AH = 8
AHD = D // AH
NF = 128
BLK = 32
DEN_EPS = 1e-8

XH = 16
XHD = D // XH
XG = XH // 4
CW = 64

E = 32
TOPK = 8
FI = 64
NP = E // 2
NU = NP + 1


def ds(i, n):
    return bass.ds(i, n)


def decoder_layer(nc, x_in, ctx_in, w_qkv, w_out, b_out, proj, Wq, bq, Wk, bk, Wv, bv, Wo, bo,
                  Wr, br, Wg_s, bg_s, Wu_s, bu_s, Wd_s, bd_s, Wg, bg, Wu, bu, Wd, bd, out):
    NT = x_in.shape[0] * x_in.shape[1] // P
    G = NT // TPG
    assert x_in.shape[1] == P and G % 2 == 0 and G >= 4

    x_tiles = x_in.rearrange("n p d -> p n d")
    ctx_tiles = ctx_in.rearrange("n p d -> p n d")
    out_tiles = out.rearrange("n p d -> p n d")

    with ExitStack() as ctx:
        def sb(name, shape, dt=F32):
            return ctx.enter_context(nc.sbuf_tensor(name, shape, dt))

        def sem(name):
            return ctx.enter_context(nc.semaphore(name))

        bank = [ctx.enter_context(nc.psum_tensor(f"bank{i}", [P, 512], F32)) for i in range(8)]
        tbank = bank[7]

        X = sb("X", [P, NT, D])
        ident = sb("ident", [P, P])
        neg_half = sb("neg_half", [P, TPG])
        eps_b = sb("eps_b", [P, TPG])
        stats = sb("stats", [P, TPG, 6])
        mv = sb("mv", [P, TPG, 2])
        veps = sb("veps", [P, TPG])
        rstd = sb("rstd", [P, TPG])
        xn = sb("xn", [P, TPG, D])
        xb = sb("xb", [P, TPG, D])
        XTH = [sb(f"XTH{i}", [P, GW], F32R) for i in range(2)]
        XTL = [sb(f"XTL{i}", [P, GW], F32R) for i in range(2)]

        raw_flat = sb("raw", [P, 2 * NU * P])
        raw = raw_flat[:, :].rearrange("p (a n c) -> p a n c", a=2, c=P)
        qkv_rows = raw_flat[:, 0:3 * D].rearrange("p (a d) -> p a d", a=3)
        proj_rows = raw_flat[:, 3 * D:3 * D + NF]
        wout_rows = raw_flat[:, 4 * D:5 * D]
        head_of_row = sb("head_of_row", [P, AH])
        CH = sb("CH", [P, 2 * AH, NF], F32R)
        CL = sb("CL", [P, 2 * AH, NF], F32R)
        WVH = sb("WVH", [P, D], F32R)
        WVL = sb("WVL", [P, D], F32R)
        WOT = sb("WOT", [P, D])
        bout_b = sb("bout_b", [P, D])
        blockmask = sb("blockmask", [P, P])
        work = sb("work", [P, 12 * GW])

        def part(n, width=GW):
            return work[:, n * GW:n * GW + width]

        proj_spread = part(0, 2 * GW).rearrange("p (h f) -> p h f", f=NF)
        expf = [part(i) for i in range(4)]
        phiK = [part(4 + i) for i in range(2)]
        phiQ = [part(6 + i) for i in range(2)]
        AM = [part(8 + i).rearrange("p (b s) -> p b s", s=P) for i in range(2)]
        V1 = part(10, 2 * GW).rearrange("p (b h c) -> p b h c", b=TPG, c=32)
        OS = [sb(f"OS{i}", [P, TPG, P]) for i in range(2)]
        den = sb("den", [P, TPG, 8])
        rden = sb("rden", [P, TPG, 8])
        ON = sb("ON", [P, TPG, D])
        ONT = sb("ONT", [P, TPG, P])

        ctxr = [sb(f"ctxr{i}", [P, TPG, 2, CW]) for i in range(2)]
        wqx = sb("wqx", [P, D])
        wkx = sb("wkx", [P, D])
        wvx = sb("wvx", [P, D])
        wx_hi = sb("wx_hi", [P, 2, D], F32R)
        wx_lo = sb("wx_lo", [P, 2, D], F32R)
        WQS = [sb(f"WQS{i}", [P, XG, 4, 4, XHD], F32R) for i in range(2)]
        WKS = [sb(f"WKS{i}", [P, XG, 4, 4, XHD], F32R) for i in range(2)]
        WVX = [sb(f"WVX{i}", [P, D], F32R) for i in range(2)]
        WOX = sb("WOX", [P, D])
        bo_b = sb("bo_b", [P, D])
        wo_rows = sb("wo_rows", [P, D])
        bv_col = sb("bv_col", [P, 1])
        bv_cols = sb("bv_cols", [P, P])
        bqs = sb("bqs", [P, XG])
        bks = sb("bks", [P, XG])
        bqm = sb("bqm", [P, XG])
        bkm = sb("bkm", [P, XG])
        lo_q = sb("lo_q", [P, 1])
        lo_k = sb("lo_k", [P, 1])
        lo_c = sb("lo_c", [P, 1])
        ones_k = sb("ones_k", [P, 1])
        HM = [sb(f"HM{i}", [P, GW], F32R) for i in range(2)]
        HC = sb("HC", [P, GW], F32R)
        CS = [sb(f"CS{i}", [P, GW], F32R) for i in range(2)]
        QS = sb("QS", [P, XG, GW], F32R)
        KS = [sb(f"KS{i}", [P, GW], F32R) for i in range(2)]
        UP = [sb(f"UP{i}", [P, NU, P], F32R) for i in range(2)]
        KB = [t[:, 0:16, :].rearrange("p (b j) k -> p b j k", j=4) for t in (UP[0], UP[1], CH, CL)]
        V2 = [sb(f"V2{i}", [P, TPG * XG, 4, 32]) for i in range(2)]
        PT = [t.rearrange("p (b j q) -> p b j q", b=TPG, q=P)
              for t in (work[:, 0:4 * GW], work[:, 4 * GW:8 * GW], work[:, 8 * GW:12 * GW], raw_flat[:, 0:4 * GW])]
        negm = [sb(f"negm{i}", [P, 4, TPG]) for i in range(2)]
        MM = sb("MM", [P, 2, 4, TPG], F32R)
        MT = [sb(f"MT{i}", [32, P], F32R) for i in range(2)]

        GATE = [sb(f"GATE{i}", [P, NU, P], F32R) for i in range(2)]
        WD = sb("WD", [P, NU, D])
        WDS = [sb(f"WDS{i}", [P, D], F32R) for i in range(2)]
        WDH, WDL = ([t[:, u, :] for u in range(NP)] + [last[:, :]] for t, last in ((CH, WDS[0]), (CL, WDS[1])))
        wr_sb = sb("wr_sb", [P, E])
        WR = [sb(f"WR{i}", [P, E], F32R) for i in range(2)]
        br_b = sb("br_b", [P, E])
        bd_rows = sb("bd_rows", [P, D])
        BD = [sb(f"BD{i}", [P, D], F32R) for i in range(2)]
        bias_rows = sb("bias_rows", [64, P])
        BT = sb("BT", [P, 64])
        SEL = QS[:, :, :].rearrange("p g (u m) -> p (g u) m", m=P)
        lg = sb("lg", [P, TPG, E])
        sig = sb("sig", [P, TPG, E])
        zap = sb("zap", [P, TPG, E])
        wsel = sb("wsel", [P, TPG, E])
        wfull = sb("wfull", [P, TPG, E])
        top8 = sb("top8", [P, TPG, TOPK])
        wsum = sb("wsum", [P, TPG])
        winv = sb("winv", [P, TPG])
        WS = KS[0][:, :].rearrange("p (t c) -> p t c", c=P)
        WT = CS
        silu = [part(i) for i in range(2)]
        upm = [part(2 + i) for i in range(2)]
        hid = [part(4 + i) for i in range(3)]
        HH = [HM[0][:, :], HM[1][:, :], WQS[0][:, :, :, :, :].rearrange("p g j t d -> p (g j t d)")]
        HL = [KS[1][:, :], HC[:, :], WQS[1][:, :, :, :, :].rearrange("p g j t d -> p (g j t d)")]
        YS = part(7)
        OST = [part(8 + i).rearrange("p (b d) -> p b d", d=D) for i in range(2)]

        ld_w = sem("ld_w")
        ld_p = sem("ld_p")
        c_spread = sem("c_spread")
        ld_x0 = sem("ld_x0")
        ld_x = sem("ld_x")
        c_pool = sem("c_pool")
        c_wT = sem("c_wT")
        c_hi = sem("c_hi")
        c_lo = sem("c_lo")
        ln_mv = sem("ln_mv")
        ln_eps = sem("ln_eps")
        ln_rstd = sem("ln_rstd")
        ln_xc = sem("ln_xc")
        ln_xn = sem("ln_xn")
        xt_full = sem("xt_full")
        xt_hi_ok = sem("xt_hi_ok")
        xt_lo_ok = sem("xt_lo_ok")
        a_feat = sem("a_feat")
        a_exp = sem("a_exp")
        a_mink = sem("a_mink")
        a_neg = sem("a_neg")
        a_phi = sem("a_phi")
        a_score = sem("a_score")
        a_mask = sem("a_mask")
        a_o = sem("a_o")
        a_os = sem("a_os")
        a_vp = sem("a_vp")
        a_v1 = sem("a_v1")
        a_ot = sem("a_ot")
        a_den = sem("a_den")
        a_rden = sem("a_rden")
        a_norm = sem("a_norm")
        a_ontp = sem("a_ontp")
        a_ont = sem("a_ont")
        a_proj = sem("a_proj")
        a_xb = sem("a_xb")
        a_x1 = sem("a_x1")
        ld_c = [sem(f"ld_c{i}") for i in range(2)]
        ld_b = sem("ld_b")
        s_pool = sem("s_pool")
        s_kinds = sem("s_kinds")
        s_stack = sem("s_stack")
        b_ctx = sem("b_ctx")
        b_cm = sem("b_cm")
        b_cs = sem("b_cs")
        b_pp = sem("b_pp")
        b_hm = sem("b_hm")
        b_split = sem("b_split")
        b_vp = sem("b_vp")
        b_v2 = sem("b_v2")
        b_kb = [sem(f"b_kb{i}") for i in range(2)]
        b_s = sem("b_s")
        b_max = sem("b_max")
        b_mm = sem("b_mm")
        b_mtp = sem("b_mtp")
        b_mt = sem("b_mt")
        b_mq = sem("b_mq")
        b_st = sem("b_st")
        b_exp = sem("b_exp")
        b_pv = sem("b_pv")
        b_os = sem("b_os")
        b_ot = sem("b_ot")
        b_rden = sem("b_rden")
        b_norm = sem("b_norm")
        b_ontp = sem("b_ontp")
        b_ont = sem("b_ont")
        b_proj = sem("b_proj")
        b_xb = sem("b_xb")
        b_x2 = sem("b_x2")
        ld_f = sem("ld_f")
        ld_raw = sem("ld_raw")
        s_zero = sem("s_zero")
        f_pool = sem("f_pool")
        f_zero = sem("f_zero")
        f_prep = sem("f_prep")
        f_sel = sem("f_sel")
        s_bv = sem("s_bv")
        f_bt = sem("f_bt")
        f_g = sem("f_g")
        f_u = sem("f_u")
        f_w = sem("f_w")
        f_s = sem("f_s")
        f_t = sem("f_t")
        f_h = sem("f_h")
        f_hh = sem("f_hh")
        f_hl = sem("f_hl")
        f_wd = [sem(f"f_wd{i}") for i in range(2)]
        f_d = sem("f_d")
        f_y = sem("f_y")
        f_yt = sem("f_yt")
        f_o = sem("f_o")
        st_y = [sem(f"st_y{i}") for i in range(2)]
        r_lp = sem("r_lp")
        r_lg = sem("r_lg")
        r_sig = sem("r_sig")
        r_zap = sem("r_zap")
        r_w = sem("r_w")
        r_wp = sem("r_wp")
        r_wt = sem("r_wt")

        FPREP = 6
        LDF = 16 * 11
        SPOOL = 14
        SSTACK = 21
        LDB = 16 * (4 + 4 + XH + 24)

        FOLDS = (2, 0, 3, 1)

        block = ctx.enter_context(nc.Block())

        def walk(eng, body):
            body(0, 0)
            body(1, 1)
            with eng.Fori(1, G // 2 - 1) as i:
                body(i * 2, 0)
                body(i * 2 + 1, 1)
            body(G - 2, 0)
            body(G - 1, 1)

        def some(g):
            return not isinstance(g, int) or 0 <= g < G

        def later(g):
            return not isinstance(g, int) or 0 < g <= G

        def steps(step):
            def body(g, par):
                for gi in range(XG):
                    step(g, gi, par)
            return body

        def needed(count):
            return not isinstance(count, int) or count > 0

        def after(g, gi, par, k):
            over = (gi + k) // XG
            return g + over, (gi + k) % XG, (par + over) % 2, g * XG + gi + k

        def head_copy(gi, j):
            rows = slice(32 * j, 32 * j + 32)
            return KB[gi][rows, :, j, :], KS[gi % 2][rows, :].bitcast(F32).rearrange("p (b k) -> p b k", k=P)

        def slot_user(g, u):
            return g * NU + u - 2 if u >= 3 else (g - 1) * NU + (16, 17, 15)[u]

        def is_first(g):
            return isinstance(g, int) and g == 0

        def is_last(g):
            return isinstance(g, int) and g == G - 1

        @block.sync
        def _(sp):
            sp.dma_start(X[:, 0:TPG, :], x_tiles[:, 0:TPG, :]).then_inc(ld_x0, 16)
            sp.dma_start(proj_rows, proj.rearrange("h r f -> (h r) f")).then_inc(ld_p, 16)
            sp.dma_start(qkv_rows, w_qkv.rearrange("(a p) d -> p a d", a=3)).then_inc(ld_w, 16)
            sp.dma_start(wout_rows[:, :], w_out).then_inc(ld_w, 16)
            sp.dma_start(bout_b[:, :], b_out.partition_broadcast(P)).then_inc(ld_w, 16)
            sp.dma_start(X[:, TPG:NT, :], x_tiles[:, TPG:NT, :]).then_inc(ld_x, 16)
            for i in range(2):
                rows = slice(i * CW, (i + 1) * CW)
                sp.dma_start(wkx[rows, :], Wk).then_inc(ld_b, 16)
                sp.dma_start(wvx[rows, :], Wv).then_inc(ld_b, 16)
            sp.dma_start(wqx[:, :], Wq).then_inc(ld_b, 16)
            sp.dma_start(bo_b[:, :], bo.partition_broadcast(P)).then_inc(ld_b, 16)
            sp.dma_start(wo_rows[:, :], Wo).then_inc(ld_b, 16)
            sp.dma_start(bv_col[:, :], bv.rearrange("(d a) -> d a", a=1)).then_inc(ld_b, 16)
            for h in range(XH):
                gi, j = h // 4, h % 4
                row = (gi // 2) * 64 + j * 16 + (gi % 2) * 8
                sp.dma_start(WOX[row:row + XHD, :], Wo[h * XHD:(h + 1) * XHD, :]).then_inc(ld_b, 16)
            sp.wait_ge(s_pool, 2)
            for j in range(4):
                for t in range(3):
                    row = 32 * j + 8 * t
                    for dst, src in ((bqs, bq), (bks, bk)):
                        v = src.rearrange("(g j d) -> j d g", j=4, d=XHD)
                        sp.dma_start(dst[row:row + XHD, :], v[j], allow_slow_non_contiguous=True).then_inc(ld_b, 16)

            sp.wait_ge(f_zero, 3)
            sp.dma_start(WD[:, 0:NP, :], Wd.rearrange("(n e) i d -> (e i) n d", e=2)).then_inc(ld_f, 16)
            sp.dma_start(WD[0:FI, NP, :], Wd_s).then_inc(ld_f, 16)
            sp.dma_start(wr_sb[:, :], Wr).then_inc(ld_f, 16)
            sp.dma_start(br_b[:, :], br.partition_broadcast(P)).then_inc(ld_f, 16)
            for i in range(2):
                sp.dma_start(bd_rows[i * E:(i + 1) * E, :], bd).then_inc(ld_f, 16)
            for row, pairs, shared in ((0, bg, bg_s), (32, bu, bu_s)):
                sp.dma_start(bias_rows[row:row + NP, :],
                             pairs.rearrange("(n e) i -> n (e i)", e=2)).then_inc(ld_f, 16)
                sp.dma_start(bias_rows[row + NP:row + NP + 1, 0:FI],
                             shared.rearrange("(a n) -> a n", a=1)).then_inc(ld_f, 16)
            sp.dma_start(bias_rows[49:50, :], bd_s.rearrange("(a n) -> a n", a=1)).then_inc(ld_f, 16)
            sp.wait_ge(c_wT, 5)
            for i, (pairs, shared) in enumerate(((Wg, Wg_s), (Wu, Wu_s))):
                sp.dma_start(raw[:, i, 0:NP, :].rearrange("p n (e c) -> p (n e) c", e=2),
                             pairs.rearrange("e d c -> d e c")).then_inc(ld_raw, 16)
                sp.dma_start(raw[:, i, NP, 0:FI], shared).then_inc(ld_raw, 16)

            def load_ctx(g, par):
                for i in range(2):
                    sp.dma_start(ctxr[par][:, :, i, :], ctx_tiles[:, ds(g * TPG, TPG), :]).then_inc(ld_c[par], 16)

            load_ctx(0, 0)

            def xattn(g, par):
                for gi in range(XG):
                    g1, _, _, q1 = after(g, gi, par, 1)
                    if gi == 1 and some(g + 2):
                        if needed(g + 1):
                            sp.wait_ge(b_ctx, g + 1)
                        load_ctx(g + 2, par)
                    if some(g1):
                        if not (isinstance(q1, int) and q1 < 0):
                            sp.wait_ge(b_mt, q1 + 1)
                            for i in range(2):
                                sp.dma_start(QS[24 + i:P:32, (gi + 1) % XG, :].bitcast(F32),
                                             MT[(gi + 1) % 2][16 * i:16 * i + 16, :].bitcast(F32)).then_inc(b_mq, 16)

            xattn(-1, 1)
            walk(sp, xattn)

            def store(g, par):
                sp.wait_ge(f_o, g + 1)
                sp.dma_start(out_tiles[:, ds(g * TPG, TPG), :], OST[par]).then_inc(st_y[par], 16)

            walk(sp, store)
            for i in range(2):
                sp.wait_ge(st_y[i], G * 8)

        @block.gpsimd
        def _(pool):
            pool.memset(ident[:, :], 0.0).then_inc(c_pool, 1)
            pool.wait_ge(c_pool, 1)
            pool.affine_select(out=ident[:, :], in_=ident[:, :], compare_op=ALU.not_equal, fill=1.0,
                               base=0, pattern=[[-1, P]], channel_multiplier=1).then_inc(c_pool, 1)
            pool.memset(neg_half[:, :], -0.5).then_inc(c_pool, 1)
            pool.memset(eps_b[:, :], EPS).then_inc(c_pool, 1)
            pool.memset(blockmask[:, :], 0.0).then_inc(c_pool, 1)
            for j in range(P // BLK):
                pool.wait_ge(c_pool, 5 + j)
                pool.memset(blockmask[j * BLK:(j + 1) * BLK, j * BLK:(j + 1) * BLK], 1.0).then_inc(c_pool, 1)
            pool.wait_ge(c_pool, 9)
            pool.memset(V1[:, :, :, :], 0.0).then_inc(c_pool, 1)
            pool.wait_ge(c_pool, 10)
            pool.memset(V1[:, :, :, AHD:AHD + 1], 1.0).then_inc(c_pool, 1)

            def layer_norm(n, g):
                pool.wait_ge(ln_mv, n * TPG + TPG)
                pool.tensor_tensor(xn[:, :, :], X[:, ds(g * TPG, TPG), :],
                                   mv[:, :, 0].unsqueeze(2).to_broadcast([P, TPG, D]),
                                   ALU.subtract).then_inc(ln_xc, 1)
                pool.tensor_tensor(veps[:, :], mv[:, :, 1], eps_b[:, :], ALU.add).then_inc(ln_eps, 1)
                pool.wait_ge(ln_eps, n + 1)
                pool.tensor_tensor(rstd[:, :], veps[:, :], neg_half[:, :], ALU.pow).then_inc(ln_rstd, 1)
                pool.wait_ge(ln_xc, n + 1)
                pool.wait_ge(ln_rstd, n + 1)
                pool.tensor_tensor(xn[:, :, :], xn[:, :, :], rstd[:, :].unsqueeze(2).to_broadcast([P, TPG, D]),
                                   ALU.mult).then_inc(ln_xn, 1)

            layer_norm(0, 0)

            def attn(g, par):
                for h in range(AH):
                    if h == 1:
                        layer_norm(g + 1, 0 if is_last(g) else g + 1)
                    if h == 2 and not is_first(g):
                        residual_bias(g - 1)
                    if h == 3 and is_first(g):
                        stack_weights()
                    if h == 3 and isinstance(g, int) and g == 1:
                        split_experts(0, GATE)

            def residual_bias(g):
                if not is_first(g):
                    pool.wait_ge(a_x1, g)
                pool.tensor_tensor(xb[:, :, :], X[:, ds(g * TPG, TPG), :],
                                   bout_b[:, :].unsqueeze(1).to_broadcast([P, TPG, D]),
                                   ALU.add).then_inc(a_xb, 1)

            pool.wait_ge(ld_w, 3 * 16)
            pool.wait_ge(ld_x, 16)
            pool.memset(bqs[:, :], 0.0).then_inc(s_pool, 1)
            pool.memset(bks[:, :], 0.0).then_inc(s_pool, 1)
            pool.memset(lo_c[:, :], 0.0).then_inc(s_pool, 1)
            pool.wait_ge(s_pool, 3)
            pool.memset(lo_c[CW:P, :], 1.0).then_inc(s_pool, 1)
            pool.wait_ge(s_pool, 4)
            for i in range(2):
                pool.memset(V2[i][:, :, :, :], 0.0).then_inc(s_pool, 1)
                pool.wait_ge(s_pool, 5 + 3 * i)
                for half in range(2):
                    pool.memset(V2[i][:, half::2, :, 16 * half + XHD:16 * half + XHD + 1], 1.0).then_inc(s_pool, 1)
            for i in range(2):
                pool.memset(WQS[i][:, :, :, 3, :].bitcast(F32), 0.0).then_inc(s_pool, 1)
                pool.memset(WKS[i][:, :, :, 3, :].bitcast(F32), 0.0).then_inc(s_pool, 1)
            pool.wait_ge(s_pool, SPOOL)
            pool.memset(bd_rows[:, :], 0.0).then_inc(f_zero, 1)
            pool.memset(bias_rows[:, :], 0.0).then_inc(f_zero, 1)
            pool.wait_ge(f_zero, 2)
            pool.memset(WD[FI:P, NP, :], 0.0).then_inc(f_zero, 1)
            pool.wait_ge(f_zero, 3)
            pool.wait_ge(c_wT, 5)
            pool.memset(raw[:, :, NP, FI:P], 0.0).then_inc(f_zero, 1)
            pool.wait_ge(f_zero, 4)

            def stack_weights():
                cnt = [0]

                def done(ins):
                    cnt[0] += 1
                    ins.then_inc(s_stack, 1)

                pool.wait_ge(ld_b, LDB)
                pool.wait_ge(s_pool, SPOOL)
                pool.wait_ge(s_kinds, 3)
                for i, w in enumerate((wqx, wkx)):
                    done(pool.tensor_copy(wx_hi[:, i, :], w[:, :]))
                done(pool.tensor_copy(WVX[0][:, :], wvx[:, :]))
                pool.wait_ge(s_stack, 3)
                for i, w in enumerate((wqx, wkx)):
                    done(pool.tensor_tensor(wx_lo[:, i, :], w[:, :], wx_hi[:, i, :].bitcast(F32), ALU.subtract))
                done(pool.tensor_tensor(WVX[1][:, :], wvx[:, :], WVX[0][:, :].bitcast(F32), ALU.subtract))
                pool.wait_ge(s_stack, 6)
                for part, w in enumerate((wx_hi, wx_lo)):
                    for i, stacked in enumerate((WQS, WKS)):
                        v = w[:, i, :].bitcast(F32).rearrange("p (g j d) -> p (g j) d", g=XG, j=4)
                        for t in range(3):
                            done(pool.tensor_copy(
                                stacked[part][:, :, :, t, :].rearrange("p g j d -> p (g j) d"), v))
                done(pool.tensor_scalar(bks[:, :], bks[:, :], ones_k[:, 0:1], None, ALU.add))
                pool.wait_ge(s_stack, 19)
                done(pool.tensor_scalar(bqm[:, :], bqs[:, :], lo_q[:, 0:1], None, ALU.mult))
                done(pool.tensor_scalar(bkm[:, :], bks[:, :], lo_k[:, 0:1], None, ALU.mult))
                assert cnt[0] == SSTACK

            def split_experts(i, dst):
                pool.wait_ge(ld_raw, 4 * 16)
                pool.wait_ge(f_zero, 4)
                pool.tensor_copy(dst[0][:, :, :], raw[:, i]).then_inc(f_pool, 1)
                pool.wait_ge(f_pool, 2 * i + 1)
                pool.tensor_tensor(dst[1][:, :, :], raw[:, i], dst[0][:, :, :].bitcast(F32),
                                   ALU.subtract).then_inc(f_pool, 1)

            for i in range(2):
                pool.memset(KB[i].bitcast(F32), 0.0).then_inc(s_zero, 1)

            walk(pool, attn)
            residual_bias(G - 1)

            def residual_bias_x(g):
                if is_first(g):
                    pool.wait_ge(a_x1, G)
                else:
                    pool.wait_ge(b_x2, g)
                pool.tensor_tensor(xb[:, :, :], X[:, ds(g * TPG, TPG), :],
                                   bo_b[:, :].unsqueeze(1).to_broadcast([P, TPG, D]),
                                   ALU.add).then_inc(b_xb, 1)

            def xattn(g, par):
                if some(g - 1):
                    residual_bias_x(g - 1)
                if later(g + 2):
                    layer_norm(g + 2 + G, 0 if isinstance(g, int) and g == G - 2 else g + 2)
                if is_last(g):
                    pool.wait_ge(b_st, 16 * g + 8)
                    split_experts(1, UP)
                    pool.wait_ge(b_kb[0], 8 * G)
                    pool.wait_ge(b_kb[1], 8 * G)
                    pool.memset(WS[:, :, 2 * E:P].bitcast(F32), 0.0).then_inc(f_zero, 1)

            pool.wait_ge(ld_b, LDB)
            pool.wait_ge(f_prep, FPREP)
            pool.wait_ge(a_score, G * AH)
            for i in range(2, 4):
                pool.memset(KB[i].bitcast(F32), 0.0).then_inc(s_zero, 1)
            xattn(-1, 1)
            walk(pool, xattn)
            xattn(G, 0)
            def hid_lo(g, u):
                pool.wait_ge(f_hh, g * NU + u + 1)
                if needed(slot_user(g, u)):
                    pool.wait_ge(f_d, slot_user(g, u))
                pool.tensor_tensor(HL[u % 3], hid[u % 3], HH[u % 3].bitcast(F32), ALU.subtract).then_inc(f_hl, 1)

            def experts(g, par):
                for u in range(NU):
                    hid_lo(g, u)
                    if u == 1 and not is_last(g):
                        layer_norm(g + 1 + 2 * G, g + 1)

            for hi, lo, raw_w in ((CH, CL, WD[:, 0:NP, :]), (WDS[0], WDS[1], WD[:, NP, :])):
                pool.wait_ge(f_wd[0], 2)
                src = hi[:, :, :] if hi is CH else hi[:, :]
                dst = lo[:, :, :] if hi is CH else lo[:, :]
                pool.tensor_tensor(dst, raw_w, src.bitcast(F32), ALU.subtract).then_inc(f_wd[1], 1)
            walk(pool, experts)

        @block.scalar
        def _(act):
            def xt_hi(n, par):
                act.wait_ge(xt_full, n + 1)
                act.activation(XTH[par][:, :], tbank[:, :], ACT.Copy).then_inc(xt_hi_ok, 1)

            act.wait_ge(c_wT, 1)
            act.activation(WVH[:, :], bank[6][:, 0:D], ACT.Copy).then_inc(c_hi, 1)
            act.activation(WOT[:, :], bank[6][:, D:2 * D], ACT.Copy).then_inc(c_hi, 1)
            for i, q in enumerate(FOLDS):
                if i == 2:
                    xt_hi(0, 0)
                act.wait_ge(c_wT, i + 2)
                act.activation(CH[:, 4 * q:4 * q + 4, :], bank[i][:, :].rearrange("p (h f) -> p h f", f=NF),
                               ACT.Copy).then_inc(c_hi, 1)

            def drain_outputs(g):
                act.wait_ge(a_o, g * AH + AH)
                for r in range(2):
                    act.activation(OS[r][:, :, :], bank[5 + r][:, :].rearrange("p (b s) -> p b s", s=P),
                                   ACT.Copy).then_inc(a_os, 1)

            def ont_copy(g):
                act.wait_ge(a_ontp, g + 1)
                act.activation(ONT[:, :, :], tbank[:, :].rearrange("p (b s) -> p b s", s=P),
                               ACT.Copy).then_inc(a_ont, 1)

            def attn(g, par):
                for h in range(AH):
                    if h == 2:
                        if not is_first(g):
                            drain_outputs(g - 1)
                        act.wait_ge(a_vp, g + 1)
                        act.activation(V1[:, :, :, 0:AHD],
                                       tbank[:, :].rearrange("p (b h d) -> p b h d", b=TPG, d=AHD),
                                       ACT.Copy).then_inc(a_v1, 1)
                    if h == 5 and not is_first(g):
                        ont_copy(g - 1)
                    if h == 6:
                        xt_hi(g + 1, 1 - par)
                    for f in range(2):
                        n = 2 * h + f
                        act.wait_ge(a_feat, g * 16 + n + 1)
                        if f == 0:
                            act.activation(expf[n % 4], bank[n % 4][:, :], ACT.Exp).then_inc(a_exp, 1)
                        else:
                            act.activation(expf[n % 4], bank[n % 4][:, :], ACT.Relu, scale=-1.0).then_inc(a_neg, 1)
                            act.wait_ge(a_neg, g * AH + h + 1)
                            act.activation(expf[n % 4], expf[n % 4], ACT.Exp, scale=-1.0).then_inc(a_exp, 1)

            act.wait_ge(c_pool, 11)
            walk(act, attn)

            def ctx_hi(g):
                act.wait_ge(b_ctx, g + 1)
                if needed(g):
                    act.wait_ge(b_cs, g)
                act.activation(HC[:, :], tbank[:, :], ACT.Copy, scale=lo_c[:, 0:1]).then_inc(b_cm, 1)

            def drain_outputs_x(g, r):
                act.wait_ge(b_pv, g * 8 + r * 4 + 4)
                if needed(g * 2 + r - 1):
                    act.wait_ge(b_ot, g * 2 + r - 1)
                act.activation(OS[r][:, :, :], bank[4][:, :].rearrange("p (b s) -> p b s", s=P),
                               ACT.Copy).then_inc(b_os, 1)

            def ont_copy_x(g):
                act.wait_ge(b_ontp, g + 1)
                act.activation(ONT[:, :, :], tbank[:, :].rearrange("p (b s) -> p b s", s=P),
                               ACT.Copy).then_inc(b_ont, 1)

            def values_copy(g, par):
                act.wait_ge(b_vp, g + 1)
                if needed(g - 1):
                    act.wait_ge(b_pv, (g - 1) * 8)
                for half in range(2):
                    act.activation(V2[par][:, half::2, :, 16 * half:16 * half + XHD],
                                   tbank[:, :].rearrange("p (c j d) -> p c j d", j=4, d=XHD)[:, half::2],
                                   ACT.Copy).then_inc(b_v2, 1)

            def hi_part(f, q, gi):
                lo, bias = ((lo_k, bkm), (lo_q, bqm))[f]
                act.wait_ge(b_pp, q * 2 + f + 1)
                if needed(q * 2 + f - 1):
                    act.wait_ge(b_split, q * 2 + f - 1)
                act.activation(HM[f][:, :], bank[f][:, :], ACT.Identity, scale=lo[:, 0:1],
                               bias=bias[:, gi:gi + 1]).then_inc(b_hm, 1)

            def exp_scores(q, gi, b):
                act.wait_ge(b_st, q * 4 + b + 1)
                act.activation(PT[gi][:, b, :, :], bank[5 + b % 2][:, :].rearrange("p (j q) -> p j q", q=P),
                               ACT.Exp, scale=float(XHD) ** -0.5).then_inc(b_exp, 1)

            def step(g, gi, par):
                g1, _, _, q1 = after(g, gi, par, 1)
                g3, gi3, _, q3 = after(g, gi, par, 3)
                q0 = g * XG + gi
                if gi == 0 and some(g - 1):
                    drain_outputs_x(g - 1, 0)
                if gi == 2 and some(g - 1):
                    drain_outputs_x(g - 1, 1)
                if some(g3):
                    hi_part(0, q3, gi3)
                if some(g):
                    exp_scores(q0, gi, 0)
                if some(g1) and not (isinstance(q1, int) and q1 < 0):
                    act.wait_ge(b_mtp, q1 + 1)
                    if needed(q1 - 1):
                        act.wait_ge(b_mq, (q1 - 1) * 32)
                    act.activation(MT[(gi + 1) % 2][:, :], bank[1][0:32, 0:P], ACT.Copy).then_inc(b_mt, 1)
                if gi == 0 and some(g + 1):
                    ctx_hi(g + 1)
                if gi == 3 and some(g - 1):
                    ont_copy_x(g - 1)
                if some(g):
                    exp_scores(q0, gi, 1)
                if gi == 2 and some(g + 1):
                    values_copy(g + 1, 1 - par)
                if some(g3):
                    if needed(q3 * 4 - 12):
                        act.wait_ge(b_st, q3 * 4 - 12)
                    else:
                        act.wait_ge(s_zero, gi3 + 1)
                    act.wait_ge(b_split, q3 * 2 + 1)
                    to, frm = head_copy(gi3, 0)
                    act.activation(to, frm, ACT.Copy).then_inc(b_kb[0], 1)
                    hi_part(1, q3, gi3)
                if some(g):
                    exp_scores(q0, gi, 2)
                if some(g3):
                    to, frm = head_copy(gi3, 1)
                    act.activation(to, frm, ACT.Copy).then_inc(b_kb[0], 1)
                if gi == 0 and later(g + 1):
                    xt_hi(g + 1 + G, 1 - par)
                if some(g):
                    exp_scores(q0, gi, 3)

            act.wait_ge(s_stack, SSTACK)
            act.wait_ge(s_pool, SPOOL)
            act.wait_ge(f_pool, 2)
            ctx_hi(0)
            drain_outputs(G - 1)
            step(-1, 1, 1)
            step(-1, 2, 1)
            ont_copy(G - 1)
            step(-1, 3, 1)
            walk(act, steps(step))

            def sigmoids(g):
                act.wait_ge(r_lg, g + 1)
                act.activation(sig[:, :, :], lg[:, :, :], ACT.Sigmoid).then_inc(r_sig, 1)

            def weights_copy(g, par):
                act.wait_ge(r_wp, g + 1)
                act.activation(WT[par][:, :], tbank[:, :], ACT.Copy).then_inc(r_wt, 1)

            def hid_hi(g, u):
                if u < NP:
                    act.wait_ge(f_h, g * NP + u + 1)
                else:
                    act.wait_ge(f_t, g * NU + NU)
                if needed(slot_user(g, u)):
                    act.wait_ge(f_d, slot_user(g, u))
                act.activation(HH[u % 3], hid[u % 3], ACT.Copy).then_inc(f_hh, 1)

            def drain_sum(g):
                act.wait_ge(f_d, g * NU + NU)
                act.activation(YS, bank[6][:, :], ACT.Identity, bias=BT[:, 49:50]).then_inc(f_y, 1)

            def experts(g, par):
                for u in range(NU):
                    act.wait_ge(f_g, g * NU + u + 1)
                    act.activation(silu[(par + u) % 2], bank[(par + u) % 2][:, :], ACT.Silu,
                                   bias=BT[:, u:u + 1]).then_inc(f_s, 1)
                    if u > 0:
                        hid_hi(g, u - 1)
                    elif not is_first(g):
                        hid_hi(g - 1, NP)
                    if u == 2 and not is_first(g):
                        drain_sum(g - 1)
                    if u == 1 and is_first(g):
                        ont_copy_x(G - 1)
                    if not is_last(g):
                        if u == 6:
                            xt_hi(g + 1 + 2 * G, 1 - par)
                        if u == 9:
                            sigmoids(g + 1)
                        if u == 16:
                            weights_copy(g + 1, 1 - par)

            step(G, 0, 0)
            act.wait_ge(f_prep, FPREP)
            sigmoids(0)
            act.wait_ge(ld_f, LDF)
            act.wait_ge(f_zero, 3)
            act.wait_ge(b_st, G * 16)
            act.activation(CH[:, :, :], WD[:, 0:NP, :], ACT.Copy).then_inc(f_wd[0], 1)
            act.activation(WDS[0][:, :], WD[:, NP, :], ACT.Copy).then_inc(f_wd[0], 1)
            step(G, 1, 0)
            step(G, 2, 0)
            weights_copy(0, 0)
            walk(act, experts)
            hid_hi(G - 1, NP)
            drain_sum(G - 1)

        @block.vector
        def _(dve):
            def ln_moments(n, g):
                for t in range(TPG):
                    dve.bn_stats(stats[:, t, :], X[:, ds(g * TPG + t, 1), :])
                dve.drain()
                for t in range(TPG):
                    dve.bn_aggr(mv[:, t, :], stats[:, t, :]).then_inc(ln_mv, 1)

            def xt_lo(n, par):
                dve.wait_ge(xt_hi_ok, n + 1)
                dve.tensor_tensor(XTL[par][:, :], tbank[:, :], XTH[par][:, :].bitcast(F32),
                                  ALU.subtract).then_inc(xt_lo_ok, 1)

            dve.wait_ge(ld_x0, 16)
            ln_moments(0, 0)
            dve.wait_ge(c_pool, 2)
            dve.tensor_reduce(head_of_row[:, :], ident[:, :].rearrange("p (h r) -> p h r", r=AHD),
                              AX.X, ALU.add).then_inc(c_spread, 1)
            dve.wait_ge(ld_p, 16)
            dve.wait_ge(c_spread, 1)
            dve.tensor_tensor(proj_spread, proj_rows.unsqueeze(1).to_broadcast([P, AH, NF]),
                              head_of_row[:, :].unsqueeze(2).to_broadcast([P, AH, NF]),
                              ALU.mult).then_inc(c_spread, 1)
            kinds = ident[:, :].rearrange("p (j t d) -> p t j d", j=4, d=XHD)
            dve.tensor_reduce(lo_k[:, :], kinds[:, 1], AX.XY, ALU.add).then_inc(s_kinds, 1)
            dve.tensor_reduce(lo_q[:, :], kinds[:, 2], AX.XY, ALU.add).then_inc(s_kinds, 1)
            dve.tensor_reduce(ones_k[:, :], kinds[:, 3, :, 0:2], AX.XY, ALU.add).then_inc(s_kinds, 1)
            dve.wait_ge(c_hi, 2)
            dve.tensor_tensor(WVL[:, :], bank[6][:, 0:D], WVH[:, :].bitcast(F32), ALU.subtract).then_inc(c_lo, 1)
            for i, q in enumerate(FOLDS):
                if i == 2:
                    xt_lo(0, 0)
                dve.wait_ge(c_hi, i + 3)
                dve.tensor_tensor(CL[:, 4 * q:4 * q + 4, :],
                                  bank[i][:, :].rearrange("p (h f) -> p h f", f=NF),
                                  CH[:, 4 * q:4 * q + 4, :].bitcast(F32), ALU.subtract).then_inc(c_lo, 1)

            def mask_scores(gh, par):
                dve.wait_ge(a_score, gh)
                dve.tensor_tensor(AM[par][:, :, :], bank[4][:, :].rearrange("p (b s) -> p b s", s=P),
                                  blockmask[:, :].unsqueeze(1).to_broadcast([P, TPG, P]),
                                  ALU.mult).then_inc(a_mask, 1)

            def normalise(g, r):
                ot = tbank[:, :].rearrange("p (b j c) -> p b j c", b=TPG, c=32)
                dve.wait_ge(a_ot, g * 2 + r + 1)
                dve.tensor_scalar(den[:, :, 0:4], ot[:, :, :, AHD], DEN_EPS, None, ALU.add).then_inc(a_den, 1)
                dve.wait_ge(a_den, g * 2 + r + 1)
                dve.reciprocal(rden[:, :, 0:4], den[:, :, 0:4]).then_inc(a_rden, 1)
                dve.wait_ge(a_rden, g * 2 + r + 1)
                dve.tensor_tensor(ON[:, :, r * 64:r * 64 + 64].rearrange("p b (j c) -> p b j c", c=AHD),
                                  ot[:, :, :, 0:AHD],
                                  rden[:, :, 0:4].unsqueeze(3).to_broadcast([P, TPG, 4, AHD]),
                                  ALU.mult).then_inc(a_norm, 1)

            def residual(g):
                dve.wait_ge(a_proj, g + 1)
                dve.wait_ge(a_xb, g + 1)
                dve.tensor_tensor(X[:, ds(g * TPG, TPG), :], tbank[:, :].rearrange("p (b d) -> p b d", d=D),
                                  xb[:, :, :], ALU.add).then_inc(a_x1, 1)

            def attn(g, par):
                for h in range(AH):
                    gh = g * AH + h
                    dve.wait_ge(a_exp, gh * 2 + 1)
                    ek = expf[(2 * h) % 4]
                    eq = expf[(2 * h + 1) % 4]
                    dve.tensor_scalar(ek[:, :], ek[:, :], 1.0, None, ALU.min).then_inc(a_mink, 1)
                    dve.wait_ge(a_mink, gh + 1)
                    dve.scalar_tensor_tensor(out=phiK[h % 2][:, :], in0=bank[(2 * h) % 4][:, :], scalar=1.0,
                                             in1=ek[:, :], op0=ALU.add, op1=ALU.max).then_inc(a_phi, 1)
                    if not (is_first(g) and h == 0):
                        mask_scores(gh, (h + 1) % 2)
                    dve.wait_ge(a_exp, gh * 2 + 2)
                    dve.scalar_tensor_tensor(out=phiQ[h % 2][:, :], in0=bank[(2 * h + 1) % 4][:, :], scalar=0.0,
                                             in1=eq[:, :], op0=ALU.max, op1=ALU.add).then_inc(a_phi, 1)
                    if h == 2 and not is_first(g):
                        normalise(g - 1, 0)
                    if h == 3 and not is_first(g):
                        normalise(g - 1, 1)
                    if h == 1:
                        ln_moments(g + 1, 0 if is_last(g) else g + 1)
                    if h == 6:
                        xt_lo(g + 1, 1 - par)
                    if h == 6 and is_first(g):
                        dve.wait_ge(ld_b, LDB)
                        dve.tensor_copy(bv_cols[:, :], bv_col[:, 0:1].to_broadcast([P, P])).then_inc(s_bv, 1)
                    if h == 7 and is_first(g):
                        small_weights()
                    if h == 7 and not is_first(g):
                        residual(g - 1)

            def small_weights():
                dve.wait_ge(ld_f, LDF)
                dve.tensor_copy(WR[0][:, :], wr_sb[:, :]).then_inc(f_prep, 1)
                dve.tensor_copy(BD[0][:, :], bd_rows[:, :]).then_inc(f_prep, 1)
                dve.wait_ge(f_prep, 2)
                dve.tensor_tensor(WR[1][:, :], wr_sb[:, :], WR[0][:, :].bitcast(F32), ALU.subtract).then_inc(f_prep, 1)
                dve.tensor_tensor(BD[1][:, :], bd_rows[:, :], BD[0][:, :].bitcast(F32), ALU.subtract).then_inc(f_prep, 1)
                dve.wait_ge(f_bt, 1)
                dve.tensor_copy(BT[:, :], tbank[:, 0:64]).then_inc(f_prep, 1)
                dve.tensor_tensor(bo_b[:, :], bo_b[:, :], tbank[:, P:2 * P], ALU.add).then_inc(f_prep, 1)

            dve.wait_ge(ld_x, 16)
            dve.wait_ge(c_pool, 9)
            walk(dve, attn)
            mask_scores(G * AH, 1)

            def ctx_lo(g, par):
                dve.wait_ge(b_cm, g + 1)
                dve.tensor_tensor(CS[par][:, :], tbank[:, :], HC[:, :].bitcast(F32), ALU.subtract).then_inc(b_cs, 1)

            def normalise_x(g, r):
                ot = tbank[:, :].rearrange("p (b c w) -> p b c w", b=TPG, w=16)
                dve.wait_ge(b_ot, g * 2 + r + 1)
                dve.reciprocal(rden[:, :, :], ot[:, :, :, XHD]).then_inc(b_rden, 1)
                dve.wait_ge(b_rden, g * 2 + r + 1)
                dve.tensor_tensor(ON[:, :, r * 64:r * 64 + 64].rearrange("p b (c d) -> p b c d", d=XHD),
                                  ot[:, :, :, 0:XHD],
                                  rden[:, :, :].unsqueeze(3).to_broadcast([P, TPG, 8, XHD]),
                                  ALU.mult).then_inc(b_norm, 1)

            def residual_x(g):
                dve.wait_ge(b_proj, g + 1)
                dve.wait_ge(b_xb, g + 1)
                dve.tensor_tensor(X[:, ds(g * TPG, TPG), :], tbank[:, :].rearrange("p (b d) -> p b d", d=D),
                                  xb[:, :, :], ALU.add).then_inc(b_x2, 1)

            def split(f, q, gi):
                dst, bias = ((KS[gi % 2][:, :], bks), (QS[:, gi, :], bqs))[f]
                dve.wait_ge(b_hm, q * 2 + f + 1)
                if f == 0 and needed(q - 1):
                    for i in range(2):
                        dve.wait_ge(b_kb[i], (q - 1) * 2)
                if f == 1 and needed(q - 3):
                    dve.wait_ge(b_st, (q - 3) * 4)
                dve.scalar_tensor_tensor(out=dst, in0=bank[f][:, :], scalar=bias[:, gi:gi + 1],
                                         in1=HM[f][:, :].bitcast(F32), op0=ALU.add,
                                         op1=ALU.subtract).then_inc(b_split, 1)

            def maxima(q, gi, b):
                dve.wait_ge(b_s, q * 4 + b + 1)
                dve.tensor_reduce(negm[gi % 2][:, :, b], bank[2 + b % 2][:, :].rearrange("p (j k) -> p j k", k=P),
                                  AX.X, ALU.max, negate=True).then_inc(b_max, 1)

            def split_maxima(q, gi):
                dve.wait_ge(b_max, q * 4 + 4)
                if needed(q):
                    dve.wait_ge(b_mtp, q)
                dve.tensor_copy(MM[:, 0, :, :], negm[gi % 2][:, :, :]).then_inc(b_mm, 1)
                dve.wait_ge(b_mm, q * 2 + 1)
                dve.tensor_tensor(MM[:, 1, :, :], negm[gi % 2][:, :, :], MM[:, 0, :, :].bitcast(F32),
                                  ALU.subtract).then_inc(b_mm, 1)

            def step(g, gi, par):
                g2, gi2, _, q2 = after(g, gi, par, 2)
                g3, gi3, _, q3 = after(g, gi, par, 3)
                s2 = some(g2) and not (isinstance(q2, int) and q2 < 0)
                if s2:
                    maxima(q2, gi2, 0)
                if some(g3):
                    split(0, q3, gi3)
                if s2:
                    maxima(q2, gi2, 1)
                if some(g3):
                    dve.wait_ge(b_split, q3 * 2 + 1)
                    if needed(q3 * 4 - 12):
                        dve.wait_ge(b_st, q3 * 4 - 12)
                    else:
                        dve.wait_ge(s_zero, gi3 + 1)
                    for j in range(2, 4):
                        to, frm = head_copy(gi3, j)
                        dve.tensor_copy(to, frm).then_inc(b_kb[1], 1)
                if gi == 0 and some(g + 1):
                    ctx_lo(g + 1, 1 - par)
                if gi == 1 and some(g - 1):
                    normalise_x(g - 1, 0)
                if s2:
                    maxima(q2, gi2, 2)
                if some(g3):
                    split(1, q3, gi3)
                if s2:
                    maxima(q2, gi2, 3)
                    split_maxima(q2, gi2)
                if gi == 0 and later(g + 1):
                    xt_lo(g + 1 + G, 1 - par)
                if gi == 1 and later(g + 2):
                    ln_moments(g + 2 + G, 0 if isinstance(g, int) and g == G - 2 else g + 2)
                if gi == 2 and some(g - 1):
                    normalise_x(g - 1, 1)
                if gi == 3 and some(g - 1):
                    residual_x(g - 1)

            ctx_lo(0, 0)
            normalise(G - 1, 0)
            step(-1, 1, 1)
            normalise(G - 1, 1)
            step(-1, 2, 1)
            residual(G - 1)
            step(-1, 3, 1)
            walk(dve, steps(step))

            def selector():
                dve.wait_ge(b_st, G * 16)
                dve.tensor_tensor(SEL.rearrange("p u (e c) -> p (u e) c", e=2),
                                  ident[:, 0:E].unsqueeze(2).to_broadcast([P, E, FI]),
                                  ident[:, E:2 * E].unsqueeze(2).to_broadcast([P, E, FI]),
                                  ALU.add).then_inc(f_sel, 1)

            def route_logits(g):
                dve.wait_ge(r_lp, g + 1)
                if not is_first(g):
                    dve.wait_ge(r_sig, g)
                dve.tensor_tensor(lg[:, :, :], tbank[:, 0:TPG * E].rearrange("p (t e) -> p t e", e=E),
                                  br_b[:, :].unsqueeze(1).to_broadcast([P, TPG, E]), ALU.add).then_inc(r_lg, 1)
                dve.drain()
                for t in range(TPG):
                    dve.max(top8[:, t, :], lg[:, t, :])

            def route_top(g):
                dve.drain()
                for t in range(TPG):
                    dve.match_replace(zap[:, t, :], top8[:, t, :], lg[:, t, :], -3.0e38).then_inc(r_zap, 1)

            def route_weights(g, half):
                steps = [g * 8 + 4 * half]

                def done(ins):
                    steps[0] = steps[0] + 1
                    ins.then_inc(r_w, 1)
                    dve.wait_ge(r_w, steps[0])

                if half == 0:
                    dve.wait_ge(r_zap, g * TPG + TPG)
                    done(dve.tensor_tensor(wfull[:, :, :], lg[:, :, :], zap[:, :, :], ALU.not_equal))
                    dve.wait_ge(r_sig, g + 1)
                    done(dve.tensor_tensor(wsel[:, :, :], wfull[:, :, :], sig[:, :, :], ALU.mult))
                    done(dve.tensor_reduce(wsum[:, :], wsel[:, :, :], AX.X, ALU.add))
                    done(dve.tensor_scalar(winv[:, :], wsum[:, :], 1e-9, None, ALU.add))
                else:
                    done(dve.reciprocal(wsum[:, :], winv[:, :]))
                    done(dve.tensor_tensor(wfull[:, :, :], wsel[:, :, :],
                                           wsum[:, :].unsqueeze(2).to_broadcast([P, TPG, E]), ALU.mult))
                    done(dve.tensor_copy(WS[:, :, 0:E], wfull[:, :, :]))
                    done(dve.tensor_tensor(WS[:, :, E:2 * E], wfull[:, :, :], WS[:, :, 0:E].bitcast(F32),
                                           ALU.subtract))

            def output(g, par):
                dve.wait_ge(f_yt, g + 1)
                if not (isinstance(g, int) and g < 2):
                    dve.wait_ge(st_y[par], (g - par) * 8)
                dve.tensor_tensor(OST[par], X[:, ds(g * TPG, TPG), :],
                                  tbank[:, :].rearrange("p (b d) -> p b d", d=D), ALU.add).then_inc(f_o, 1)

            def experts(g, par):
                for u in range(NU):
                    n = g * NU + u
                    k = (par + u) % 2
                    dve.wait_ge(f_s, n + 1)
                    dve.wait_ge(f_u, n + 1)
                    if needed(slot_user(g, u)):
                        dve.wait_ge(f_hl, slot_user(g, u))
                    dst = upm[k] if u < NP else hid[u % 3]
                    dve.scalar_tensor_tensor(out=dst, in0=bank[2 + k][:, :], scalar=BT[:, 32 + u:33 + u],
                                             in1=silu[k], op0=ALU.add, op1=ALU.mult).then_inc(f_t, 1)
                    if u < NP:
                        dve.wait_ge(f_w, g * NP + u + 1)
                        dve.wait_ge(f_t, n + 1)
                        dve.tensor_tensor(hid[u % 3], upm[k], bank[4 + u % 2][:, :], ALU.mult).then_inc(f_h, 1)
                    if u == 4 and not is_first(g):
                        output(g - 1, 1 - par)
                    if u == 3 and is_first(g):
                        residual_x(G - 1)
                    if not is_last(g):
                        if u == 1:
                            ln_moments(g + 1 + 2 * G, g + 1)
                        if u == 6:
                            xt_lo(g + 1 + 2 * G, 1 - par)
                        if u == 9:
                            route_logits(g + 1)
                        if u == 10:
                            route_top(g + 1)
                        if u == 12 or u == 13:
                            route_weights(g + 1, u - 12)

            step(G, 0, 0)
            route_logits(0)
            route_top(0)
            step(G, 1, 0)
            route_weights(0, 0)
            route_weights(0, 1)
            step(G, 2, 0)
            selector()
            walk(dve, experts)
            output(G - 1, 1)

        @block.tensor
        def _(pe):
            def product3(dst, wh, wl, mh, ml, start=True, stop=True):
                pe.matmul(dst, wh, mh, start=start, stop=False)
                pe.matmul(dst, wh, ml, start=False, stop=False)
                return pe.matmul(dst, wl, mh, start=False, stop=stop)

            def transposes(src, n=TPG):
                for t in range(n):
                    last = pe.transpose(tbank[:, t * P:(t + 1) * P], src[:, t, :], ident[:, :])
                return last

            def norm_transposed(n):
                pe.wait_ge(ln_xn, n + 1)
                transposes(xn).then_inc(xt_full, 1)

            pe.wait_ge(c_pool, 2)
            pe.wait_ge(ld_w, 3 * 16)
            pe.transpose(bank[6][:, 0:D], qkv_rows[:, 2, :], ident[:, :])
            pe.transpose(bank[6][:, D:2 * D], wout_rows[:, :], ident[:, :]).then_inc(c_wT, 1)
            pe.wait_ge(c_spread, 2)
            for i, q in enumerate(FOLDS):
                if i == 2:
                    norm_transposed(0)
                qk, h0 = q // 2, 4 * (q % 2)
                pe.matmul(bank[i][:, :], qkv_rows[:, qk, :],
                          proj_spread[:, h0:h0 + 4, :].rearrange("p h f -> p (h f)"),
                          start=True, stop=True).then_inc(c_wT, 1)

            def scores(gh, par):
                pe.wait_ge(a_phi, gh * 2 + 2)
                if not (isinstance(gh, int) and gh == 0):
                    pe.wait_ge(a_mask, gh)
                for b in range(TPG):
                    last = pe.matmul(bank[4][:, b * P:(b + 1) * P], phiK[par][:, b * P:(b + 1) * P],
                                     phiQ[par][:, b * P:(b + 1) * P], start=True, stop=True)
                last.then_inc(a_score, 1)

            def outputs(gh, h):
                pe.wait_ge(a_mask, gh + 1)
                j = h % 4
                for b in range(TPG):
                    last = pe.matmul(bank[5 + h // 4][32 * j:32 * j + 32, b * P:(b + 1) * P],
                                     V1[:, b, h, :], AM[h % 2][:, b, :], start=True, stop=True)
                last.then_inc(a_o, 1)

            def values(g, par):
                for b in range(TPG):
                    t = slice(b * P, (b + 1) * P)
                    last = product3(tbank[:, t], XTH[par][:, t], XTL[par][:, t], WVH[:, :], WVL[:, :])
                last.then_inc(a_vp, 1)

            def token_major(g, r):
                transposes(OS[r]).then_inc(a_ot, 1)

            def feature_major(g):
                pe.wait_ge(a_norm, g * 2 + 2)
                transposes(ON).then_inc(a_ontp, 1)

            def project(g):
                pe.wait_ge(a_ont, g + 1)
                for b in range(TPG):
                    last = pe.matmul(tbank[:, b * P:(b + 1) * P], ONT[:, b, :], WOT[:, :], start=True, stop=True)
                last.then_inc(a_proj, 1)

            def attn(g, par):
                for h in range(AH):
                    gh = g * AH + h
                    if h == 0:
                        pe.wait_ge(xt_lo_ok, g + 1)
                    for f in range(2):
                        n = 2 * h + f
                        head = (1 - f) * AH + h
                        if not (is_first(g) and n < 4):
                            pe.wait_ge(a_phi, g * 16 + n - 3)
                        elif is_first(g):
                            pe.wait_ge(c_lo, n + 2)
                        if is_first(g) and n == 4:
                            pe.wait_ge(c_lo, 5)
                        product3(bank[n % 4][:, :], CH[:, head, :], CL[:, head, :],
                                 XTH[par][:, :], XTL[par][:, :]).then_inc(a_feat, 1)
                    if not (is_first(g) and h == 0):
                        scores(gh - 1, (h + 1) % 2)
                    if h == 2:
                        pe.wait_ge(a_v1, g + 1)
                    if not (is_first(g) and h < 2):
                        outputs(gh - 2, (h - 2) % AH)
                    if h == 1:
                        if isinstance(g, int) and g == 1:
                            pe.wait_ge(f_prep, FPREP)
                        elif not is_first(g):
                            pe.wait_ge(a_x1, g - 1)
                        values(g, par)
                    if h == 2 and not is_first(g):
                        token_major(g - 1, 0)
                    if h == 3 and not is_first(g):
                        pe.wait_ge(a_norm, (g - 1) * 2 + 1)
                        token_major(g - 1, 1)
                    if h == 4 and not is_first(g):
                        feature_major(g - 1)
                    if h == 5:
                        if not is_first(g):
                            pe.wait_ge(a_ont, g)
                        norm_transposed(g + 1)
                    if h == 7:
                        pe.wait_ge(xt_lo_ok, g + 2)
                        if is_first(g):
                            pe.wait_ge(s_bv, 1)
                            pe.matmul(tbank[:, P:2 * P], bv_cols[:, :], wo_rows[:, :], start=True, stop=True)
                            pe.wait_ge(ld_f, LDF)
                            pe.transpose(tbank[:, 0:64], bias_rows[:, :], ident[0:64, 0:64]).then_inc(f_bt, 1)
                        else:
                            project(g - 1)

            walk(pe, attn)
            def ctx_transposed(g, par):
                pe.wait_ge(ld_c[par], (g - par) * 16 + 32)
                for b in range(TPG):
                    last = pe.transpose(tbank[:, b * P:(b + 1) * P],
                                        ctxr[par][:, b, :, :].rearrange("p i c -> p (i c)"), ident[:, :])
                last.then_inc(b_ctx, 1)

            def project_k(g, q, gi, par):
                if gi == 0:
                    pe.wait_ge(b_cs, g + 1)
                if needed(q):
                    pe.wait_ge(b_split, q * 2 - 1)
                w = [WKS[i][:, gi, :, :, :].rearrange("p j t d -> p (j t d)") for i in range(2)]
                pe.matmul(bank[0][:, :], w[0], CS[par][:, :], start=True, stop=False)
                pe.matmul(bank[0][:, :], w[1], CS[par][:, :], start=False, stop=True).then_inc(b_pp, 1)

            def project_q(g, q, gi, par):
                if gi == 0:
                    pe.wait_ge(xt_lo_ok, g + 1 + G)
                if needed(q - 1):
                    pe.wait_ge(b_mt, q - 1)
                elif needed(q):
                    pe.wait_ge(b_split, q * 2)
                w = [WQS[i][:, gi, :, :, :].rearrange("p j t d -> p (j t d)") for i in range(2)]
                product3(bank[1][:, :], w[0], w[1], XTH[par][:, :], XTL[par][:, :]).then_inc(b_pp, 1)

            def values_x(g, par):
                for b in range(TPG):
                    t = slice(b * P, (b + 1) * P)
                    pe.matmul(tbank[:, t], CS[par][:, t], WVX[0][:, :], start=True, stop=False)
                    last = pe.matmul(tbank[:, t], CS[par][:, t], WVX[1][:, :], start=False, stop=True)
                last.then_inc(b_vp, 1)

            def scores_by_query(q, gi, b):
                if b == 0:
                    for i in range(2):
                        pe.wait_ge(b_kb[i], q * 2 + 2)
                    pe.wait_ge(b_split, q * 2 + 2)
                if needed(q * 4 + b - 1):
                    pe.wait_ge(b_max, q * 4 + b - 1)
                pe.matmul(bank[2 + b % 2][:, :], QS[:, gi, b * P:(b + 1) * P],
                          KB[gi][:, b, :, :].rearrange("p j k -> p (j k)"),
                          start=True, stop=True).then_inc(b_s, 1)

            def maxima_transposed(q):
                pe.wait_ge(b_mm, q * 2 + 2)
                pe.wait_ge(b_split, min(q * 2 + 4, 8 * G) if isinstance(q, int) else q * 2 + 4)
                if needed(q):
                    pe.wait_ge(b_mt, q)
                pe.transpose(bank[1][0:32, 0:P], MM[:, :, :, :].bitcast(F32).rearrange("p i j b -> p (i j b)"),
                             ident[:, :]).then_inc(b_mtp, 1)

            def scores_by_key(q, gi, b):
                if b == 0:
                    pe.wait_ge(b_mq, q * 32 + 32)
                if needed(q * 4 + b - 1):
                    pe.wait_ge(b_exp, q * 4 + b - 1)
                for j in range(4):
                    last = pe.matmul(bank[5 + b % 2][:, j * P:(j + 1) * P], KB[gi][:, b, j, :],
                                     QS[:, gi, b * P:(b + 1) * P], start=True, stop=True)
                last.then_inc(b_st, 1)

            def attend(g, par, r, b):
                if b == 0:
                    pe.wait_ge(b_exp, g * 16 + r * 8 + 8)
                    if needed(g * 2 + r):
                        pe.wait_ge(b_os, g * 2 + r)
                    if r == 0:
                        pe.wait_ge(b_v2, g * 2 + 2)
                for half in range(2):
                    gi = 2 * r + half
                    for j in range(4):
                        last = pe.matmul(bank[4][32 * j:32 * j + 32, b * P:(b + 1) * P],
                                         V2[par][:, b * XG + gi, j, :], PT[gi][:, b, j, :],
                                         start=(half == 0), stop=(half == 1))
                last.then_inc(b_pv, 1)

            def feature_major_x(g):
                pe.wait_ge(b_norm, g * 2 + 2)
                transposes(ON).then_inc(b_ontp, 1)

            def project_x(g):
                pe.wait_ge(b_ont, g + 1)
                for b in range(TPG):
                    last = pe.matmul(tbank[:, b * P:(b + 1) * P], ONT[:, b, :], WOX[:, :],
                                     start=True, stop=True)
                last.then_inc(b_proj, 1)

            def token_major_x(g, r):
                pe.wait_ge(b_os, g * 2 + r + 1)
                transposes(OS[r]).then_inc(b_ot, 1)

            def step(g, gi, par):
                q0 = g * XG + gi
                g1, _, _, q1 = after(g, gi, par, 1)
                g2, gi2, _, q2 = after(g, gi, par, 2)
                g3, gi3, par3, q3 = after(g, gi, par, 3)
                s1 = some(g1) and not (isinstance(q1, int) and q1 < 0)
                s2 = some(g2) and not (isinstance(q2, int) and q2 < 0)
                ga, para = (g, par) if gi >= 2 else (g - 1, 1 - par)
                if some(g3):
                    project_k(g3, q3, gi3, par3)
                if s2:
                    scores_by_query(q2, gi2, 0)
                if some(g):
                    scores_by_key(q0, gi, 0)
                if s1:
                    maxima_transposed(q1)
                if gi == 0 and later(g + 1):
                    if needed(g - 1):
                        pe.wait_ge(b_x2, g - 1)
                    elif isinstance(g, int) and g == 1:
                        pe.wait_ge(b_v2, 4)
                    else:
                        pe.wait_ge(a_x1, G)
                    if some(g + 1):
                        ctx_transposed(g + 1, 1 - par)
                if gi == 1 and some(g - 1):
                    if some(g):
                        pe.wait_ge(xt_lo_ok, g + 2 + G)
                    else:
                        pe.wait_ge(r_lg, 1)
                    token_major_x(g - 1, 0)
                if gi == 2 and some(g + 1):
                    if some(g - 1):
                        pe.wait_ge(b_norm, (g - 1) * 2 + 1)
                    elif isinstance(g, int) and g < 0:
                        pe.wait_ge(a_norm, G * 2)
                    else:
                        pe.wait_ge(xt_lo_ok, g + 2 + G)
                    values_x(g + 1, 1 - par)
                if gi == 3 and some(g - 1):
                    feature_major_x(g - 1)
                if s2:
                    scores_by_query(q2, gi2, 1)
                if some(g):
                    scores_by_key(q0, gi, 1)
                if some(g3):
                    project_q(g3, q3, gi3, par3)
                if some(ga):
                    attend(ga, para, 1 - gi // 2, 2 * (gi % 2))
                if s2:
                    scores_by_query(q2, gi2, 2)
                if some(g):
                    scores_by_key(q0, gi, 2)
                if gi == 0 and later(g + 1):
                    if some(g + 1):
                        pe.wait_ge(b_cs, g + 2)
                    norm_transposed(g + 1 + G)
                if gi == 2 and some(g - 1):
                    pe.wait_ge(b_norm, (g - 1) * 2 + 1)
                    if some(g + 1):
                        pe.wait_ge(b_v2, g * 2 + 4)
                    token_major_x(g - 1, 1)
                if gi == 3 and some(g - 1):
                    project_x(g - 1)
                if s2:
                    scores_by_query(q2, gi2, 3)
                if some(g):
                    scores_by_key(q0, gi, 3)
                if some(ga):
                    attend(ga, para, 1 - gi // 2, 2 * (gi % 2) + 1)

            scores(G * AH - 1, 1)
            outputs(G * AH - 2, AH - 2)
            pe.wait_ge(a_x1, G - 1)
            ctx_transposed(0, 0)
            outputs(G * AH - 1, AH - 1)
            pe.wait_ge(s_stack, SSTACK)
            pe.wait_ge(a_os, G * 2)
            pe.wait_ge(b_cs, 1)
            token_major(G - 1, 0)
            step(-1, 1, 1)
            pe.wait_ge(a_norm, (G - 1) * 2 + 1)
            token_major(G - 1, 1)
            step(-1, 2, 1)
            pe.wait_ge(b_v2, 2)
            feature_major(G - 1)
            project(G - 1)
            step(-1, 3, 1)
            walk(pe, steps(step))

            def logits(g, par):
                for t in range(TPG):
                    c = slice(t * P, (t + 1) * P)
                    last = product3(tbank[:, t * E:(t + 1) * E], XTH[par][:, c], XTL[par][:, c],
                                    WR[0][:, :], WR[1][:, :])
                last.then_inc(r_lp, 1)

            def weights_transposed(g):
                pe.wait_ge(r_w, g * 8 + 8)
                transposes(WS.bitcast(F32)).then_inc(r_wp, 1)

            def down(g, par, u):
                if u == 0:
                    if not is_first(g):
                        pe.wait_ge(f_y, g)
                    pe.matmul(bank[6][:, :], BD[0][:, :], WT[par][:, :], start=True, stop=False)
                    pe.matmul(bank[6][:, :], BD[1][:, :], WT[par][:, :], start=False, stop=False)
                n = g * NU + u
                pe.wait_ge(f_hl, n + 1)
                product3(bank[6][:, :], WDH[u], WDL[u], HH[u % 3], HL[u % 3],
                         start=False, stop=(u == NP)).then_inc(f_d, 1)

            def sum_transposed(g):
                pe.wait_ge(f_y, g + 1)
                transposes(YS.rearrange("p (t c) -> p t c", c=P)).then_inc(f_yt, 1)

            def experts(g, par):
                for u in range(NU):
                    n = g * NU + u
                    k = (par + u) % 2
                    if u == 0:
                        pe.wait_ge(xt_lo_ok, g + 1 + 2 * G)
                    for w, b, full, drained in ((GATE, k, f_g, f_s), (UP, 2 + k, f_u, f_t)):
                        if not (is_first(g) and u < 2):
                            pe.wait_ge(drained, n - 1)
                        product3(bank[b][:, :], w[0][:, u, :], w[1][:, u, :], XTH[par][:, :],
                                 XTL[par][:, :]).then_inc(full, 1)
                    if u < NP:
                        if u == 0:
                            pe.wait_ge(r_wt, g + 1)
                        if not (is_first(g) and u < 2):
                            pe.wait_ge(f_h, g * NP + u - 1)
                        pe.matmul(bank[4 + u % 2][:, :], SEL[:, u, :], WT[par][:, :],
                                  start=True, stop=True).then_inc(f_w, 1)
                    if u > 2:
                        down(g, par, u - 3)
                    elif not is_first(g):
                        down(g - 1, 1 - par, NP - 2 + u)
                    if u == 4 and not is_first(g):
                        sum_transposed(g - 1)
                    if u == 1 and is_first(g):
                        feature_major_x(G - 1)
                    if u == 3 and is_first(g):
                        project_x(G - 1)
                    if not is_last(g):
                        if u == 5:
                            if is_first(g):
                                pe.wait_ge(b_x2, G)
                            else:
                                pe.wait_ge(f_o, g)
                            norm_transposed(g + 1 + 2 * G)
                        if u == 8:
                            pe.wait_ge(xt_lo_ok, g + 2 + 2 * G)
                            logits(g + 1, 1 - par)
                        if u == 15:
                            weights_transposed(g + 1)

            step(G, 0, 0)
            pe.wait_ge(b_x2, G - 1)
            pe.wait_ge(xt_lo_ok, 2 * G + 1)
            logits(0, 0)
            step(G, 1, 0)
            step(G, 2, 0)
            pe.wait_ge(b_norm, G * 2)
            pe.wait_ge(f_zero, 5)
            weights_transposed(0)
            pe.wait_ge(f_pool, 4)
            pe.wait_ge(f_sel, 1)
            for i in range(2):
                pe.wait_ge(f_wd[i], 2)
            walk(pe, experts)
            down(G - 1, 1, NP - 2)
            down(G - 1, 1, NP - 1)
            down(G - 1, 1, NP)
            sum_transposed(G - 1)


_INS = ['x', 'ctx_512', 'L0_attn_w_qkv', 'L0_attn_w_out', 'L0_attn_b_out', 'L0_attn_proj',
        'L0_xattn_Wq', 'L0_xattn_bq', 'L0_xattn_Wk', 'L0_xattn_bk', 'L0_xattn_Wv', 'L0_xattn_bv',
        'L0_xattn_Wo', 'L0_xattn_bo', 'L0_ffn_Wr', 'L0_ffn_br', 'L0_ffn_Wg_s', 'L0_ffn_bg_s',
        'L0_ffn_Wu_s', 'L0_ffn_bu_s', 'L0_ffn_Wd_s', 'L0_ffn_bd_s', 'L0_ffn_Wg', 'L0_ffn_bg',
        'L0_ffn_Wu', 'L0_ffn_bu', 'L0_ffn_Wd', 'L0_ffn_bd']


def kernel(**inputs):
    import numpy as _np
    import concourse.bacc as _bacc
    from concourse import mybir as _mybir
    from concourse.bass_utils import run_bass_kernel_spmd as _run

    nc = _bacc.Bacc("TRN2", target_bir_lowering=False, num_devices=1)
    arrays, args = {}, []
    for name in _INS:
        a = _np.ascontiguousarray(inputs[name])
        arrays[f"in_{name}_dram"] = a
        args.append(nc.dram_tensor(f"in_{name}_dram", a.shape, _mybir.dt.from_np(a.dtype), kind="ExternalInput").ap())
    shape = tuple(inputs["x"].shape)
    args.append(nc.dram_tensor("out_0_dram", shape, _mybir.dt.float32, kind="ExternalOutput").ap())
    decoder_layer(nc, *args)
    r = _run(nc, [arrays], core_ids=[0])
    return r.results[0]["out_0_dram"]
```
